# Optimizing a Trainium2 kernel written in Bass

```python
import numpy as np
import jax
import jax.numpy as jnp

def _softmax(x, axis=-1):
    return jax.nn.softmax(x, axis=axis)

def _gelu(x):
    return jax.nn.gelu(x, approximate=True)

def _silu(x):
    return jax.nn.silu(x)

def _sigmoid(x):
    return jax.nn.sigmoid(x)

def _layernorm(x, axis=-1, eps=1e-05):
    m = jnp.mean(x, axis=axis, keepdims=True)
    v = jnp.var(x, axis=axis, keepdims=True)
    return (x - m) / jnp.sqrt(v + eps)

def _scatter_add(tgt, idx, src, axis=0):
    return tgt.at[idx].add(src)

def _segment_sum(src, seg, n):
    return jax.ops.segment_sum(src, seg, n)
kernel_name = 'mk_xattn_seq_d2_seqx_r4_780fea'

def setup_inputs(seed: int=0):
    np.random.seed(seed)
    _w = jnp.asarray

    def _rec_inputs():
        import jax
        import jax.numpy as jnp
        _rk = jax.random.key(seed)
        x = -0.0002928 + 1 * jax.random.normal(jax.random.fold_in(_rk, 1), (8, 256, 512), jnp.float32)
        _lenS = 256 - jax.random.randint(jax.random.fold_in(_rk, 7), (8,), 0, max(1, 256 // 4) + 1, jnp.int32)
        _lenS2 = 256 - jax.random.randint(jax.random.fold_in(_rk, 8), (8,), 0, max(1, 256 // 4) + 1, jnp.int32)
        _ctx_2048P = jax.random.normal(jax.random.fold_in(_rk, 12), (8, 16, 512), jnp.float32)
        _ctx_2048c = jax.random.dirichlet(jax.random.fold_in(_rk, 512), 0.3 * jnp.ones((16,), jnp.float32), (8, 256))
        _ctx_2048t = jnp.einsum('bsk,bkd->bsd', _ctx_2048c, _ctx_2048P)
        _ctx_2048t = _ctx_2048t * jax.lax.rsqrt(jnp.mean(jnp.square(_ctx_2048t)) + 1e-12) * 0.953939
        ctx_2048 = -1.39393e-06 + 0.999914 * (_ctx_2048t + 0.3 * jax.random.normal(jax.random.fold_in(_rk, 612), (8, 256, 512), jnp.float32))
        _validS = jnp.arange(256)[None, :] < _lenS[:, None]
        _validS2 = jnp.arange(256)[None, :] < _lenS2[:, None]
        _causal = jnp.tril(jnp.ones((256, 256), dtype=bool))
        mask_Bx1x2048_bf1 = jnp.ones((8, 1, 512), dtype=bool)
        mask_1x1xSxS2_fc1 = jnp.where(jnp.broadcast_to(_validS2[0:1, None, None, :], (1, 1, 256, 256)), 1.0, 0.0).astype(jnp.float32)
        mask_Bx1xSxS2_ff1 = jnp.where(jnp.ones((8, 1, 256, 256), dtype=bool), 1.0, 0.0).astype(jnp.float32)
        return (x, ctx_2048, mask_Bx1x2048_bf1, mask_1x1xSxS2_fc1, mask_Bx1xSxS2_ff1)
    x, ctx_2048, mask_Bx1x2048_bf1, mask_1x1xSxS2_fc1, mask_Bx1xSxS2_ff1 = _rec_inputs()

    def _L0_xattn_setup():
        import jax, jax.numpy as jnp
        import numpy as np
        import math
        N_HEADS = 16
        EPS = 1e-05

        def _masked_instance_norm(x, mask):
            m = mask.astype(x.dtype)
            x = x * m
            n_valid = jnp.sum(m, axis=-1, keepdims=True)
            mean = jnp.sum(x, axis=-1, keepdims=True) / n_valid
            var = jnp.sum(x * x, axis=-1, keepdims=True) / n_valid - mean * mean
            x = (x - mean) / jnp.sqrt(jax.nn.relu(var) + EPS)
            return x * m
        key = jax.random.key(seed)
        ks = jax.random.split(key, 8)
        bs, c, t1, t2 = (2, 256, 512, 512)
        s = 1.0 / math.sqrt(c)
        return {'x': jax.random.normal(ks[0], (bs, c, t1), jnp.float32), 'mask': jnp.ones((bs, 1, t1), jnp.bool_), 'kv': jax.random.normal(ks[1], (bs, c, t2), jnp.float32), 'kv_mask': jnp.ones((bs, 1, t2), jnp.bool_), 'Wq': jax.random.normal(ks[2], (c, c), jnp.float32) * s, 'bq': jnp.zeros((c,), jnp.float32), 'Wk': jax.random.normal(ks[3], (c, c), jnp.float32) * s, 'bk': jnp.zeros((c,), jnp.float32), 'Wv': jax.random.normal(ks[4], (c, c), jnp.float32) * s, 'bv': jnp.zeros((c,), jnp.float32)}
    _L0_xattn_all = _L0_xattn_setup()
    _L0_xattn_in = {k: v for k, v in _L0_xattn_all.items() if k in ('Wq', 'bq', 'Wk', 'bk', 'Wv', 'bv')}
    del _L0_xattn_all

    def _L1_xattn_setup():
        import jax, jax.numpy as jnp
        import numpy as np
        H = 512
        NH = 16
        HD = H // NH
        EPS = 1e-05

        def gelu(x):
            return 0.5 * x * (1.0 + jnp.tanh(0.7978845608028654 * x * (1.0 + 0.044715 * x * x)))

        def layernorm(x, scale, bias):
            m = jnp.mean(x, axis=-1, keepdims=True)
            v = jnp.mean(jnp.square(x - m), axis=-1, keepdims=True)
            return (x - m) * jax.lax.rsqrt(v + EPS) * scale + bias

        def split_heads(x):
            b, s, _ = x.shape
            return x.reshape(b, s, NH, HD).transpose(0, 2, 1, 3)

        def merge_heads(x):
            b, nh, s, hd = x.shape
            return x.transpose(0, 2, 1, 3).reshape(b, s, nh * hd)

        def attention(q, k, v, mask):
            scores = jnp.einsum('bhqd,bhkd->bhqk', q, k) / jnp.sqrt(jnp.float32(HD))
            scores = scores * mask - 10000.0 * (1.0 - mask)
            probs = jax.nn.softmax(scores, axis=-1)
            return jnp.einsum('bhqk,bhkd->bhqd', probs, v)
        key = jax.random.key(seed)
        ks = jax.random.split(key, 16)
        b, s, t = (2, 256, 256)
        w = lambda k, i, o: jax.random.normal(k, (i, o), jnp.float32) * 0.02
        inp = {'hidden_states': jax.random.normal(ks[0], (b, s, H), jnp.float32), 'encoder_states': jax.random.normal(ks[1], (b, t, H), jnp.float32), 'ltor_mask': jnp.tril(jnp.ones((1, 1, s, s), jnp.float32)), 'cross_mask': jnp.ones((b, 1, s, t), jnp.float32), 'ln1_s': jnp.ones((H,), jnp.float32), 'ln1_b': jnp.zeros((H,), jnp.float32), 'w_qkv': w(ks[2], H, 3 * H), 'b_qkv': jnp.zeros((3 * H,), jnp.float32), 'w_ao': w(ks[3], H, H), 'b_ao': jnp.zeros((H,), jnp.float32), 'ln2_s': jnp.ones((H,), jnp.float32), 'ln2_b': jnp.zeros((H,), jnp.float32), 'w_q': w(ks[4], H, H), 'b_q': jnp.zeros((H,), jnp.float32), 'w_kv': w(ks[5], H, 2 * H), 'b_kv': jnp.zeros((2 * H,), jnp.float32), 'w_co': w(ks[6], H, H), 'b_co': jnp.zeros((H,), jnp.float32), 'ln3_s': jnp.ones((H,), jnp.float32), 'ln3_b': jnp.zeros((H,), jnp.float32), 'w1': w(ks[7], H, 4 * H), 'b1': jnp.zeros((4 * H,), jnp.float32), 'w2': w(ks[8], 4 * H, H), 'b2': jnp.zeros((H,), jnp.float32)}
        return inp
    _L1_xattn_all = _L1_xattn_setup()
    _L1_xattn_in = {k: v for k, v in _L1_xattn_all.items() if k in ('ln1_s', 'ln1_b', 'w_qkv', 'b_qkv', 'w_ao', 'b_ao', 'ln2_s', 'ln2_b', 'w_q', 'b_q', 'w_kv', 'b_kv', 'w_co', 'b_co', 'ln3_s', 'ln3_b', 'w1', 'b1', 'w2', 'b2')}
    del _L1_xattn_all
    return {'x': x, 'ctx_2048': ctx_2048, 'mask_Bx1x2048_bf1': mask_Bx1x2048_bf1, 'mask_1x1xSxS2_fc1': mask_1x1xSxS2_fc1, 'mask_Bx1xSxS2_ff1': mask_Bx1xSxS2_ff1, 'L0_xattn_Wq': _L0_xattn_in['Wq'], 'L0_xattn_bq': _L0_xattn_in['bq'], 'L0_xattn_Wk': _L0_xattn_in['Wk'], 'L0_xattn_bk': _L0_xattn_in['bk'], 'L0_xattn_Wv': _L0_xattn_in['Wv'], 'L0_xattn_bv': _L0_xattn_in['bv'], 'L1_xattn_ln1_s': _L1_xattn_in['ln1_s'], 'L1_xattn_ln1_b': _L1_xattn_in['ln1_b'], 'L1_xattn_w_qkv': _L1_xattn_in['w_qkv'], 'L1_xattn_b_qkv': _L1_xattn_in['b_qkv'], 'L1_xattn_w_ao': _L1_xattn_in['w_ao'], 'L1_xattn_b_ao': _L1_xattn_in['b_ao'], 'L1_xattn_ln2_s': _L1_xattn_in['ln2_s'], 'L1_xattn_ln2_b': _L1_xattn_in['ln2_b'], 'L1_xattn_w_q': _L1_xattn_in['w_q'], 'L1_xattn_b_q': _L1_xattn_in['b_q'], 'L1_xattn_w_kv': _L1_xattn_in['w_kv'], 'L1_xattn_b_kv': _L1_xattn_in['b_kv'], 'L1_xattn_w_co': _L1_xattn_in['w_co'], 'L1_xattn_b_co': _L1_xattn_in['b_co'], 'L1_xattn_ln3_s': _L1_xattn_in['ln3_s'], 'L1_xattn_ln3_b': _L1_xattn_in['ln3_b'], 'L1_xattn_w1': _L1_xattn_in['w1'], 'L1_xattn_b1': _L1_xattn_in['b1'], 'L1_xattn_w2': _L1_xattn_in['w2'], 'L1_xattn_b2': _L1_xattn_in['b2']}

def reference(x, ctx_2048, mask_Bx1x2048_bf1, mask_1x1xSxS2_fc1, mask_Bx1xSxS2_ff1, L0_xattn_Wq, L0_xattn_bq, L0_xattn_Wk, L0_xattn_bk, L0_xattn_Wv, L0_xattn_bv, L1_xattn_ln1_s, L1_xattn_ln1_b, L1_xattn_w_qkv, L1_xattn_b_qkv, L1_xattn_w_ao, L1_xattn_b_ao, L1_xattn_ln2_s, L1_xattn_ln2_b, L1_xattn_w_q, L1_xattn_b_q, L1_xattn_w_kv, L1_xattn_b_kv, L1_xattn_w_co, L1_xattn_b_co, L1_xattn_ln3_s, L1_xattn_ln3_b, L1_xattn_w1, L1_xattn_b1, L1_xattn_w2, L1_xattn_b2):
    import jax
    import jax.numpy as jnp

    def _L0_xattn_ref(x, mask, kv, kv_mask, Wq, bq, Wk, bk, Wv, bv):
        import jax, jax.numpy as jnp
        import numpy as np
        import math
        N_HEADS = 16
        EPS = 1e-05

        def _masked_instance_norm(x, mask):
            m = mask.astype(x.dtype)
            x = x * m
            n_valid = jnp.sum(m, axis=-1, keepdims=True)
            mean = jnp.sum(x, axis=-1, keepdims=True) / n_valid
            var = jnp.sum(x * x, axis=-1, keepdims=True) / n_valid - mean * mean
            x = (x - mean) / jnp.sqrt(jax.nn.relu(var) + EPS)
            return x * m
        bs, c, t1 = x.shape
        h = N_HEADS
        d = c // h
        scale = 1.0 / math.sqrt(d)
        q = jnp.einsum('oc,bct->bot', Wq, x) + bq[None, :, None]
        k = jnp.einsum('oc,bct->bot', Wk, kv) + bk[None, :, None]
        v = jnp.einsum('oc,bct->bot', Wv, kv) + bv[None, :, None]
        q = q.reshape(bs, h, d, t1).transpose(0, 1, 3, 2)
        k = k.reshape(bs, h, d, -1)
        v = v.reshape(bs, h, d, -1).transpose(0, 1, 3, 2)
        attn = jnp.einsum('bhqd,bhdk->bhqk', q * scale, k)
        attn = jnp.where(kv_mask[:, :, None, :], attn, -jnp.inf)
        attn = jax.nn.softmax(attn, axis=-1)
        mean = jnp.einsum('bhqk,bhkd->bhqd', attn, v)
        ex2 = jnp.einsum('bhqk,bhkd->bhqd', attn, v * v)
        std = jnp.sqrt(jax.nn.relu(ex2 - mean * mean))
        mean = mean.transpose(0, 1, 3, 2).reshape(bs, c, t1)
        std = std.transpose(0, 1, 3, 2).reshape(bs, c, t1)
        xn = _masked_instance_norm(x, mask)
        out = (xn * std + mean) * mask.astype(x.dtype)
        return out

    def _L1_xattn_ref(hidden_states, encoder_states, ltor_mask, cross_mask, ln1_s, ln1_b, w_qkv, b_qkv, w_ao, b_ao, ln2_s, ln2_b, w_q, b_q, w_kv, b_kv, w_co, b_co, ln3_s, ln3_b, w1, b1, w2, b2):
        import jax, jax.numpy as jnp
        import numpy as np
        H = 512
        NH = 16
        HD = H // NH
        EPS = 1e-05

        def gelu(x):
            return 0.5 * x * (1.0 + jnp.tanh(0.7978845608028654 * x * (1.0 + 0.044715 * x * x)))

        def layernorm(x, scale, bias):
            m = jnp.mean(x, axis=-1, keepdims=True)
            v = jnp.mean(jnp.square(x - m), axis=-1, keepdims=True)
            return (x - m) * jax.lax.rsqrt(v + EPS) * scale + bias

        def split_heads(x):
            b, s, _ = x.shape
            return x.reshape(b, s, NH, HD).transpose(0, 2, 1, 3)

        def merge_heads(x):
            b, nh, s, hd = x.shape
            return x.transpose(0, 2, 1, 3).reshape(b, s, nh * hd)

        def attention(q, k, v, mask):
            scores = jnp.einsum('bhqd,bhkd->bhqk', q, k) / jnp.sqrt(jnp.float32(HD))
            scores = scores * mask - 10000.0 * (1.0 - mask)
            probs = jax.nn.softmax(scores, axis=-1)
            return jnp.einsum('bhqk,bhkd->bhqd', probs, v)
        ln_out = layernorm(hidden_states, ln1_s, ln1_b)
        qkv = ln_out @ w_qkv + b_qkv
        q, k, v = jnp.split(qkv, 3, axis=-1)
        ctx = merge_heads(attention(split_heads(q), split_heads(k), split_heads(v), ltor_mask))
        attn_out = ctx @ w_ao + b_ao
        x = hidden_states + attn_out
        ln_out = layernorm(x, ln2_s, ln2_b)
        q = ln_out @ w_q + b_q
        kv = encoder_states @ w_kv + b_kv
        k, v = jnp.split(kv, 2, axis=-1)
        ctx = merge_heads(attention(split_heads(q), split_heads(k), split_heads(v), cross_mask))
        cross_out = ctx @ w_co + b_co
        x = x + cross_out
        ln_out = layernorm(x, ln3_s, ln3_b)
        mlp_out = gelu(ln_out @ w1 + b1) @ w2 + b2
        return x + mlp_out
    x = _L0_xattn_ref(x, mask_Bx1x2048_bf1, ctx_2048, mask_Bx1x2048_bf1, L0_xattn_Wq, L0_xattn_bq, L0_xattn_Wk, L0_xattn_bk, L0_xattn_Wv, L0_xattn_bv)
    x = _L1_xattn_ref(x, ctx_2048, mask_1x1xSxS2_fc1, mask_Bx1xSxS2_ff1, L1_xattn_ln1_s, L1_xattn_ln1_b, L1_xattn_w_qkv, L1_xattn_b_qkv, L1_xattn_w_ao, L1_xattn_b_ao, L1_xattn_ln2_s, L1_xattn_ln2_b, L1_xattn_w_q, L1_xattn_b_q, L1_xattn_w_kv, L1_xattn_b_kv, L1_xattn_w_co, L1_xattn_b_co, L1_xattn_ln3_s, L1_xattn_ln3_b, L1_xattn_w1, L1_xattn_b1, L1_xattn_w2, L1_xattn_b2)
    return x

_drawn_inputs = setup_inputs


def setup_inputs(seed=0):
    import zlib

    import numpy as np

    out = dict(_drawn_inputs(seed))
    spreads = {'L0_xattn_bq': (0.0, 0.1),
     'L0_xattn_bk': (0.0, 2.0),
     'L0_xattn_bv': (0.0, 0.1),
     'L1_xattn_ln1_s': (1.0, 0.6),
     'L1_xattn_ln1_b': (0.0, 0.422),
     'L1_xattn_b_qkv': (0.0, 0.1),
     'L1_xattn_b_ao': (0.0, 0.1),
     'L1_xattn_ln2_s': (1.0, 0.6),
     'L1_xattn_ln2_b': (0.0, 2.0),
     'L1_xattn_b_q': (0.0, 2.0),
     'L1_xattn_b_kv': (0.0, 0.1),
     'L1_xattn_b_co': (0.0, 0.1),
     'L1_xattn_ln3_s': (1.0, 0.2),
     'L1_xattn_ln3_b': (0.0, 0.374),
     'L1_xattn_b1': (0.0, 0.1),
     'L1_xattn_b2': (0.0, 0.1)}
    factors = {'L1_xattn_w_q': 64.0}
    for name, (base, spread) in spreads.items():
        noise = np.random.default_rng([zlib.crc32(name.encode()), seed]).standard_normal(out[name].shape)
        drawn = base * np.exp(spread * noise) if base else spread * noise
        out[name] = jnp.asarray(drawn.astype(out[name].dtype))
    for name, factor in factors.items():
        out[name] = (out[name] * factor).astype(out[name].dtype)
    return out
```

```python
from contextlib import ExitStack

import numpy as np

import concourse.bass as bass
from concourse import mybir

F32 = mybir.dt.float32
F32R = mybir.dt.float32r
U8 = mybir.dt.uint8
ALU = mybir.AluOpType
ACT = mybir.ActivationFunctionType
AX = mybir.AxisListType.X

P = 128
NB = 8
S = 256
D = 512
NH = 16
SB = S // P
DC = D // P
HG = 4
NG = NH // HG
QD = P // HG
HD0 = S // NH
HD1 = D // NH
FF = 4 * D
FC = FF // P
EPS = 1e-5
FAR = 1.0e30
OFF = 10000.0
NEVER = 3.0e38
DMA = 16

NEG_LO, IS_LOW, ONE_AT, FAR_AT = range(4)


class Count:

    def __init__(self, sem, per, before=0):
        self.sem, self.per, self.before = sem, per, before

    def at(self, batch, k):
        return batch * self.per + (self.before + k)

    def wait(self, eng, batch, k):
        eng.wait_ge(self.sem, self.at(batch, k))


def every_batch(eng, body):
    body(0, True, False)
    with eng.Fori(1, NB - 1) as batch:
        body(batch, False, False)
    body(NB - 1, False, True)


class Links:

    def __init__(self, eng, sem):
        self.eng, self.sem, self.n, self.base = eng, sem, 0, 0

    def start(self, base):
        self.base, self.n = base, 0

    def add(self, ins):
        ins.then_inc(self.sem, 1)
        self.n += 1
        self.eng.wait_ge(self.sem, self.base + self.n)


def keep_rows(eng, links, g, batch, s, rows, six, two):
    links.add(eng.bn_stats(six[:], rows))
    eng.tensor_scalar(g["X"][:, batch, s, :], rows, 1.0, None, ALU.mult)
    links.add(eng.bn_aggr(two[:], six[:]))
    links.add(eng.tensor_scalar(g["moments"][:, batch, s, :], two[:], 1.0, None, ALU.mult))


def linked_batches(eng, sem, body, before, per):
    links = Links(eng, sem)

    def padded(batch, first, last):
        links.start(batch * per + before)
        body(batch, first, last, links)
        if links.n < per:
            eng.sem_inc(sem, per - links.n)
            eng.wait_ge(sem, links.base + per)
        assert links.n <= per, links.n

    every_batch(eng, padded)


def layer0_items(last):
    at = {0: [("q", 2)], 1: [("k", 2)], 2: [("q", 3)], 3: [("k", 3)], 4: [("v", 1)]}
    if not last:
        at.update({17: [("q", 0)], 18: [("k", 0)], 19: [("q", 1)], 20: [("k", 1)], 22: [("v", 0)]})
    for G in range(NG):
        at.setdefault(8 * G + 7, []).append(("turn", G))
        at.setdefault(min(8 * G + 8, 31), []).append(("spread", G))
    index = {name: n for n, name in enumerate(x for step in sorted(at) for x in at[step])}
    return at, index


def layer0(nc, d, g):
    STEPS, UNITS = 32, 16
    at_full, index_full = layer0_items(False)
    at_last, index_last = layer0_items(True)
    A_ITEMS = 5
    X, ident, sel, row, moments = g["X"], g["ident"], g["sel"], g["row"], g["moments"]
    ps = g["ps"]
    SC, PT, OB, IB = 0, 4, 6, 7

    with ExitStack() as ctx:
        def sb(name, shape, dt=F32):
            return ctx.enter_context(nc.sbuf_tensor(name, shape, dt))

        def sem(name):
            return g["whole"].enter_context(nc.semaphore("l0_" + name))

        w0 = sb("w0", [P, SB, 2 * D + S])
        b0 = sb("b0", [P, 2, NG])
        bv0 = sb("bv0", [P, S])
        x_in = sb("x_in", [P, SB, D])
        c_in = sb("c_in", [P, SB, D])
        m_in = sb("m_in", [P, D], U8)
        mask = sb("mask", [P, D])
        mask_done = sb("mask_done", [P, D])
        far = sb("far", [P, D])
        raw = sb("raw", [P, 2, D])
        q_hi = sb("q_hi", [P, D], F32R)
        q_low = sb("q_low", [P, D])
        k_rest = sb("k_rest", [P, D])
        q1 = sb("q1", [P, NG, D], F32R)
        q2 = sb("q2", [P, NG, D], F32R)
        k1 = sb("k1", [P, NG, D], F32R)
        k2 = sb("k2", [P, NG, D], F32R)
        v = sb("v", [P, DC, NH, 2 * HD0])
        nmax = sb("nmax", [P, 4, 2])
        prob = sb("prob", [P, 2, 2, D])
        probT = sb("probT", [P, 2, HG, DC, P])
        z = sb("z", [P, 2, DC, HG])
        rz = sb("rz", [P, DC * HG])
        rzT = sb("rzT", [HG, D])
        rz_wide = sb("rz_wide", [P, D])
        out_n = sb("out_n", [P, 2, D])
        mean_a = sb("mean_a", [P, SB, D])
        second = sb("second", [P, SB, D])
        std_a = sb("std_a", [P, SB, D])
        sums = sb("sums", [P, 4, SB])
        cnt = sb("cnt", [P, 2])
        x_mean = sb("x_mean", [P, SB])
        x_var = sb("x_var", [P, SB])
        x_rstd = sb("x_rstd", [P, SB])
        six = sb("six", [P, 6])
        two = sb("two", [P, 2])
        x_masked = sb("x_masked", [P, SB, D])
        scrap = sb("scrap", [P, D])

        s_set = sem("set")
        s_big = sem("big")
        s_v0 = sem("v0")
        s_load = Count(sem("load"), 3 * DMA)
        s_score = Count(sem("score"), STEPS)
        s_max = Count(sem("max"), STEPS)
        s_exp = Count(sem("exp"), STEPS)
        s_turn = Count(sem("turn"), 2 * STEPS)
        s_cpv = Count(sem("cpv"), STEPS)
        s_cpa = Count(sem("cpa"), STEPS)
        s_pv = Count(sem("pv"), UNITS)
        s_item = Count(sem("item"), len(index_full), A_ITEMS)
        s_free = Count(sem("free"), len(index_full), A_ITEMS)
        s_k1 = Count(sem("k1"), NG)
        s_kq = Count(sem("kq"), 2 * NG)
        s_low = Count(sem("low"), NG)
        s_gkq = Count(sem("gkq"), 2 * NG)
        s_gv = Count(sem("gv"), 2)
        s_rz = Count(sem("rz"), NG)
        s_norm = Count(sem("norm"), NG)
        s_re = [Count(sem(f"re{k}"), NG // 2 * 8 * DMA) for k in range(2)]
        s_stat = Count(sem("stat"), SB)
        s_fin_g = Count(sem("fin_g"), 2)
        s_fin_v = Count(sem("fin_v"), 2)
        s_fin_a = Count(sem("fin_a"), 1)
        s_link = sem("link")
        LINKS, LINKS0 = 60, 40

        def number_of(batch, name, n):
            if n >= 2 or (name, n) == ("v", 1):
                return batch, index_full[(name, n)] + 1
            if isinstance(batch, int) and batch == 0:
                return 0, [("q", 0), ("k", 0), ("q", 1), ("k", 1), ("v", 0)].index((name, n)) + 1 - A_ITEMS
            return batch - 1, index_full[(name, n)] + 1

        def item_at(batch, last, name, n):
            index = index_last if last else index_full
            return index[(name, n)] + 1

        wq, wk, wv = w0[:, :, 0:D], w0[:, :, D:2 * D], w0[:, :, 2 * D:2 * D + S]

        with nc.Block() as block:
            @block.sync
            def _(eng):
                for dst, src in ((w0, d["w0"]), (b0, d["b0"]), (bv0, d["bv0"]), (ident, d["ident"]),
                                 (sel, d["sel"]), (row, d["row"])):
                    eng.dma_start(dst[:], src).then_inc(s_set, DMA)

                def load(batch):
                    eng.dma_start(x_in[:], d["x"][batch].rearrange("(h p) t -> p h t", p=P)).then_inc(s_load.sem, DMA)
                    eng.dma_start(c_in[:], d["ctx"][batch].rearrange("(h p) t -> p h t", p=P)).then_inc(s_load.sem, DMA)
                    eng.dma_start(m_in[:], d["mask0"][batch].broadcast_to([P, D])).then_inc(s_load.sem, DMA)

                load(0)
                for dst, src in ((g["gb"], d["gb"]), (g["b_feat"], d["b_feat"]), (g["b_row"], d["b_row"]),
                                 (g["b1"], d["b1"]), (g["w_self"], d["w_self"])):
                    eng.dma_start(dst[:], src).then_inc(s_big, DMA)

                def batch_loads(batch, first, last):
                    if not last:
                        s_item.wait(eng, batch, item_at(batch, last, "v", 1))
                        s_stat.wait(eng, batch, SB)
                        load(batch + 1)
                    for G in range(NG):
                        s_norm.wait(eng, batch, G + 1)
                        if G == 0 and not first:
                            s_fin_g.wait(eng, batch - 1, 2)
                        for k in range(HG):
                            head = HG * (G % 2) + k
                            for j, dst in enumerate((mean_a, second)):
                                src = out_n[QD * k + HD0 * j:QD * k + HD0 * (j + 1), G % 2, :]
                                eng.dma_start(dst[HD0 * head:HD0 * (head + 1), G // 2, :], src).then_inc(s_re[G % 2].sem, DMA)

                every_batch(eng, batch_loads)
                eng.wait_ge(s_big, 5 * DMA)

            @block.tensor
            def _(eng):
                def scores(batch, m):
                    G, j, p = m // 8, m // 2 % 4, m % 2
                    if m % 8 == 0:
                        s_kq.wait(eng, batch, 2 * G + 2)
                        s_gkq.wait(eng, batch, 2 * G + 2)
                    for a, b in ((q1, k1), (q2, k2)):
                        for i in range(2):
                            r = slice(QD * (2 * p + i), QD * (2 * p + i + 1))
                            mm = eng.matmul(ps[:, SC + 2 * p + i, :], a[r, G, P * j:P * (j + 1)], b[r, G, :],
                                            start=(a is q1), stop=(a is q2))
                    mm.then_inc(s_score.sem, 1)

                def turn(batch, m):
                    for i in range(2):
                        (s_cpv, s_cpa)[i].wait(eng, batch, m)
                        for c in range(DC):
                            mm = eng.transpose(ps[:, PT + i, P * c:P * (c + 1)], prob[:, m % 2, i, P * c:P * (c + 1)],
                                               ident[:])
                        mm.then_inc(s_turn.sem, 1)

                def pv(batch, u, first):
                    G, j = u // 4, u % 4
                    s_cpv.wait(eng, batch, 2 * u + 2)
                    s_cpa.wait(eng, batch, 2 * u + 2)
                    if u % 8 == 0:
                        s_gv.wait(eng, batch, u // 8 + 1)
                    if j == 0 and not (first and u == 0):
                        s_norm.wait(eng, batch, G)
                    for c in range(DC):
                        for k in range(HG):
                            mm = eng.matmul(ps[QD * k:QD * (k + 1), OB, P * j:P * (j + 1)], v[:, c, HG * G + k, :],
                                            probT[:, u % 2, k, c, :], start=(c == 0), stop=(c == DC - 1))
                    mm.then_inc(s_pv.sem, 1)

                def item(batch, name, n, number):
                    if not (isinstance(batch, int) and batch == 0 and number == -A_ITEMS):
                        s_free.wait(eng, batch, number)
                    bank = ps[:, IB, :]
                    if name in "qk":
                        w, src = (wq, x_in) if name == "q" else (wk, c_in)
                        for c in range(SB):
                            mm = eng.matmul(bank, w[:, c, P * n:P * (n + 1)], src[:, c, :], start=(c == 0), stop=(c == SB - 1))
                    elif name == "v":
                        for t in range(DC):
                            for c in range(SB):
                                mm = eng.matmul(bank[:, P * t:P * (t + 1)], c_in[:, c, P * t:P * (t + 1)],
                                                wv[:, c, P * n:P * (n + 1)], start=(c == 0), stop=(c == SB - 1))
                    elif name == "turn":
                        s_rz.wait(eng, batch, n + 1)
                        for j in range(DC):
                            mm = eng.transpose(ps[0:HG, IB, P * j:P * (j + 1)], rz[:, HG * j:HG * (j + 1)], ident[:])
                    else:
                        mm = eng.matmul(bank, sel[:], rzT[:], start=True, stop=True)
                    mm.then_inc(s_item.sem, 1)

                eng.wait_ge(s_set, 6 * DMA)
                s_load.wait(eng, 0, 3 * DMA)
                for n, (name, tile) in enumerate((("q", 0), ("k", 0), ("q", 1), ("k", 1), ("v", 0))):
                    item(0, name, tile, n - A_ITEMS)
                scores(0, 0)
                scores(0, 1)

                def batch_steps(batch, first, last):
                    at, index = (at_last, index_last) if last else (at_full, index_full)
                    for m in range(STEPS):
                        s_exp.wait(eng, batch, m + 1)
                        if m + 2 < STEPS:
                            scores(batch, m + 2)
                        elif not last:
                            scores(batch + 1, m + 2 - STEPS)
                        turn(batch, m)
                        if m % 2 == 0 and m:
                            pv(batch, m // 2 - 1, first)
                        for name, n in at.get(m, []):
                            if m == STEPS - 1 and name == "spread":
                                pv(batch, UNITS - 1, first)
                            if m == 17 and name == "q":
                                s_load.wait(eng, batch + 1, 3 * DMA)
                            item(batch, name, n, index[(name, n)])

                every_batch(eng, batch_steps)

            @block.vector
            def _(eng):
                def maxima(batch, m):
                    s_score.wait(eng, batch, m + 1)
                    eng.tensor_reduce(nmax[:, m % 4, :], ps[:, SC + 2 * (m % 2):SC + 2 * (m % 2) + 2, :], AX, ALU.max,
                                      negate=True).then_inc(s_max.sem, 1)

                def masks(links):
                    links.add(eng.tensor_copy(mask[:], m_in[:]))
                    links.add(eng.tensor_scalar(far[:], mask[:], 1.0, row[:, FAR_AT:FAR_AT + 1], ALU.subtract, ALU.mult))

                def statistics(batch, links):
                    eng.tensor_reduce(cnt[:, 0:1], mask[:], AX, ALU.add)
                    for h in range(SB):
                        eng.tensor_tensor_reduce(x_masked[:, h, :], x_in[:, h, :], mask[:], 1.0, 0.0, ALU.mult, ALU.add,
                                                 sums[:, 0, h:h + 1]).then_inc(s_stat.sem, 1)
                    s_stat.wait(eng, batch, SB)
                    for h in range(SB):
                        links.add(eng.tensor_tensor_reduce(scrap[:], x_masked[:, h, :], x_masked[:, h, :], 1.0, 0.0,
                                                           ALU.mult, ALU.add, sums[:, 1, h:h + 1]))
                    links.add(eng.tensor_scalar(X[:, batch, :, :], x_masked[:], 1.0, None, ALU.mult))

                def moments_of_x(links):
                    links.add(eng.reciprocal(cnt[:, 1:2], cnt[:, 0:1]))
                    links.add(eng.tensor_scalar(x_mean[:], sums[:, 0, :], cnt[:, 1:2], None, ALU.mult))
                    links.add(eng.tensor_scalar(x_var[:], sums[:, 1, :], cnt[:, 1:2], None, ALU.mult))
                    links.add(eng.tensor_tensor(sums[:, 2, :], x_mean[:], x_mean[:], ALU.mult))
                    links.add(eng.tensor_tensor(x_var[:], x_var[:], sums[:, 2, :], ALU.subtract))
                    links.add(eng.tensor_scalar(x_var[:], x_var[:], 0.0, EPS, ALU.max, ALU.add))

                def tile(batch, name, n, first, links):
                    if name == "q":
                        s_free.wait(eng, *number_of(batch, name, n))
                        if not first:
                            s_score.wait(eng, batch - 1, 8 * n + 8)
                        links.add(eng.tensor_copy(q_hi[:], raw[:, 0, :]))
                        eng.scalar_tensor_tensor(out=q1[:, n, :], in0=q_hi[:].bitcast(F32), scalar=row[:, NEG_LO:NEG_LO + 1],
                                                 in1=raw[:, 0, :], op0=ALU.mult, op1=ALU.add).then_inc(s_kq.sem, 1)
                    else:
                        s_free.wait(eng, *number_of(batch, name, n))
                        if not first:
                            s_score.wait(eng, batch - 1, 8 * n + 8)
                        eng.tensor_copy(k1[:, n, :], raw[:, 1, :]).then_inc(s_k1.sem, 1)
                        s_gkq.wait(eng, batch, 2 * n + 2)
                        eng.scalar_tensor_tensor(out=k2[:, n, :], in0=k_rest[:], scalar=row[:, IS_LOW:IS_LOW + 1],
                                                 in1=far[:], op0=ALU.mult, op1=ALU.add).then_inc(s_kq.sem, 1)

                def values(batch, hf, first):
                    s_item.wait(eng, *number_of(batch, "v", hf))
                    if not first:
                        s_pv.wait(eng, batch - 1, 8 * hf + 8)
                        s_gv.wait(eng, batch - 1, hf + 1)
                    half = slice(NH // 2 * hf, NH // 2 * (hf + 1))
                    eng.tensor_tensor(v[:, :, half, 0:HD0],
                                      ps[:, IB, :].rearrange("p (c h e) -> p c h e", c=DC, e=HD0),
                                      bv0[:, P * hf:P * (hf + 1)].rearrange("p (h e) -> p h e", e=HD0)[:, None, :, :]
                                      .broadcast_to([P, DC, NH // 2, HD0]), ALU.add).then_inc(s_free.sem, 1)

                links = Links(eng, s_link)
                links.start(0)
                eng.wait_ge(s_set, 6 * DMA)
                links.add(eng.tensor_scalar(b0[:, 0, :], b0[:, 0, :], float(HD0) ** -0.5, None, ALU.mult))
                eng.memset(cnt[:], 0.0).then_inc(s_v0, 1)
                s_load.wait(eng, 0, 3 * DMA)
                masks(links)
                statistics(0, links)
                for name, n in (("q", 0), ("k", 0), ("q", 1), ("k", 1)):
                    tile(0, name, n, True, links)
                values(0, 0, True)
                maxima(0, 0)
                maxima(0, 1)
                if links.n < LINKS0:
                    eng.sem_inc(s_link, LINKS0 - links.n)

                def batch_steps(batch, first, last, links):
                    for m in range(STEPS):
                        u = m // 2
                        if m + 2 < STEPS:
                            maxima(batch, m + 2)
                        elif not last:
                            maxima(batch + 1, m + 2 - STEPS)
                        s_turn.wait(eng, batch, 2 * m + 1)
                        if m % 2 == 0 and not (first and u < 2):
                            s_pv.wait(eng, batch, u - 1)
                        eng.tensor_copy(probT[:, u % 2, 2 * (m % 2), :, :].rearrange("p c q -> p (c q)"),
                                        ps[:, PT, :]).then_inc(s_cpv.sem, 1)
                        if m % 8 == 7:
                            G = m // 8
                            s_exp.wait(eng, batch, m + 1)
                            if G:
                                s_item.wait(eng, batch, item_at(batch, last, "turn", G - 1))
                            elif not first:
                                s_item.wait(eng, batch - 1, index_full[("turn", NG - 1)] + 1)
                            eng.reciprocal(rz[:], z[:, G % 2, :, :].rearrange("p j h -> p (j h)")).then_inc(s_rz.sem, 1)
                        if (m % 8 == 1 and m > 1) or m == STEPS - 1:
                            G = (m - 1) // 8 if m == STEPS - 1 else m // 8 - 1
                            s_free.wait(eng, batch, item_at(batch, last, "spread", G))
                            s_pv.wait(eng, batch, 4 * G + 4)
                            if G >= 2:
                                s_re[G % 2].wait(eng, batch, 8 * DMA)
                            elif not first:
                                s_re[G % 2].wait(eng, batch - 1, 2 * 8 * DMA)
                            eng.tensor_tensor(out_n[:, G % 2, :], ps[:, OB, :], rz_wide[:], ALU.mult).then_inc(s_norm.sem, 1)
                        if m in (1, 2, 3, 4):
                            tile(batch, "qk"[(m + 1) % 2], 2 + (m - 1) // 2, first, links)
                        if m == 5:
                            values(batch, 1, first)
                        if not first and m == 8:
                            finish_variance(batch - 1)
                        if not first and m == 10:
                            finish_norm(batch - 1, links)
                        if not first and m == 14:
                            finish_mask(batch - 1, links)
                        if m == 16:
                            links.add(eng.tensor_copy(mask_done[:], mask[:]))
                            moments_of_x(links)
                        if m == 17 and not last:
                            s_load.wait(eng, batch + 1, 3 * DMA)
                            masks(links)
                        if m == 24 and not last:
                            statistics(batch + 1, links)
                        if m in (18, 19, 20, 21) and not last:
                            tile(batch + 1, "qk"[m % 2], (m - 18) // 2, False, links)
                        if m == 23 and not last:
                            values(batch + 1, 0, False)

                def finish_variance(batch):
                    s_fin_g.wait(eng, batch, 1)
                    eng.tensor_scalar(std_a[:], std_a[:], 0.0, None, ALU.max).then_inc(s_fin_v.sem, 1)

                def finish_norm(batch, links):
                    s_fin_a.wait(eng, batch, 1)
                    links.add(eng.reciprocal(x_rstd[:], x_rstd[:]))
                    for h in range(SB):
                        ins = eng.tensor_scalar(X[:, batch, h, :], X[:, batch, h, :], x_mean[:, h:h + 1],
                                                x_rstd[:, h:h + 1], ALU.subtract, ALU.mult)
                    ins.then_inc(s_fin_v.sem, 1)

                def finish_mask(batch, links):
                    s_fin_g.wait(eng, batch, 2)
                    for h in range(SB):
                        links.add(eng.tensor_tensor(scrap[:], X[:, batch, h, :], mask_done[:], ALU.mult))
                        keep_rows(eng, links, g, batch, h, scrap[:], six, two)

                linked_batches(eng, s_link, batch_steps, LINKS0, LINKS)
                links.start(NB * LINKS + LINKS0)
                finish_variance(NB - 1)
                finish_norm(NB - 1, links)
                finish_mask(NB - 1, links)

            @block.scalar
            def _(eng):
                def probabilities(batch, m):
                    G, j, p = m // 8, m // 2 % 4, m % 2
                    s_max.wait(eng, batch, m + 1)
                    for i in range(2):
                        ins = eng.activation(prob[:, m % 2, i, :], ps[:, SC + 2 * p + i, :], ACT.Exp,
                                             bias=nmax[:, m % 4, i:i + 1],
                                             accum_out=z[:, G % 2, j, 2 * p + i:2 * p + i + 1])
                    ins.then_inc(s_exp.sem, 1)

                def take(batch, name, n, first, number):
                    s_item.wait(eng, batch, number + 1)
                    own = batch + 1 if n < 2 and name in "qkv" else batch
                    if name in "qk":
                        k = 0 if name == "q" else 1
                        if not (first and n == 0):
                            s_kq.wait(eng, own, 2 * n + k - 1)
                            s_gkq.wait(eng, own, 2 * n + k - 1)
                        eng.activation(raw[:, k, :], ps[:, IB, :], ACT.Identity, bias=b0[:, k, n:n + 1],
                                       scale=(float(HD0) ** -0.5 if k == 0 else 1.0)).then_inc(s_free.sem, 1)
                    elif name == "turn":
                        eng.activation(rzT[:], ps[0:HG, IB, :], ACT.Copy).then_inc(s_free.sem, 1)
                    elif name == "spread":
                        if not (first and n == 0):
                            s_norm.wait(eng, batch, n)
                        eng.activation(rz_wide[:], ps[:, IB, :], ACT.Copy).then_inc(s_free.sem, 1)

                eng.wait_ge(s_v0, 1)
                for n, (name, tile) in enumerate((("q", 0), ("k", 0), ("q", 1), ("k", 1))):
                    s_item.wait(eng, 0, n + 1 - A_ITEMS)
                    k = n % 2
                    if tile:
                        s_kq.wait(eng, 0, 1 + k)
                        s_gkq.wait(eng, 0, 1 + k)
                    eng.activation(raw[:, k, :], ps[:, IB, :], ACT.Identity, bias=b0[:, k, tile:tile + 1],
                                   scale=(float(HD0) ** -0.5 if k == 0 else 1.0)).then_inc(s_free.sem, 1)
                probabilities(0, 0)

                def finish_roots(batch):
                    s_fin_v.wait(eng, batch, 1)
                    eng.activation(std_a[:], std_a[:], ACT.Sqrt)
                    eng.activation(x_rstd[:], x_var[:], ACT.Sqrt).then_inc(s_fin_a.sem, 1)

                def batch_steps(batch, first, last):
                    at, index = (at_last, index_last) if last else (at_full, index_full)
                    for m in range(STEPS):
                        u = m // 2
                        s_turn.wait(eng, batch, 2 * m)
                        if m + 1 < STEPS:
                            probabilities(batch, m + 1)
                        elif not last:
                            probabilities(batch + 1, 0)
                        s_turn.wait(eng, batch, 2 * m + 2)
                        if m % 2 == 0 and not (first and u < 2):
                            s_pv.wait(eng, batch, u - 1)
                        eng.activation(probT[:, u % 2, 2 * (m % 2) + 1, :, :].rearrange("p c q -> p (c q)"),
                                       ps[:, PT + 1, :], ACT.Copy).then_inc(s_cpa.sem, 1)
                        for name, n in at.get(m, []):
                            if name != "v":
                                take(batch, name, n, first and m < 8, index[(name, n)])
                        if not first and m == 9:
                            finish_roots(batch - 1)

                every_batch(eng, batch_steps)
                finish_roots(NB - 1)

            @block.gpsimd
            def _(eng):
                def parts(batch, name, n, first):
                    if name == "q":
                        if not first:
                            s_score.wait(eng, batch - 1, 8 * n + 8)
                        s_free.wait(eng, *number_of(batch, name, n))
                        low, one = (row[:, k:k + 1].broadcast_to([P, D]) for k in (IS_LOW, ONE_AT))
                        eng.tensor_tensor(q_low[:], raw[:, 0, :], low, ALU.mult).then_inc(s_low.sem, 1)
                        s_low.wait(eng, batch, n + 1)
                        eng.tensor_tensor(q2[:, n, :], q_low[:], one, ALU.add).then_inc(s_gkq.sem, 1)
                    else:
                        s_k1.wait(eng, batch, n + 1)
                        if not (first and n == 0):
                            s_kq.wait(eng, batch, 2 * n)
                        eng.tensor_tensor(k_rest[:], raw[:, 1, :], k1[:, n, :].bitcast(F32), ALU.subtract)\
                           .then_inc(s_gkq.sem, 1)

                def squares(batch, hf):
                    s_free.wait(eng, *number_of(batch, "v", hf))
                    half = slice(NH // 2 * hf, NH // 2 * (hf + 1))
                    vv = v[:, :, half, 0:HD0]
                    eng.tensor_tensor(v[:, :, half, HD0:2 * HD0], vv, vv, ALU.mult).then_inc(s_gv.sem, 1)

                def finish_a(batch):
                    for by_parity in s_re:
                        by_parity.wait(eng, batch, NG // 2 * 8 * DMA)
                    eng.tensor_tensor(std_a[:], mean_a[:], mean_a[:], ALU.mult).then_inc(s_g, 1)
                    eng.wait_ge(s_g, 2 * batch + 1)
                    eng.tensor_tensor(std_a[:], second[:], std_a[:], ALU.subtract).then_inc(s_fin_g.sem, 1)

                def finish_b(batch):
                    eng.wait_ge(s_set, 6 * DMA)
                    s_fin_v.wait(eng, batch, 2)
                    s_fin_a.wait(eng, batch, 1)
                    eng.tensor_tensor(X[:, batch, :, :], X[:, batch, :, :], std_a[:], ALU.mult).then_inc(s_g, 1)
                    eng.wait_ge(s_set, 6 * DMA)
                    eng.wait_ge(s_g, 2 * batch + 2)
                    eng.tensor_tensor(X[:, batch, :, :], X[:, batch, :, :], mean_a[:], ALU.add).then_inc(s_fin_g.sem, 1)

                s_g = sem("g")
                eng.wait_ge(s_set, 6 * DMA)
                for name, n in (("q", 0), ("k", 0), ("q", 1), ("k", 1)):
                    parts(0, name, n, True)
                squares(0, 0)

                def batch_parts(batch, first, last):
                    for name, n in (("q", 2), ("k", 2), ("q", 3), ("k", 3)):
                        parts(batch, name, n, first)
                    squares(batch, 1)
                    if not first:
                        finish_a(batch - 1)
                        finish_b(batch - 1)
                    if not last:
                        for name, n in (("q", 0), ("k", 0), ("q", 1), ("k", 1)):
                            parts(batch + 1, name, n, False)
                        squares(batch + 1, 0)

                every_batch(eng, batch_parts)
                finish_a(NB - 1)
                finish_b(NB - 1)


def layer1_items(last):
    at = {0: [("q", 1)], 1: [("k", 1)], 2: [("out", 0)], 3: [("out", 1)], 4: [("v", 1)]}
    if not last:
        at.update({5: [("x", 0)], 6: [("x", 1)], 7: [("q", 0)], 9: [("k", 0)], 10: [("v", 0)]})
    for T in range(NG):
        at.setdefault(4 * T + 3, []).append(("turn", T))
        at.setdefault(min(4 * T + 4, 15), []).append(("spread", T))
    return at


def attention(nc, d, g, which):
    cross = which == "cross"
    layer = 1 if cross else 0
    STEPS, UNITS = 16, 8
    BEFORE = 5
    X, ident, sel, moments, rstd, ps = g["X"], g["ident"], g["sel"], g["moments"], g["rstd"], g["ps"]
    w = g["w_cross"] if cross else g["w_self"]
    wq, wk, wv, wo = (w[:, :, D * k:D * (k + 1)] for k in range(4))
    b_v, b_o = g["b_row"][:, 2 * layer, :], g["b_row"][:, 2 * layer + 1, :]
    SC, PT, OB, IB = 0, 4, 6, 7
    NM = NB if cross else 1
    SCALE = float(HD1) ** -0.5

    def items_of(first, last):
        at = {m: [x for x in names if not (first and x[0] == "out")] for m, names in layer1_items(last).items()}
        return at, {x: n for n, x in enumerate(x for m in sorted(at) for x in at[m])}

    full, full_index = items_of(False, False)
    FIRST_SHORT = 2
    ahead = [("x", 0), ("x", 1), ("q", 0), ("k", 0), ("v", 0)]

    with ExitStack() as ctx:
        def sb(name, shape, dt=F32):
            return ctx.enter_context(nc.sbuf_tensor(f"{which}_{name}", shape, dt))

        def sem(name):
            return g["whole"].enter_context(nc.semaphore(f"{which}_{name}"))

        mask = sb("mask", [P, NM, SB, S])
        off = sb("off", [P, SB, S])
        ctxT = sb("ctxT", [P, DC, S]) if cross else None
        xn = sb("xn", [P, SB, D])
        xT = sb("xT", [P, DC, S])
        raw = sb("raw", [P, 2, 2, S])
        qh, ql, kh, kl = (sb(n, [P, NG, S], F32R) for n in ("qh", "ql", "kh", "kl"))
        v = sb("v", [P, SB, D])
        t = sb("t", [P, 2, 2, S])
        nmax = sb("nmax", [P, 4, 2])
        prob = sb("prob", [P, 2, 2, S])
        probT = sb("probT", [P, 2, HG, SB, P])
        z = sb("z", [P, 2, SB, HG])
        rz = sb("rz", [P, SB * HG])
        rzT = sb("rzT", [HG, S])
        rz_wide = sb("rz_wide", [P, S])
        heads = sb("heads", [P, NG, S])
        part = sb("part", [P, D])
        six = sb("six", [P, 6])
        two = sb("two", [P, 2])

        s_in = sem("in")
        s_w = sem("w")
        s_w2 = sem("w2")
        s_ctx = Count(sem("ctx"), DMA)
        s_t = Count(sem("t"), STEPS)
        s_var = sem("var")
        s_root = sem("root")
        s_xn = Count(sem("xn"), SB)
        s_score = Count(sem("score"), STEPS)
        s_max = Count(sem("max"), STEPS)
        s_exp = Count(sem("exp"), STEPS)
        s_turn = Count(sem("turn"), STEPS)
        s_cpv = Count(sem("cpv"), STEPS // 4)
        s_cpa = Count(sem("cpa"), STEPS - STEPS // 4)
        s_pv = Count(sem("pv"), UNITS)
        s_item = Count(sem("item"), len(full_index), BEFORE - FIRST_SHORT)
        s_free = Count(sem("free"), len(full_index), BEFORE - FIRST_SHORT)
        s_hi = Count(sem("hi"), 4)
        s_lo = Count(sem("lo"), 4)
        s_rz = Count(sem("rz"), NG)
        s_norm = Count(sem("norm"), NG)
        s_link = sem("link")
        LINKS, LINKS0 = 40, 10

        def index_of(first, last):
            index = items_of(first, last)[1]
            return {x: n + (FIRST_SHORT if first else 0) for x, n in index.items()}

        def number_of(batch, name, n):
            if name == "out":
                if isinstance(batch, int) and batch == NB - 1:
                    return NB - 1, len(index_of(False, True)) + n + 1
                return batch + 1, full_index[(name, n)] + 1
            if n == 1 and name != "x" or name in ("turn", "spread"):
                if isinstance(batch, int):
                    return batch, index_of(batch == 0, batch == NB - 1)[(name, n)] + 1
                return batch, full_index[(name, n)] + 1
            if isinstance(batch, int) and batch == 0:
                return 0, ahead.index((name, n)) + 1 - (BEFORE - FIRST_SHORT)
            if isinstance(batch, int) and batch == 1:
                return 0, index_of(True, False)[(name, n)] + 1
            return batch - 1, full_index[(name, n)] + 1

        def owner(batch, name, n):
            if name == "out":
                return batch - 1
            return batch + 1 if name == "x" or (name in "qkv" and n == 0) else batch

        def copied(eng, batch, m):
            s_cpv.wait(eng, batch, m // 4 + 1)
            s_cpa.wait(eng, batch, m - m // 4)

        with nc.Block() as block:
            @block.sync
            def _(eng):
                if cross:
                    eng.dma_start(ctxT[:], d["ctxT"][0].rearrange("(c p) s -> p c s", p=P)).then_inc(s_ctx.sem, DMA)
                for n in range(NM):
                    src = (d["mask_cross"][n] if cross else d["mask_self"][n]).rearrange("a (j p) k -> p (a j) k", p=P)
                    eng.dma_start(mask[:, n, :, :], src).then_inc(s_in, DMA)
                if not cross:
                    eng.dma_start(g["w_cross"][:], d["w_cross"]).then_inc(s_w, DMA)
                else:
                    eng.dma_start(g["w_self"][:], d["w1"]).then_inc(s_w, DMA)

                def batch_loads(batch, first, last):
                    if not last:
                        s_item.wait(eng, *number_of(batch, "v", 1))
                        eng.dma_start(ctxT[:], d["ctxT"][batch + 1].rearrange("(c p) s -> p c s", p=P))\
                           .then_inc(s_ctx.sem, DMA)

                if cross:
                    every_batch(eng, batch_loads)
                    w2 = g["w_cross"][:].rearrange("p c (q n) -> p (c q) n", n=D)
                    s_item.wait(eng, *number_of(NB - 1, "v", 1))
                    for c in range(DC):
                        eng.dma_start(w2[:, 4 * c:4 * c + 3, :], d["w2"][:, 4 * c:4 * c + 3, :]).then_inc(s_w2, DMA)
                    s_item.wait(eng, *number_of(NB - 1, "out", 1))
                    for c in range(DC):
                        eng.dma_start(w2[:, 4 * c + 3, :], d["w2"][:, 4 * c + 3, :]).then_inc(s_w2, DMA)
                    eng.wait_ge(s_w2, 8 * DMA)
                eng.wait_ge(s_w, DMA)

            @block.tensor
            def _(eng):
                def scores(batch, m):
                    T, j, p = m // 4, m // 2 % 2, m % 2
                    if m % 8 == 0:
                        s_hi.wait(eng, batch, 2 * (m // 8) + 2)
                        s_lo.wait(eng, batch, 2 * (m // 8) + 2)
                    for n, (a, b) in enumerate(((qh, kh), (qh, kl), (ql, kh))):
                        for i in range(2):
                            r = slice(QD * (2 * p + i), QD * (2 * p + i + 1))
                            mm = eng.matmul(ps[:, SC + 2 * p + i, 0:S], a[r, T, P * j:P * (j + 1)], b[r, T, :],
                                            start=(n == 0), stop=(n == 2))
                    mm.then_inc(s_score.sem, 1)

                def turn(batch, m):
                    if m >= 2:
                        copied(eng, batch, m - 2)
                    else:
                        copied(eng, batch, -1)
                    for i in range(2):
                        for c in range(SB):
                            k = SB * i + c
                            mm = eng.transpose(ps[:, PT + m % 2, P * k:P * (k + 1)], prob[:, m % 2, i, P * c:P * (c + 1)],
                                               ident[:])
                    mm.then_inc(s_turn.sem, 1)

                def pv(batch, u, first):
                    T, j = u // 2, u % 2
                    copied(eng, batch, 2 * u + 1)
                    if u % 4 == 0:
                        s_free.wait(eng, *number_of(batch, "v", u // 4))
                    if j == 0 and not (first and u == 0):
                        s_norm.wait(eng, batch, T)
                    for c in range(SB):
                        for k in range(HG):
                            mm = eng.matmul(ps[QD * k:QD * (k + 1), OB, P * j:P * (j + 1)],
                                            v[:, c, QD * (HG * T + k):QD * (HG * T + k + 1)], probT[:, u % 2, k, c, :],
                                            start=(c == 0), stop=(c == SB - 1))
                    mm.then_inc(s_pv.sem, 1)

                def item(batch, name, n, own):
                    where, number = number_of(own, name, n)
                    if not (name == "x" and isinstance(own, int) and own == 0 and n == 0):
                        s_free.wait(eng, where, number - 1)
                    bank = ps[:, IB, :]
                    if name == "x":
                        s_xn.wait(eng, own, SB)
                        for c in range(2):
                            for s in range(SB):
                                mm = eng.transpose(bank[:, S * c + P * s:S * c + P * (s + 1)],
                                                   xn[:, s, P * (2 * n + c):P * (2 * n + c + 1)], ident[:])
                    elif name in "qk":
                        wt, src = (wq, xT) if name == "q" else (wk, ctxT if cross else xT)
                        if cross and name == "k" and n == 0:
                            s_ctx.wait(eng, own, DMA)
                        for T in range(2):
                            for c in range(DC):
                                mm = eng.matmul(bank[:, S * T:S * (T + 1)], wt[:, c, P * (2 * n + T):P * (2 * n + T + 1)],
                                                src[:, c, :], start=(c == 0), stop=(c == DC - 1))
                    elif name == "v":
                        src = ctxT if cross else xT
                        for s in range(SB):
                            for c in range(DC):
                                mm = eng.matmul(bank[:, S * s:S * (s + 1)], src[:, c, P * s:P * (s + 1)],
                                                wv[:, c, S * n:S * (n + 1)], start=(c == 0), stop=(c == DC - 1))
                    elif name == "out":
                        if n == 0:
                            s_norm.wait(eng, own, NG)
                        for T in range(NG):
                            mm = eng.matmul(bank, heads[:, T, P * n:P * (n + 1)], wo[:, T, :], start=(T == 0), stop=(T == NG - 1))
                    elif name == "turn":
                        s_rz.wait(eng, own, n + 1)
                        for j in range(SB):
                            mm = eng.transpose(ps[0:HG, IB, P * j:P * (j + 1)], rz[:, HG * j:HG * (j + 1)], ident[:])
                    else:
                        mm = eng.matmul(bank[:, 0:S], sel[:], rzT[:], start=True, stop=True)
                    mm.then_inc(s_item.sem, 1)

                for name, n in ahead:
                    item(0, name, n, 0)
                scores(0, 0)
                scores(0, 1)

                def batch_steps(batch, first, last):
                    at, _ = items_of(first, last)
                    for m in range(STEPS):
                        s_exp.wait(eng, batch, m + 1)
                        if m + 2 < STEPS:
                            scores(batch, m + 2)
                        elif not last:
                            scores(batch + 1, m + 2 - STEPS)
                        turn(batch, m)
                        if m % 2 == 0 and m:
                            pv(batch, m // 2 - 1, first)
                        for name, n in at.get(m, []):
                            if m == STEPS - 1 and name == "spread":
                                pv(batch, UNITS - 1, first)
                            item(batch, name, n, owner(batch, name, n))

                every_batch(eng, batch_steps)
                item(None, "out", 0, NB - 1)
                item(None, "out", 1, NB - 1)

            @block.vector
            def _(eng):
                def mask_off(batch, links):
                    n = batch if cross else 0
                    links.add(eng.tensor_scalar(off[:], mask[:, n, :, :], -1.0, 1.0, ALU.mult, ALU.add))
                    links.add(eng.tensor_scalar(off[:], off[:], OFF, None, ALU.mult))

                def maxima(batch, m):
                    i, j = m % 2, m // 2 % 2
                    s_score.wait(eng, batch, m + 1)
                    n = batch if cross else 0
                    eng.scalar_tensor_tensor(out=t[:, i, :, :], in0=ps[:, SC + 2 * i:SC + 2 * i + 2, 0:S], scalar=-SCALE,
                                             in1=mask[:, n, j, :][:, None, :].broadcast_to([P, 2, S]),
                                             op0=ALU.mult, op1=ALU.mult).then_inc(s_t.sem, 1)
                    eng.wait_ge(s_in, NM * DMA)
                    s_t.wait(eng, batch, m + 1)
                    for k in range(2):
                        ins = eng.tensor_tensor_reduce(t[:, i, k, :], t[:, i, k, :], off[:, j, :], 1.0, NEVER,
                                                       ALU.add, ALU.min, nmax[:, m % 4, k:k + 1])
                    ins.then_inc(s_max.sem, 1)

                def layer_norm(batch):
                    for s in range(SB):
                        eng.tensor_scalar(xn[:, s, :], X[:, batch, s, :], moments[:, batch, s, 0:1],
                                          rstd[:, batch, s:s + 1], ALU.subtract, ALU.mult).then_inc(s_xn.sem, 1)

                def high(batch, name, n, first):
                    k = 0 if name == "q" else 1
                    s_free.wait(eng, *number_of(batch, name, n))
                    if not first:
                        s_score.wait(eng, batch - 1, 8 * n + 8)
                    eng.tensor_copy((qh, kh)[k][:, 2 * n:2 * n + 2, :], raw[:, k, :, :]).then_inc(s_hi.sem, 1)

                def values(batch, n, first):
                    s_item.wait(eng, *number_of(batch, "v", n))
                    if not first:
                        s_pv.wait(eng, batch - 1, 4 * n + 4)
                    eng.tensor_tensor(v[:, :, S * n:S * (n + 1)], ps[:, IB, :].rearrange("p (s e) -> p s e", s=SB),
                                      b_v[:, S * n:S * (n + 1)][:, None, :].broadcast_to([P, SB, S]), ALU.add)\
                       .then_inc(s_free.sem, 1)

                def residual(batch, s, links):
                    s_item.wait(eng, *number_of(batch, "out", s))
                    eng.tensor_tensor(part[:], ps[:, IB, :], b_o, ALU.add).then_inc(s_free.sem, 1)
                    s_free.wait(eng, *number_of(batch, "out", s))
                    links.add(eng.tensor_tensor(part[:], X[:, batch, s, :], part[:], ALU.add))
                    keep_rows(eng, links, g, batch, s, part[:], six, two)

                links = Links(eng, s_link)
                links.start(0)
                roots_of_variances(eng, g, s_var, s_root, links)
                layer_norm(0)
                high(0, "q", 0, True)
                high(0, "k", 0, True)
                values(0, 0, True)
                eng.wait_ge(s_in, NM * DMA)
                mask_off(0, links)
                maxima(0, 0)
                maxima(0, 1)
                eng.sem_inc(s_link, LINKS0 - links.n)

                def batch_steps(batch, first, last, links):
                    for m in range(STEPS):
                        u, T = m // 2, m // 4
                        if m + 2 < STEPS:
                            maxima(batch, m + 2)
                        elif not last:
                            if m + 2 == STEPS and cross:
                                s_max.wait(eng, batch, STEPS)
                                mask_off(batch + 1, links)
                            maxima(batch + 1, m + 2 - STEPS)
                        if m % 4 == 0:
                            s_turn.wait(eng, batch, m + 1)
                            if not (first and u < 2):
                                s_pv.wait(eng, batch, u - 1)
                            eng.tensor_copy(probT[:, u % 2, 2 * (m % 2):2 * (m % 2) + 2, :, :]
                                            .rearrange("p h c q -> p (h c q)"), ps[:, PT + m % 2, :]).then_inc(s_cpv.sem, 1)
                        if m % 4 == 3:
                            s_exp.wait(eng, batch, m + 1)
                            if T:
                                s_item.wait(eng, *number_of(batch, "turn", T - 1))
                            elif not first:
                                s_item.wait(eng, *number_of(batch - 1, "turn", NG - 1))
                            eng.reciprocal(rz[:], z[:, T % 2, :, :].rearrange("p j h -> p (j h)")).then_inc(s_rz.sem, 1)
                        if (m % 4 == 1 and m > 1) or m == STEPS - 1:
                            G = NG - 1 if m == STEPS - 1 else T - 1
                            s_free.wait(eng, *number_of(batch, "spread", G))
                            s_pv.wait(eng, batch, 2 * G + 2)
                            if G == 0 and not first:
                                s_item.wait(eng, *number_of(batch - 1, "out", 1))
                            eng.tensor_tensor(heads[:, G, :], ps[:, OB, 0:S], rz_wide[:], ALU.mult).then_inc(s_norm.sem, 1)
                        if m in (0, 1):
                            high(batch, "qk"[m], 1, first)
                        if m in (2, 3) and not first:
                            residual(batch - 1, m - 2, links)
                        if m == 4:
                            values(batch, 1, first)
                            if not last:
                                s_item.wait(eng, *number_of(batch, "x", 1))
                                layer_norm(batch + 1)
                        if m in (8, 10) and not last:
                            high(batch + 1, "qk"[m // 2 - 4], 0, False)
                        if m == 11 and not last:
                            values(batch + 1, 0, False)

                linked_batches(eng, s_link, batch_steps, LINKS0, LINKS)
                links.start(NB * LINKS + LINKS0)
                for s in range(SB):
                    residual(NB - 1, s, links)

            @block.scalar
            def _(eng):
                def probabilities(batch, m):
                    T, j, p = m // 4, m // 2 % 2, m % 2
                    s_max.wait(eng, batch, m + 1)
                    for i in range(2):
                        ins = eng.activation(prob[:, m % 2, i, :], t[:, p, i, :], ACT.Exp, scale=-1.0,
                                             bias=nmax[:, m % 4, i:i + 1],
                                             accum_out=z[:, T % 2, j, 2 * p + i:2 * p + i + 1])
                    ins.then_inc(s_exp.sem, 1)

                def take(own, name, n, first):
                    s_item.wait(eng, *number_of(own, name, n))
                    if name == "x":
                        for c in range(2):
                            ins = eng.activation(xT[:, 2 * n + c, :], ps[:, IB, S * c:S * (c + 1)], ACT.Identity,
                                                 bias=g["gb"][:, layer, 1, 2 * n + c:2 * n + c + 1],
                                                 scale=g["gb"][:, layer, 0, 2 * n + c:2 * n + c + 1])
                    elif name in "qk":
                        k = 0 if name == "q" else 1
                        if not (n == 0 and first):
                            s_hi.wait(eng, own, 2 * n + k - 1)
                            s_lo.wait(eng, own, 2 * n + k - 1)
                        for T in range(2):
                            ins = eng.activation(raw[:, k, T, :], ps[:, IB, S * T:S * (T + 1)], ACT.Identity,
                                                 bias=g["b_feat"][:, 2 * layer + k, 2 * n + T:2 * n + T + 1])
                    elif name == "turn":
                        ins = eng.activation(rzT[:], ps[0:HG, IB, 0:S], ACT.Copy)
                    else:
                        if not (first and n == 0):
                            s_norm.wait(eng, own, n)
                        ins = eng.activation(rz_wide[:], ps[:, IB, 0:S], ACT.Copy)
                    ins.then_inc(s_free.sem, 1)

                eng.wait_ge(s_var, 1)
                eng.activation(rstd[:], rstd[:], ACT.Sqrt).then_inc(s_root, 1)
                for name, n in ahead[:4]:
                    take(0, name, n, True)
                probabilities(0, 0)

                def batch_steps(batch, first, last):
                    at, _ = items_of(first, last)
                    for m in range(STEPS):
                        u = m // 2
                        s_turn.wait(eng, batch, m)
                        if m + 1 < STEPS:
                            probabilities(batch, m + 1)
                        elif not last:
                            probabilities(batch + 1, 0)
                        if m % 4:
                            s_turn.wait(eng, batch, m + 1)
                            if not (first and u < 2):
                                s_pv.wait(eng, batch, u - 1)
                            eng.activation(probT[:, u % 2, 2 * (m % 2):2 * (m % 2) + 2, :, :]
                                           .rearrange("p h c q -> p (h c q)"), ps[:, PT + m % 2, :], ACT.Copy)\
                               .then_inc(s_cpa.sem, 1)
                        for name, n in at.get(m, []):
                            if name not in ("v", "out"):
                                take(owner(batch, name, n), name, n, first and name == "spread")

                every_batch(eng, batch_steps)

            @block.gpsimd
            def _(eng):
                def low(batch, name, n, first):
                    k = 0 if name == "q" else 1
                    s_hi.wait(eng, batch, 2 * n + 1 + k)
                    hi, lo = ((qh, ql), (kh, kl))[k]
                    half = slice(2 * n, 2 * n + 2)
                    eng.tensor_tensor(lo[:, half, :], raw[:, k, :, :], hi[:, half, :].bitcast(F32), ALU.subtract)\
                       .then_inc(s_lo.sem, 1)

                low(0, "q", 0, True)
                low(0, "k", 0, True)

                def batch_parts(batch, first, last):
                    low(batch, "q", 1, first)
                    low(batch, "k", 1, first)
                    if not last:
                        low(batch + 1, "q", 0, False)
                        low(batch + 1, "k", 0, False)

                every_batch(eng, batch_parts)


def roots_of_variances(eng, g, s_var, s_root, links):
    eng.tensor_scalar(g["rstd"][:], g["moments"][:, :, :, 1], EPS, None, ALU.add).then_inc(s_var, 1)
    eng.wait_ge(s_root, 1)
    links.add(eng.reciprocal(g["rstd"][:], g["rstd"][:]))


def mlp(nc, d, g):
    X, ident, moments, rstd, ps = g["X"], g["ident"], g["moments"], g["rstd"], g["ps"]
    w1 = g["w_self"]
    w2 = g["w_cross"][:].rearrange("p c (q n) -> p (c q) n", n=D)
    NI = FC // 2
    RING = 4
    XB, HB, YB = 0, 2, 4

    with ExitStack() as ctx:
        def sb(name, shape, dt=F32):
            return ctx.enter_context(nc.sbuf_tensor("mlp_" + name, shape, dt))

        def sem(name):
            return g["whole"].enter_context(nc.semaphore("mlp_" + name))

        xn = sb("xn", [P, SB, D])
        xT = sb("xT", [P, DC, S])
        h = sb("h", [P, RING, 2, S])
        part = sb("part", [P, SB, D])
        res = sb("res", [P, SB, D])

        s_var, s_root, s_link = sem("var"), sem("root"), sem("link")
        s_xn = Count(sem("xn"), SB)
        s_xt = Count(sem("xt"), 2)
        s_x = Count(sem("x"), 2)
        s_h = Count(sem("h"), NI)
        s_gelu = Count(sem("gelu"), NI)
        s_y = Count(sem("y"), NI)
        s_part = Count(sem("part"), SB)
        s_res = Count(sem("res"), SB)
        s_out = Count(sem("out"), SB * DMA)

        with nc.Block() as block:
            @block.tensor
            def _(eng):
                def turn(batch, n, first):
                    s_xn.wait(eng, batch, SB)
                    if not first:
                        s_x.wait(eng, batch - 1, n + 1)
                    for c in range(2):
                        for s in range(SB):
                            mm = eng.transpose(ps[:, XB + n, S * c + P * s:S * c + P * (s + 1)],
                                               xn[:, s, P * (2 * n + c):P * (2 * n + c + 1)], ident[:])
                    mm.then_inc(s_xt.sem, 1)

                def hidden(batch, n, first):
                    if not (first and n < 2):
                        s_gelu.wait(eng, batch, n - 1)
                    if n == 0:
                        s_x.wait(eng, batch, 2)
                    for i in range(2):
                        for c in range(DC):
                            mm = eng.matmul(ps[:, HB + n % 2, S * i:S * (i + 1)], w1[:, c, P * (2 * n + i):P * (2 * n + i + 1)],
                                            xT[:, c, :], start=(c == 0), stop=(c == DC - 1))
                    mm.then_inc(s_h.sem, 1)

                def output(batch, n, first):
                    s_gelu.wait(eng, batch, n + 1)
                    if n == 0 and not first:
                        s_part.wait(eng, batch - 1, SB)
                    for i in range(2):
                        for s in range(SB):
                            mm = eng.matmul(ps[:, YB + s, :], h[:, n % RING, i, P * s:P * (s + 1)], w2[:, 2 * n + i, :],
                                            start=(n == 0 and i == 0), stop=(n == NI - 1 and i == 1))
                    mm.then_inc(s_y.sem, 1)

                turn(0, 0, True)
                turn(0, 1, True)

                def batch_items(batch, first, last):
                    hidden(batch, 0, first)
                    for n in range(1, NI):
                        hidden(batch, n, first)
                        output(batch, n - 1, first)
                    if not last:
                        turn(batch + 1, 0, False)
                        turn(batch + 1, 1, False)
                    output(batch, NI - 1, first)

                every_batch(eng, batch_items)

            @block.scalar
            def _(eng):
                def take_x(batch, first):
                    if not first:
                        s_h.wait(eng, batch - 1, NI)
                    for n in range(2):
                        s_xt.wait(eng, batch, n + 1)
                        for c in range(2):
                            ins = eng.activation(xT[:, 2 * n + c, :], ps[:, XB + n, S * c:S * (c + 1)], ACT.Identity,
                                                 bias=g["gb"][:, 2, 1, 2 * n + c:2 * n + c + 1],
                                                 scale=g["gb"][:, 2, 0, 2 * n + c:2 * n + c + 1])
                        ins.then_inc(s_x.sem, 1)

                eng.wait_ge(s_var, 1)
                eng.activation(rstd[:], rstd[:], ACT.Sqrt).then_inc(s_root, 1)
                take_x(0, True)

                def batch_items(batch, first, last):
                    for n in range(NI):
                        s_h.wait(eng, batch, n + 1)
                        if not (first and n < RING):
                            s_y.wait(eng, batch, n - RING + 1)
                        for i in range(2):
                            ins = eng.activation(h[:, n % RING, i, :], ps[:, HB + n % 2, S * i:S * (i + 1)],
                                                 ACT.Gelu_apprx_tanh, bias=g["b1"][:, 2 * n + i:2 * n + i + 1])
                        ins.then_inc(s_gelu.sem, 1)
                    if not last:
                        take_x(batch + 1, False)

                every_batch(eng, batch_items)

            @block.vector
            def _(eng):
                def layer_norm(batch):
                    for s in range(SB):
                        eng.tensor_scalar(xn[:, s, :], X[:, batch, s, :], moments[:, batch, s, 0:1],
                                          rstd[:, batch, s:s + 1], ALU.subtract, ALU.mult).then_inc(s_xn.sem, 1)

                links = Links(eng, s_link)
                links.start(0)
                roots_of_variances(eng, g, s_var, s_root, links)
                layer_norm(0)

                def batch_items(batch, first, last):
                    if not last:
                        s_xt.wait(eng, batch, 2)
                        layer_norm(batch + 1)
                    if not first:
                        s_res.wait(eng, batch - 1, SB)
                    s_y.wait(eng, batch, NI)
                    for s in range(SB):
                        eng.tensor_tensor(part[:, s, :], ps[:, YB + s, :], g["b_row"][:, 4, :], ALU.add)\
                           .then_inc(s_part.sem, 1)
                    if not first:
                        s_out.wait(eng, batch - 1, SB * DMA)
                    for s in range(SB):
                        s_part.wait(eng, batch, s + 1)
                        eng.tensor_tensor(res[:, s, :], part[:, s, :], X[:, batch, s, :], ALU.add).then_inc(s_res.sem, 1)

                every_batch(eng, batch_items)

            @block.sync
            def _(eng):
                def batch_out(batch, first, last):
                    for s in range(SB):
                        s_res.wait(eng, batch, s + 1)
                        eng.dma_start(d["out"][batch].rearrange("(s p) n -> p s n", p=P)[:, s, :], res[:, s, :])\
                           .then_inc(s_out.sem, DMA)

                every_batch(eng, batch_out)
                s_out.wait(eng, NB - 1, SB * DMA)


def build(nc, d):
    with ExitStack() as ctx:
        def sb(name, shape, dt=F32):
            return ctx.enter_context(nc.sbuf_tensor(name, shape, dt))

        g = {
            "whole": ctx,
            "X": sb("X", [P, NB, SB, D]),
            "moments": sb("moments", [P, NB, SB, 2]),
            "rstd": sb("rstd", [P, NB, SB]),
            "ident": sb("ident", [P, P]),
            "sel": sb("sel", [HG, P]),
            "row": sb("row", [P, 4]),
            "gb": sb("gb", [P, 3, 2, DC]),
            "b_feat": sb("b_feat", [P, 4, DC]),
            "b_row": sb("b_row", [P, 5, D]),
            "b1": sb("b1", [P, FC]),
            "w_self": sb("w_self", [P, DC, 4 * D]),
            "ps": ctx.enter_context(nc.psum_tensor("ps", [P, 8, 512], F32)),
        }
        layer0(nc, d, g)
        g["w_cross"] = sb("w_cross", [P, DC, 4 * D])
        attention(nc, d, g, "self")
        attention(nc, d, g, "cross")
        mlp(nc, d, g)


def kernel(**inputs):
    import concourse.bacc as bacc
    from concourse.bass_utils import run_bass_kernel_spmd

    a = {name: np.asarray(x) for name, x in inputs.items()}
    L0 = {k: a["L0_xattn_" + k] for k in ("Wq", "bq", "Wk", "bk", "Wv", "bv")}
    L1 = {k[len("L1_xattn_"):]: x for k, x in a.items() if k.startswith("L1_xattn_")}

    def rows_to_partitions(w):
        return w.reshape(w.shape[0] // P, P, -1).transpose(1, 0, 2)

    def by_partition(b):
        return b.reshape(-1, P).T

    def along_columns(b):
        return np.broadcast_to(b, (P, b.shape[0]))

    def twice(w):
        w = w.reshape(w.shape[0], NH, 1, HD0)
        return np.concatenate([w, w], 2).reshape(w.shape[0], D)

    where = np.arange(P) % QD
    row = np.zeros((P, 4), np.float32)
    row[:, NEG_LO] = np.where(where >= HD0, -1.0, 0.0)
    row[:, IS_LOW] = np.where(where < HD0, 1.0, 0.0)
    row[:, ONE_AT] = np.where(where == HD0, 1.0, 0.0)
    row[:, FAR_AT] = np.where(where == HD0, FAR, 0.0)

    arrays = {
        "x": a["x"],
        "ctx": a["ctx_2048"],
        "ctxT": a["ctx_2048"].transpose(0, 2, 1),
        "mask0": a["mask_Bx1x2048_bf1"].view(np.uint8),
        "mask_self": a["mask_1x1xSxS2_fc1"],
        "mask_cross": a["mask_Bx1xSxS2_ff1"],
        "w0": rows_to_partitions(np.concatenate([twice(L0["Wq"].T), twice(L0["Wk"].T), L0["Wv"].T], 1)),
        "b0": np.stack([by_partition(twice(L0[k][None])[0]) for k in ("bq", "bk")], 1),
        "bv0": along_columns(L0["bv"]),
        "w_self": rows_to_partitions(np.concatenate([L1["w_qkv"], L1["w_ao"]], 1)),
        "w_cross": rows_to_partitions(np.concatenate([L1["w_q"], L1["w_kv"], L1["w_co"]], 1)),
        "w1": rows_to_partitions(L1["w1"]),
        "w2": rows_to_partitions(L1["w2"]),
        "gb": np.stack([np.stack([by_partition(L1[f"ln{n}_{k}"]) for k in "sb"], 1) for n in (1, 2, 3)], 1),
        "b_feat": np.stack([by_partition(b) for b in (L1["b_qkv"][0:D], L1["b_qkv"][D:2 * D], L1["b_q"], L1["b_kv"][0:D])], 1),
        "b_row": np.stack([along_columns(b) for b in (L1["b_qkv"][2 * D:], L1["b_ao"], L1["b_kv"][D:], L1["b_co"], L1["b2"])], 1),
        "b1": by_partition(L1["b1"]),
        "ident": np.eye(P, dtype=np.float32),
        "sel": np.kron(np.eye(HG), np.ones((1, QD))).astype(np.float32),
        "row": row,
    }
    arrays = {name: np.ascontiguousarray(x) for name, x in arrays.items()}
    nc = bacc.Bacc("TRN2", target_bir_lowering=False, num_devices=1)
    d = {name: nc.dram_tensor("in_" + name, x.shape, mybir.dt.from_np(x.dtype), kind="ExternalInput").ap()
         for name, x in arrays.items()}
    d["out"] = nc.dram_tensor("out", (NB, S, D), F32, kind="ExternalOutput").ap()
    build(nc, d)
    arrays = {"in_" + name: x for name, x in arrays.items()}
    return run_bass_kernel_spmd(nc, [arrays], core_ids=[0]).results[0]["out"]
```

```python
from contextlib import ExitStack

import numpy as np

import concourse.bass as bass
from concourse import mybir

F32 = mybir.dt.float32
F32R = mybir.dt.float32r
U8 = mybir.dt.uint8
ALU = mybir.AluOpType
ACT = mybir.ActivationFunctionType
AX = mybir.AxisListType.X

P = 128
NB = 8
S = 256
D = 512
NH = 16
SB = S // P
DC = D // P
HG = 4
NG = NH // HG
QD = P // HG
HD0 = S // NH
HD1 = D // NH
FF = 4 * D
FC = FF // P
EPS = 1e-5
FAR = 1.0e30
OFF = 10000.0
NEVER = 3.0e38
DMA = 16

NEG_LO, IS_LOW, ONE_AT, FAR_AT = range(4)


class Count:

    def __init__(self, sem, per, before=0):
        self.sem, self.per, self.before = sem, per, before

    def at(self, batch, k):
        return batch * self.per + (self.before + k)

    def wait(self, eng, batch, k):
        eng.wait_ge(self.sem, self.at(batch, k))


def every_batch(eng, body):
    body(0, True, False)
    with eng.Fori(1, NB - 1) as batch:
        body(batch, False, False)
    body(NB - 1, False, True)


class Links:

    def __init__(self, eng, sem):
        self.eng, self.sem, self.n, self.base = eng, sem, 0, 0

    def start(self, base):
        self.base, self.n = base, 0

    def add(self, ins):
        ins.then_inc(self.sem, 1)
        self.n += 1
        self.eng.wait_ge(self.sem, self.base + self.n)


def keep_rows(eng, links, g, batch, s, rows, six, two):
    links.add(eng.bn_stats(six[:], rows))
    eng.tensor_scalar(g["X"][:, batch, s, :], rows, 1.0, None, ALU.mult)
    links.add(eng.bn_aggr(two[:], six[:]))
    links.add(eng.tensor_scalar(g["moments"][:, batch, s, :], two[:], 1.0, None, ALU.mult))


def linked_batches(eng, sem, body, before, per):
    links = Links(eng, sem)

    def padded(batch, first, last):
        links.start(batch * per + before)
        body(batch, first, last, links)
        if links.n < per:
            eng.sem_inc(sem, per - links.n)
            eng.wait_ge(sem, links.base + per)
        assert links.n <= per, links.n

    every_batch(eng, padded)


def layer0_items(last):
    at = {0: [("q", 2)], 1: [("k", 2)], 2: [("q", 3)], 3: [("k", 3)], 4: [("v", 1)]}
    if not last:
        at.update({17: [("q", 0)], 18: [("k", 0)], 19: [("q", 1)], 20: [("k", 1)], 22: [("v", 0)]})
    for G in range(NG):
        at.setdefault(8 * G + 7, []).append(("turn", G))
        at.setdefault(min(8 * G + 8, 31), []).append(("spread", G))
    index = {name: n for n, name in enumerate(x for step in sorted(at) for x in at[step])}
    return at, index


def layer0(nc, d, g):
    STEPS, UNITS = 32, 16
    at_full, index_full = layer0_items(False)
    at_last, index_last = layer0_items(True)
    A_ITEMS = 5
    X, ident, sel, row, moments = g["X"], g["ident"], g["sel"], g["row"], g["moments"]
    ps = g["ps"]
    SC, PT, OB, IB = 0, 4, 6, 7

    with ExitStack() as ctx:
        def sb(name, shape, dt=F32):
            return ctx.enter_context(nc.sbuf_tensor(name, shape, dt))

        def sem(name):
            return g["whole"].enter_context(nc.semaphore("l0_" + name))

        w0 = sb("w0", [P, SB, 2 * D + S])
        b0 = sb("b0", [P, 2, NG])
        bv0 = sb("bv0", [P, S])
        x_in = sb("x_in", [P, SB, D])
        c_in = sb("c_in", [P, SB, D])
        m_in = sb("m_in", [P, D], U8)
        mask = sb("mask", [P, D])
        mask_done = sb("mask_done", [P, D])
        far = sb("far", [P, D])
        raw = sb("raw", [P, 2, D])
        q_hi = sb("q_hi", [P, D], F32R)
        q_low = sb("q_low", [P, D])
        k_rest = sb("k_rest", [P, D])
        q1 = sb("q1", [P, NG, D], F32R)
        q2 = sb("q2", [P, NG, D], F32R)
        k1 = sb("k1", [P, NG, D], F32R)
        k2 = sb("k2", [P, NG, D], F32R)
        v = sb("v", [P, DC, NH, 2 * HD0])
        nmax = sb("nmax", [P, 4, 2])
        prob = sb("prob", [P, 2, 2, D])
        probT = sb("probT", [P, 2, HG, DC, P])
        z = sb("z", [P, 2, DC, HG])
        rz = sb("rz", [P, DC * HG])
        rzT = sb("rzT", [HG, D])
        rz_wide = sb("rz_wide", [P, D])
        out_n = sb("out_n", [P, 2, D])
        mean_a = sb("mean_a", [P, SB, D])
        second = sb("second", [P, SB, D])
        std_a = sb("std_a", [P, SB, D])
        sums = sb("sums", [P, 4, SB])
        cnt = sb("cnt", [P, 2])
        x_mean = sb("x_mean", [P, SB])
        x_var = sb("x_var", [P, SB])
        x_rstd = sb("x_rstd", [P, SB])
        six = sb("six", [P, 6])
        two = sb("two", [P, 2])
        x_masked = sb("x_masked", [P, SB, D])
        scrap = sb("scrap", [P, D])

        s_set = sem("set")
        s_big = sem("big")
        s_v0 = sem("v0")
        s_load = Count(sem("load"), 3 * DMA)
        s_score = Count(sem("score"), STEPS)
        s_max = Count(sem("max"), STEPS)
        s_exp = Count(sem("exp"), STEPS)
        s_turn = Count(sem("turn"), 2 * STEPS)
        s_cpv = Count(sem("cpv"), STEPS)
        s_cpa = Count(sem("cpa"), STEPS)
        s_pv = Count(sem("pv"), UNITS)
        s_item = Count(sem("item"), len(index_full), A_ITEMS)
        s_free = Count(sem("free"), len(index_full), A_ITEMS)
        s_k1 = Count(sem("k1"), NG)
        s_kq = Count(sem("kq"), 2 * NG)
        s_low = Count(sem("low"), NG)
        s_gkq = Count(sem("gkq"), 2 * NG)
        s_gv = Count(sem("gv"), 2)
        s_rz = Count(sem("rz"), NG)
        s_norm = Count(sem("norm"), NG)
        s_re = [Count(sem(f"re{k}"), NG // 2 * 8 * DMA) for k in range(2)]
        s_stat = Count(sem("stat"), SB)
        s_fin_g = Count(sem("fin_g"), 2)
        s_fin_v = Count(sem("fin_v"), 2)
        s_fin_a = Count(sem("fin_a"), 1)
        s_link = sem("link")
        LINKS, LINKS0 = 60, 40

        def number_of(batch, name, n):
            if n >= 2 or (name, n) == ("v", 1):
                return batch, index_full[(name, n)] + 1
            if isinstance(batch, int) and batch == 0:
                return 0, [("q", 0), ("k", 0), ("q", 1), ("k", 1), ("v", 0)].index((name, n)) + 1 - A_ITEMS
            return batch - 1, index_full[(name, n)] + 1

        def item_at(batch, last, name, n):
            index = index_last if last else index_full
            return index[(name, n)] + 1

        wq, wk, wv = w0[:, :, 0:D], w0[:, :, D:2 * D], w0[:, :, 2 * D:2 * D + S]

        with nc.Block() as block:
            @block.sync
            def _(eng):
                for dst, src in ((w0, d["w0"]), (b0, d["b0"]), (bv0, d["bv0"]), (ident, d["ident"]),
                                 (sel, d["sel"]), (row, d["row"])):
                    eng.dma_start(dst[:], src).then_inc(s_set, DMA)

                def load(batch):
                    eng.dma_start(x_in[:], d["x"][batch].rearrange("(h p) t -> p h t", p=P)).then_inc(s_load.sem, DMA)
                    eng.dma_start(c_in[:], d["ctx"][batch].rearrange("(h p) t -> p h t", p=P)).then_inc(s_load.sem, DMA)
                    eng.dma_start(m_in[:], d["mask0"][batch].broadcast_to([P, D])).then_inc(s_load.sem, DMA)

                load(0)
                for dst, src in ((g["gb"], d["gb"]), (g["b_feat"], d["b_feat"]), (g["b_row"], d["b_row"]),
                                 (g["b1"], d["b1"]), (g["w_self"], d["w_self"])):
                    eng.dma_start(dst[:], src).then_inc(s_big, DMA)

                def batch_loads(batch, first, last):
                    if not last:
                        s_item.wait(eng, batch, item_at(batch, last, "v", 1))
                        s_stat.wait(eng, batch, SB)
                        load(batch + 1)
                    for G in range(NG):
                        s_norm.wait(eng, batch, G + 1)
                        if G == 0 and not first:
                            s_fin_g.wait(eng, batch - 1, 2)
                        for k in range(HG):
                            head = HG * (G % 2) + k
                            for j, dst in enumerate((mean_a, second)):
                                src = out_n[QD * k + HD0 * j:QD * k + HD0 * (j + 1), G % 2, :]
                                eng.dma_start(dst[HD0 * head:HD0 * (head + 1), G // 2, :], src).then_inc(s_re[G % 2].sem, DMA)

                every_batch(eng, batch_loads)
                eng.wait_ge(s_big, 5 * DMA)

            @block.tensor
            def _(eng):
                def scores(batch, m):
                    G, j, p = m // 8, m // 2 % 4, m % 2
                    if m % 8 == 0:
                        s_kq.wait(eng, batch, 2 * G + 2)
                        s_gkq.wait(eng, batch, 2 * G + 2)
                    for a, b in ((q1, k1), (q2, k2)):
                        for i in range(2):
                            r = slice(QD * (2 * p + i), QD * (2 * p + i + 1))
                            mm = eng.matmul(ps[:, SC + 2 * p + i, :], a[r, G, P * j:P * (j + 1)], b[r, G, :],
                                            start=(a is q1), stop=(a is q2))
                    mm.then_inc(s_score.sem, 1)

                def turn(batch, m):
                    for i in range(2):
                        (s_cpv, s_cpa)[i].wait(eng, batch, m)
                        for c in range(DC):
                            mm = eng.transpose(ps[:, PT + i, P * c:P * (c + 1)], prob[:, m % 2, i, P * c:P * (c + 1)],
                                               ident[:])
                        mm.then_inc(s_turn.sem, 1)

                def pv(batch, u, first):
                    G, j = u // 4, u % 4
                    s_cpv.wait(eng, batch, 2 * u + 2)
                    s_cpa.wait(eng, batch, 2 * u + 2)
                    if u % 8 == 0:
                        s_gv.wait(eng, batch, u // 8 + 1)
                    if j == 0 and not (first and u == 0):
                        s_norm.wait(eng, batch, G)
                    for c in range(DC):
                        for k in range(HG):
                            mm = eng.matmul(ps[QD * k:QD * (k + 1), OB, P * j:P * (j + 1)], v[:, c, HG * G + k, :],
                                            probT[:, u % 2, k, c, :], start=(c == 0), stop=(c == DC - 1))
                    mm.then_inc(s_pv.sem, 1)

                def item(batch, name, n, number):
                    if not (isinstance(batch, int) and batch == 0 and number == -A_ITEMS):
                        s_free.wait(eng, batch, number)
                    bank = ps[:, IB, :]
                    if name in "qk":
                        w, src = (wq, x_in) if name == "q" else (wk, c_in)
                        for c in range(SB):
                            mm = eng.matmul(bank, w[:, c, P * n:P * (n + 1)], src[:, c, :], start=(c == 0), stop=(c == SB - 1))
                    elif name == "v":
                        for t in range(DC):
                            for c in range(SB):
                                mm = eng.matmul(bank[:, P * t:P * (t + 1)], c_in[:, c, P * t:P * (t + 1)],
                                                wv[:, c, P * n:P * (n + 1)], start=(c == 0), stop=(c == SB - 1))
                    elif name == "turn":
                        s_rz.wait(eng, batch, n + 1)
                        for j in range(DC):
                            mm = eng.transpose(ps[0:HG, IB, P * j:P * (j + 1)], rz[:, HG * j:HG * (j + 1)], ident[:])
                    else:
                        mm = eng.matmul(bank, sel[:], rzT[:], start=True, stop=True)
                    mm.then_inc(s_item.sem, 1)

                eng.wait_ge(s_set, 6 * DMA)
                s_load.wait(eng, 0, 3 * DMA)
                for n, (name, tile) in enumerate((("q", 0), ("k", 0), ("q", 1), ("k", 1), ("v", 0))):
                    item(0, name, tile, n - A_ITEMS)
                scores(0, 0)
                scores(0, 1)

                def batch_steps(batch, first, last):
                    at, index = (at_last, index_last) if last else (at_full, index_full)
                    for m in range(STEPS):
                        s_exp.wait(eng, batch, m + 1)
                        if m + 2 < STEPS:
                            scores(batch, m + 2)
                        elif not last:
                            scores(batch + 1, m + 2 - STEPS)
                        turn(batch, m)
                        if m % 2 == 0 and m:
                            pv(batch, m // 2 - 1, first)
                        for name, n in at.get(m, []):
                            if m == STEPS - 1 and name == "spread":
                                pv(batch, UNITS - 1, first)
                            if m == 17 and name == "q":
                                s_load.wait(eng, batch + 1, 3 * DMA)
                            item(batch, name, n, index[(name, n)])

                every_batch(eng, batch_steps)

            @block.vector
            def _(eng):
                def maxima(batch, m):
                    s_score.wait(eng, batch, m + 1)
                    eng.tensor_reduce(nmax[:, m % 4, :], ps[:, SC + 2 * (m % 2):SC + 2 * (m % 2) + 2, :], AX, ALU.max,
                                      negate=True).then_inc(s_max.sem, 1)

                def masks(links):
                    links.add(eng.tensor_copy(mask[:], m_in[:]))
                    links.add(eng.tensor_scalar(far[:], mask[:], 1.0, row[:, FAR_AT:FAR_AT + 1], ALU.subtract, ALU.mult))

                def statistics(batch, links):
                    eng.tensor_reduce(cnt[:, 0:1], mask[:], AX, ALU.add)
                    for h in range(SB):
                        eng.tensor_tensor_reduce(x_masked[:, h, :], x_in[:, h, :], mask[:], 1.0, 0.0, ALU.mult, ALU.add,
                                                 sums[:, 0, h:h + 1]).then_inc(s_stat.sem, 1)
                    s_stat.wait(eng, batch, SB)
                    for h in range(SB):
                        links.add(eng.tensor_tensor_reduce(scrap[:], x_masked[:, h, :], x_masked[:, h, :], 1.0, 0.0,
                                                           ALU.mult, ALU.add, sums[:, 1, h:h + 1]))
                    links.add(eng.tensor_scalar(X[:, batch, :, :], x_masked[:], 1.0, None, ALU.mult))

                def moments_of_x(links):
                    links.add(eng.reciprocal(cnt[:, 1:2], cnt[:, 0:1]))
                    links.add(eng.tensor_scalar(x_mean[:], sums[:, 0, :], cnt[:, 1:2], None, ALU.mult))
                    links.add(eng.tensor_scalar(x_var[:], sums[:, 1, :], cnt[:, 1:2], None, ALU.mult))
                    links.add(eng.tensor_tensor(sums[:, 2, :], x_mean[:], x_mean[:], ALU.mult))
                    links.add(eng.tensor_tensor(x_var[:], x_var[:], sums[:, 2, :], ALU.subtract))
                    links.add(eng.tensor_scalar(x_var[:], x_var[:], 0.0, EPS, ALU.max, ALU.add))

                def tile(batch, name, n, first, links):
                    if name == "q":
                        s_free.wait(eng, *number_of(batch, name, n))
                        if not first:
                            s_score.wait(eng, batch - 1, 8 * n + 8)
                        links.add(eng.tensor_copy(q_hi[:], raw[:, 0, :]))
                        eng.scalar_tensor_tensor(out=q1[:, n, :], in0=q_hi[:].bitcast(F32), scalar=row[:, NEG_LO:NEG_LO + 1],
                                                 in1=raw[:, 0, :], op0=ALU.mult, op1=ALU.add).then_inc(s_kq.sem, 1)
                    else:
                        s_free.wait(eng, *number_of(batch, name, n))
                        if not first:
                            s_score.wait(eng, batch - 1, 8 * n + 8)
                        eng.tensor_copy(k1[:, n, :], raw[:, 1, :]).then_inc(s_k1.sem, 1)
                        s_gkq.wait(eng, batch, 2 * n + 2)
                        eng.scalar_tensor_tensor(out=k2[:, n, :], in0=k_rest[:], scalar=row[:, IS_LOW:IS_LOW + 1],
                                                 in1=far[:], op0=ALU.mult, op1=ALU.add).then_inc(s_kq.sem, 1)

                def values(batch, hf, first):
                    s_item.wait(eng, *number_of(batch, "v", hf))
                    if not first:
                        s_pv.wait(eng, batch - 1, 8 * hf + 8)
                        s_gv.wait(eng, batch - 1, hf + 1)
                    half = slice(NH // 2 * hf, NH // 2 * (hf + 1))
                    eng.tensor_tensor(v[:, :, half, 0:HD0],
                                      ps[:, IB, :].rearrange("p (c h e) -> p c h e", c=DC, e=HD0),
                                      bv0[:, P * hf:P * (hf + 1)].rearrange("p (h e) -> p h e", e=HD0)[:, None, :, :]
                                      .broadcast_to([P, DC, NH // 2, HD0]), ALU.add).then_inc(s_free.sem, 1)

                links = Links(eng, s_link)
                links.start(0)
                eng.wait_ge(s_set, 6 * DMA)
                links.add(eng.tensor_scalar(b0[:, 0, :], b0[:, 0, :], float(HD0) ** -0.5, None, ALU.mult))
                eng.memset(cnt[:], 0.0).then_inc(s_v0, 1)
                s_load.wait(eng, 0, 3 * DMA)
                masks(links)
                statistics(0, links)
                for name, n in (("q", 0), ("k", 0), ("q", 1), ("k", 1)):
                    tile(0, name, n, True, links)
                values(0, 0, True)
                maxima(0, 0)
                maxima(0, 1)
                if links.n < LINKS0:
                    eng.sem_inc(s_link, LINKS0 - links.n)

                def batch_steps(batch, first, last, links):
                    for m in range(STEPS):
                        u = m // 2
                        if m + 2 < STEPS:
                            maxima(batch, m + 2)
                        elif not last:
                            maxima(batch + 1, m + 2 - STEPS)
                        s_turn.wait(eng, batch, 2 * m + 1)
                        if m % 2 == 0 and not (first and u < 2):
                            s_pv.wait(eng, batch, u - 1)
                        eng.tensor_copy(probT[:, u % 2, 2 * (m % 2), :, :].rearrange("p c q -> p (c q)"),
                                        ps[:, PT, :]).then_inc(s_cpv.sem, 1)
                        if m % 8 == 7:
                            G = m // 8
                            s_exp.wait(eng, batch, m + 1)
                            if G:
                                s_item.wait(eng, batch, item_at(batch, last, "turn", G - 1))
                            elif not first:
                                s_item.wait(eng, batch - 1, index_full[("turn", NG - 1)] + 1)
                            eng.reciprocal(rz[:], z[:, G % 2, :, :].rearrange("p j h -> p (j h)")).then_inc(s_rz.sem, 1)
                        if (m % 8 == 1 and m > 1) or m == STEPS - 1:
                            G = (m - 1) // 8 if m == STEPS - 1 else m // 8 - 1
                            s_free.wait(eng, batch, item_at(batch, last, "spread", G))
                            s_pv.wait(eng, batch, 4 * G + 4)
                            if G >= 2:
                                s_re[G % 2].wait(eng, batch, 8 * DMA)
                            elif not first:
                                s_re[G % 2].wait(eng, batch - 1, 2 * 8 * DMA)
                            eng.tensor_tensor(out_n[:, G % 2, :], ps[:, OB, :], rz_wide[:], ALU.mult).then_inc(s_norm.sem, 1)
                        if m in (1, 2, 3, 4):
                            tile(batch, "qk"[(m + 1) % 2], 2 + (m - 1) // 2, first, links)
                        if m == 5:
                            values(batch, 1, first)
                        if not first and m == 8:
                            finish_variance(batch - 1)
                        if not first and m == 10:
                            finish_norm(batch - 1, links)
                        if not first and m == 14:
                            finish_mask(batch - 1, links)
                        if m == 16:
                            links.add(eng.tensor_copy(mask_done[:], mask[:]))
                            moments_of_x(links)
                        if m == 17 and not last:
                            s_load.wait(eng, batch + 1, 3 * DMA)
                            masks(links)
                        if m == 24 and not last:
                            statistics(batch + 1, links)
                        if m in (18, 19, 20, 21) and not last:
                            tile(batch + 1, "qk"[m % 2], (m - 18) // 2, False, links)
                        if m == 23 and not last:
                            values(batch + 1, 0, False)

                def finish_variance(batch):
                    s_fin_g.wait(eng, batch, 1)
                    eng.tensor_scalar(std_a[:], std_a[:], 0.0, None, ALU.max).then_inc(s_fin_v.sem, 1)

                def finish_norm(batch, links):
                    s_fin_a.wait(eng, batch, 1)
                    links.add(eng.reciprocal(x_rstd[:], x_rstd[:]))
                    for h in range(SB):
                        ins = eng.tensor_scalar(X[:, batch, h, :], X[:, batch, h, :], x_mean[:, h:h + 1],
                                                x_rstd[:, h:h + 1], ALU.subtract, ALU.mult)
                    ins.then_inc(s_fin_v.sem, 1)

                def finish_mask(batch, links):
                    s_fin_g.wait(eng, batch, 2)
                    for h in range(SB):
                        links.add(eng.tensor_tensor(scrap[:], X[:, batch, h, :], mask_done[:], ALU.mult))
                        keep_rows(eng, links, g, batch, h, scrap[:], six, two)

                linked_batches(eng, s_link, batch_steps, LINKS0, LINKS)
                links.start(NB * LINKS + LINKS0)
                finish_variance(NB - 1)
                finish_norm(NB - 1, links)
                finish_mask(NB - 1, links)

            @block.scalar
            def _(eng):
                def probabilities(batch, m):
                    G, j, p = m // 8, m // 2 % 4, m % 2
                    s_max.wait(eng, batch, m + 1)
                    for i in range(2):
                        ins = eng.activation(prob[:, m % 2, i, :], ps[:, SC + 2 * p + i, :], ACT.Exp,
                                             bias=nmax[:, m % 4, i:i + 1],
                                             accum_out=z[:, G % 2, j, 2 * p + i:2 * p + i + 1])
                    ins.then_inc(s_exp.sem, 1)

                def take(batch, name, n, first, number):
                    s_item.wait(eng, batch, number + 1)
                    own = batch + 1 if n < 2 and name in "qkv" else batch
                    if name in "qk":
                        k = 0 if name == "q" else 1
                        if not (first and n == 0):
                            s_kq.wait(eng, own, 2 * n + k - 1)
                            s_gkq.wait(eng, own, 2 * n + k - 1)
                        eng.activation(raw[:, k, :], ps[:, IB, :], ACT.Identity, bias=b0[:, k, n:n + 1],
                                       scale=(float(HD0) ** -0.5 if k == 0 else 1.0)).then_inc(s_free.sem, 1)
                    elif name == "turn":
                        eng.activation(rzT[:], ps[0:HG, IB, :], ACT.Copy).then_inc(s_free.sem, 1)
                    elif name == "spread":
                        if not (first and n == 0):
                            s_norm.wait(eng, batch, n)
                        eng.activation(rz_wide[:], ps[:, IB, :], ACT.Copy).then_inc(s_free.sem, 1)

                eng.wait_ge(s_v0, 1)
                for n, (name, tile) in enumerate((("q", 0), ("k", 0), ("q", 1), ("k", 1))):
                    s_item.wait(eng, 0, n + 1 - A_ITEMS)
                    k = n % 2
                    if tile:
                        s_kq.wait(eng, 0, 1 + k)
                        s_gkq.wait(eng, 0, 1 + k)
                    eng.activation(raw[:, k, :], ps[:, IB, :], ACT.Identity, bias=b0[:, k, tile:tile + 1],
                                   scale=(float(HD0) ** -0.5 if k == 0 else 1.0)).then_inc(s_free.sem, 1)
                probabilities(0, 0)

                def finish_roots(batch):
                    s_fin_v.wait(eng, batch, 1)
                    eng.activation(std_a[:], std_a[:], ACT.Sqrt)
                    eng.activation(x_rstd[:], x_var[:], ACT.Sqrt).then_inc(s_fin_a.sem, 1)

                def batch_steps(batch, first, last):
                    at, index = (at_last, index_last) if last else (at_full, index_full)
                    for m in range(STEPS):
                        u = m // 2
                        s_turn.wait(eng, batch, 2 * m)
                        if m + 1 < STEPS:
                            probabilities(batch, m + 1)
                        elif not last:
                            probabilities(batch + 1, 0)
                        s_turn.wait(eng, batch, 2 * m + 2)
                        if m % 2 == 0 and not (first and u < 2):
                            s_pv.wait(eng, batch, u - 1)
                        eng.activation(probT[:, u % 2, 2 * (m % 2) + 1, :, :].rearrange("p c q -> p (c q)"),
                                       ps[:, PT + 1, :], ACT.Copy).then_inc(s_cpa.sem, 1)
                        for name, n in at.get(m, []):
                            if name != "v":
                                take(batch, name, n, first and m < 8, index[(name, n)])
                        if not first and m == 9:
                            finish_roots(batch - 1)

                every_batch(eng, batch_steps)
                finish_roots(NB - 1)

            @block.gpsimd
            def _(eng):
                def parts(batch, name, n, first):
                    if name == "q":
                        if not first:
                            s_score.wait(eng, batch - 1, 8 * n + 8)
                        s_free.wait(eng, *number_of(batch, name, n))
                        low, one = (row[:, k:k + 1].broadcast_to([P, D]) for k in (IS_LOW, ONE_AT))
                        eng.tensor_tensor(q_low[:], raw[:, 0, :], low, ALU.mult).then_inc(s_low.sem, 1)
                        s_low.wait(eng, batch, n + 1)
                        eng.tensor_tensor(q2[:, n, :], q_low[:], one, ALU.add).then_inc(s_gkq.sem, 1)
                    else:
                        s_k1.wait(eng, batch, n + 1)
                        if not (first and n == 0):
                            s_kq.wait(eng, batch, 2 * n)
                        eng.tensor_tensor(k_rest[:], raw[:, 1, :], k1[:, n, :].bitcast(F32), ALU.subtract)\
                           .then_inc(s_gkq.sem, 1)

                def squares(batch, hf):
                    s_free.wait(eng, *number_of(batch, "v", hf))
                    half = slice(NH // 2 * hf, NH // 2 * (hf + 1))
                    vv = v[:, :, half, 0:HD0]
                    eng.tensor_tensor(v[:, :, half, HD0:2 * HD0], vv, vv, ALU.mult).then_inc(s_gv.sem, 1)

                def finish_a(batch):
                    for by_parity in s_re:
                        by_parity.wait(eng, batch, NG // 2 * 8 * DMA)
                    eng.tensor_tensor(std_a[:], mean_a[:], mean_a[:], ALU.mult).then_inc(s_g, 1)
                    eng.wait_ge(s_g, 2 * batch + 1)
                    eng.tensor_tensor(std_a[:], second[:], std_a[:], ALU.subtract).then_inc(s_fin_g.sem, 1)

                def finish_b(batch):
                    eng.wait_ge(s_set, 6 * DMA)
                    s_fin_v.wait(eng, batch, 2)
                    s_fin_a.wait(eng, batch, 1)
                    eng.tensor_tensor(X[:, batch, :, :], X[:, batch, :, :], std_a[:], ALU.mult).then_inc(s_g, 1)
                    eng.wait_ge(s_set, 6 * DMA)
                    eng.wait_ge(s_g, 2 * batch + 2)
                    eng.tensor_tensor(X[:, batch, :, :], X[:, batch, :, :], mean_a[:], ALU.add).then_inc(s_fin_g.sem, 1)

                s_g = sem("g")
                eng.wait_ge(s_set, 6 * DMA)
                for name, n in (("q", 0), ("k", 0), ("q", 1), ("k", 1)):
                    parts(0, name, n, True)
                squares(0, 0)

                def batch_parts(batch, first, last):
                    for name, n in (("q", 2), ("k", 2), ("q", 3), ("k", 3)):
                        parts(batch, name, n, first)
                    squares(batch, 1)
                    if not first:
                        finish_a(batch - 1)
                        finish_b(batch - 1)
                    if not last:
                        for name, n in (("q", 0), ("k", 0), ("q", 1), ("k", 1)):
                            parts(batch + 1, name, n, False)
                        squares(batch + 1, 0)

                every_batch(eng, batch_parts)
                finish_a(NB - 1)
                finish_b(NB - 1)


def layer1_items(last):
    at = {1: ("v", 1), 3: ("out", 0), 5: ("out", 1)}
    if not last:
        at.update({7: ("q", 0), 9: ("k", 0), 11: ("q", 1), 13: ("k", 1), 15: ("v", 0)})
    return at


def attention(nc, d, g, which):
    cross = which == "cross"
    layer = 1 if cross else 0
    STEPS, UNITS = 16, 8
    BEFORE = 5
    X, ident, sel, moments, rstd, ps = g["X"], g["ident"], g["sel"], g["moments"], g["rstd"], g["ps"]
    w = g["w_cross"] if cross else g["w_self"]
    wq, wk, wv, wo = (w[:, :, D * k:D * (k + 1)] for k in range(4))
    b_v, b_o = g["b_row"][:, 2 * layer, :], g["b_row"][:, 2 * layer + 1, :]
    SC, PT, OB, IB, TB = 0, 2, 4, 6, 7
    NM = NB if cross else 1
    SCALE = float(HD1) ** -0.5

    def items_of(first, last):
        at = {m: x for m, x in layer1_items(last).items() if not (first and x[0] == "out")}
        return at, {at[m]: n for n, m in enumerate(sorted(at))}

    full, full_index = items_of(False, False)
    FIRST_SHORT = 2
    ahead = [("q", 0), ("k", 0), ("q", 1), ("k", 1), ("v", 0)]

    with ExitStack() as ctx:
        def sb(name, shape, dt=F32):
            return ctx.enter_context(nc.sbuf_tensor(f"{which}_{name}", shape, dt))

        def sem(name):
            return g["whole"].enter_context(nc.semaphore(f"{which}_{name}"))

        mask = sb("mask", [P, NM, SB, S])
        off = sb("off", [P, SB, S])
        ctxT = sb("ctxT", [P, DC, S]) if cross else None
        xn = sb("xn", [P, SB, D])
        xT = sb("xT", [P, DC, S])
        low = sb("low", [P, 2, 2, S], F32R)
        high = sb("high", [P, 2, 2, S], F32R)
        q_stack = sb("q_stack", [3 * QD, HG, NG, S], F32R)
        k_stack = sb("k_stack", [3 * QD, HG, NG, S], F32R)
        v = sb("v", [P, SB, D])
        t = sb("t", [P, 2, 2, S])
        nmax = sb("nmax", [P, 4, 2])
        prob = sb("prob", [P, 2, 2, S])
        probT = sb("probT", [P, 2, HG, SB, P])
        z = sb("z", [P, 2, SB, HG])
        rz = sb("rz", [P, SB * HG])
        rzT = sb("rzT", [HG, S])
        rz_wide = sb("rz_wide", [P, S])
        heads = sb("heads", [P, NG, S])
        part = sb("part", [P, D])
        six = sb("six", [P, 6])
        two = sb("two", [P, 2])

        s_in = sem("in")
        s_w = sem("w")
        s_w2 = sem("w2")
        s_ctx = Count(sem("ctx"), DMA)
        s_t = Count(sem("t"), STEPS)
        s_var = sem("var")
        s_root = sem("root")
        s_xn = Count(sem("xn"), SB)
        s_score = Count(sem("score"), STEPS)
        s_max = Count(sem("max"), STEPS)
        s_exp = Count(sem("exp"), STEPS)
        s_turn = Count(sem("turn"), STEPS)
        s_cpv = Count(sem("cpv"), STEPS // 4)
        s_cpa = Count(sem("cpa"), STEPS - STEPS // 4)
        s_pv = Count(sem("pv"), UNITS)
        s_item = Count(sem("item"), len(full_index), BEFORE - FIRST_SHORT)
        s_free = Count(sem("free"), len(full_index), BEFORE - FIRST_SHORT)
        s_hi = Count(sem("hi"), 4)
        s_lo = Count(sem("lo"), 4)
        s_stack = {(name, n): Count(sem(f"stack_{name}{n}"), 2 * HG * DMA) for name in "qk" for n in range(2)}
        s_third = {(name, n): Count(sem(f"third_{name}{n}"), HG * DMA) for name in "qk" for n in range(2)}
        s_turned = Count(sem("turned"), 2)
        s_x = Count(sem("x"), 2)
        s_rz = Count(sem("rz"), NG)
        s_sums = Count(sem("sums"), 2 * NG)
        s_taken = Count(sem("taken"), 2 * NG)
        s_norm = Count(sem("norm"), NG)
        s_link = sem("link")
        LINKS, LINKS0 = 40, 10

        def index_of(first, last):
            index = items_of(first, last)[1]
            return {x: n + (FIRST_SHORT if first else 0) for x, n in index.items()}

        def number_of(batch, name, n):
            if name == "out":
                if isinstance(batch, int) and batch == NB - 1:
                    return NB - 1, len(index_of(False, True)) + n + 1
                if isinstance(batch, int) and batch == NB - 2:
                    return NB - 1, index_of(False, True)[(name, n)] + 1
                return batch + 1, full_index[(name, n)] + 1
            if (name, n) == ("v", 1):
                if isinstance(batch, int):
                    return batch, index_of(batch == 0, batch == NB - 1)[(name, n)] + 1
                return batch, full_index[(name, n)] + 1
            if isinstance(batch, int) and batch == 0:
                return 0, ahead.index((name, n)) + 1 - (BEFORE - FIRST_SHORT)
            if isinstance(batch, int) and batch == 1:
                return 0, index_of(True, False)[(name, n)] + 1
            return batch - 1, full_index[(name, n)] + 1

        def owner(batch, name, n):
            if name == "out":
                return batch - 1
            return batch if (name, n) == ("v", 1) else batch + 1

        def copied(eng, batch, m):
            s_cpv.wait(eng, batch, m // 4 + 1)
            s_cpa.wait(eng, batch, m - m // 4)

        def stack(eng, batch, name, n, parts):
            k = 0 if name == "q" else 1
            s_lo.wait(eng, batch, 2 * n + 1 + k)
            dst, done = (q_stack, k_stack)[k], (s_third if parts == (2,) else s_stack)[name, n]
            for a in parts:
                src = ((high, low, high) if name == "q" else (high, high, low))[a]
                for h in range(HG):
                    eng.dma_start(dst[QD * a:QD * (a + 1), h, 2 * n:2 * n + 2, :].bitcast(F32),
                                  src[QD * h:QD * (h + 1), k, :, :].bitcast(F32)).then_inc(done.sem, DMA)

        def stacked(eng, batch, name, n):
            s_stack[name, n].wait(eng, batch, 2 * HG * DMA)
            s_third[name, n].wait(eng, batch, HG * DMA)

        with nc.Block() as block:
            @block.sync
            def _(eng):
                if cross:
                    eng.dma_start(ctxT[:], d["ctxT"][0].rearrange("(c p) s -> p c s", p=P)).then_inc(s_ctx.sem, DMA)
                for n in range(NM):
                    src = (d["mask_cross"][n] if cross else d["mask_self"][n]).rearrange("a (j p) k -> p (a j) k", p=P)
                    eng.dma_start(mask[:, n, :, :], src).then_inc(s_in, DMA)
                if not cross:
                    eng.dma_start(g["w_cross"][:], d["w_cross"]).then_inc(s_w, DMA)
                else:
                    eng.dma_start(g["w_self"][:], d["w1"]).then_inc(s_w, DMA)

                for n in range(2):
                    stack(eng, 0, "q", n, (0, 1))
                    stack(eng, 0, "k", n, (0, 1))

                def batch_loads(batch, first, last):
                    if not last:
                        if cross:
                            s_item.wait(eng, *number_of(batch, "v", 1))
                            eng.dma_start(ctxT[:], d["ctxT"][batch + 1].rearrange("(c p) s -> p c s", p=P))\
                               .then_inc(s_ctx.sem, DMA)
                        for n in range(2):
                            stack(eng, batch + 1, "q", n, (0, 1))
                            stack(eng, batch + 1, "k", n, (0, 1))

                every_batch(eng, batch_loads)
                if cross:
                    w2 = g["w_cross"][:].rearrange("p c (q n) -> p (c q) n", n=D)
                    s_item.wait(eng, *number_of(NB - 1, "v", 1))
                    for c in range(DC):
                        eng.dma_start(w2[:, 4 * c:4 * c + 3, :], d["w2"][:, 4 * c:4 * c + 3, :]).then_inc(s_w2, DMA)
                    s_item.wait(eng, *number_of(NB - 1, "out", 1))
                    for c in range(DC):
                        eng.dma_start(w2[:, 4 * c + 3, :], d["w2"][:, 4 * c + 3, :]).then_inc(s_w2, DMA)
                    eng.wait_ge(s_w2, 8 * DMA)
                eng.wait_ge(s_w, DMA)

            @block.tensor
            def _(eng):
                def scores(batch, m):
                    T, j, p = m // 4, m // 2 % 2, m % 2
                    if m % 8 == 0:
                        for name in "qk":
                            stacked(eng, batch, name, m // 8)
                    for i in range(2):
                        mm = eng.matmul(ps[:, SC + p, S * i:S * (i + 1)], q_stack[:, 2 * p + i, T, P * j:P * (j + 1)],
                                        k_stack[:, 2 * p + i, T, :], start=True, stop=True)
                    mm.then_inc(s_score.sem, 1)

                def turn(batch, m):
                    if m >= 2:
                        copied(eng, batch, m - 2)
                    else:
                        copied(eng, batch, -1)
                    for i in range(2):
                        for c in range(SB):
                            k = SB * i + c
                            mm = eng.transpose(ps[:, PT + m % 2, P * k:P * (k + 1)], prob[:, m % 2, i, P * c:P * (c + 1)],
                                               ident[:])
                    mm.then_inc(s_turn.sem, 1)

                def pv(batch, u, first):
                    T, j = u // 2, u % 2
                    copied(eng, batch, 2 * u + 1)
                    if u % 4 == 0:
                        s_free.wait(eng, *number_of(batch, "v", u // 4))
                    if j == 0 and not (first and T < 2):
                        s_norm.wait(eng, batch, T - 1)
                    for c in range(SB):
                        for k in range(HG):
                            mm = eng.matmul(ps[QD * k:QD * (k + 1), OB + T % 2, P * j:P * (j + 1)],
                                            v[:, c, QD * (HG * T + k):QD * (HG * T + k + 1)], probT[:, u % 2, k, c, :],
                                            start=(c == 0), stop=(c == SB - 1))
                    mm.then_inc(s_pv.sem, 1)

                def item(name, n, own, parts=(0, 1)):
                    if 0 in parts and not (isinstance(own, int) and own == 0 and (name, n) == ahead[0]):
                        where, number = number_of(own, name, n)
                        s_free.wait(eng, where, number - 1)
                    bank = ps[:, IB, :]
                    if name in "qk":
                        if (name, n) == ("q", 0) and 0 in parts:
                            s_x.wait(eng, own, 2)
                        wt, src = (wq, xT) if name == "q" else (wk, ctxT if cross else xT)
                        if cross and name == "k" and n == 0 and 0 in parts:
                            s_ctx.wait(eng, own, DMA)
                        for T in parts:
                            for c in range(DC):
                                mm = eng.matmul(bank[:, S * T:S * (T + 1)], wt[:, c, P * (2 * n + T):P * (2 * n + T + 1)],
                                                src[:, c, :], start=(c == 0), stop=(c == DC - 1))
                    elif name == "v":
                        src = ctxT if cross else xT
                        for s in parts:
                            for c in range(DC):
                                mm = eng.matmul(bank[:, S * s:S * (s + 1)], src[:, c, P * s:P * (s + 1)],
                                                wv[:, c, S * n:S * (n + 1)], start=(c == 0), stop=(c == DC - 1))
                    else:
                        if n == 0 and 0 in parts:
                            s_norm.wait(eng, own, NG)
                        for T in range(NG // 2 * parts[0], NG // 2 * (parts[-1] + 1)):
                            mm = eng.matmul(bank, heads[:, T, P * n:P * (n + 1)], wo[:, T, :], start=(T == 0), stop=(T == NG - 1))
                    if 1 in parts:
                        mm.then_inc(s_item.sem, 1)

                def turn_x(own, n):
                    s_xn.wait(eng, own, SB)
                    if n:
                        s_x.wait(eng, own, 1)
                    for c in range(2):
                        for s in range(SB):
                            mm = eng.transpose(ps[:, TB, S * c + P * s:S * c + P * (s + 1)],
                                               xn[:, s, P * (2 * n + c):P * (2 * n + c + 1)], ident[:])
                    mm.then_inc(s_turned.sem, 1)

                def turn_sums(batch, T, last):
                    if T == 0:
                        s_x.wait(eng, batch if last else batch + 1, 2)
                    s_rz.wait(eng, batch, T + 1)
                    s_taken.wait(eng, batch, 2 * T)
                    for j in range(SB):
                        mm = eng.transpose(ps[0:HG, TB, P * j:P * (j + 1)], rz[:, HG * j:HG * (j + 1)], ident[:])
                    mm.then_inc(s_sums.sem, 1)

                def spread_sums(batch, T):
                    s_taken.wait(eng, batch, 2 * T + 1)
                    eng.matmul(ps[:, TB, 0:S], sel[:], rzT[:], start=True, stop=True).then_inc(s_sums.sem, 1)

                turn_x(0, 0)
                turn_x(0, 1)
                for name, n in ahead:
                    item(name, n, 0)
                scores(0, 0)
                scores(0, 1)

                def batch_steps(batch, first, last):
                    at, _ = items_of(first, last)
                    for m in range(STEPS):
                        s_exp.wait(eng, batch, m + 1)
                        if m + 2 < STEPS:
                            scores(batch, m + 2)
                        elif not last:
                            scores(batch + 1, m + 2 - STEPS)
                        turn(batch, m)
                        if m % 2 == 0 and m:
                            pv(batch, m // 2 - 1, first)
                        if m in (2, 3) and not last:
                            if m == 2:
                                s_taken.wait(eng, batch, 0)
                            turn_x(batch + 1, m - 2)
                        for part, step in enumerate((m + 1, m)):
                            if step % 2 and step in at:
                                name, n = at[step]
                                item(name, n, owner(batch, name, n), (part,))
                        if m % 4 == 1 and m > 1:
                            spread_sums(batch, m // 4 - 1)
                        if m % 4 == 0 and m or m == STEPS - 1:
                            turn_sums(batch, (m - 1) // 4, last)
                    pv(batch, UNITS - 1, first)
                    spread_sums(batch, NG - 1)

                every_batch(eng, batch_steps)
                item("out", 0, NB - 1)
                item("out", 1, NB - 1)

            @block.vector
            def _(eng):
                def mask_off(batch, links):
                    n = batch if cross else 0
                    links.add(eng.tensor_scalar(off[:], mask[:, n, :, :], -1.0, 1.0, ALU.mult, ALU.add))
                    links.add(eng.tensor_scalar(off[:], off[:], OFF, None, ALU.mult))

                def maxima(batch, m):
                    i, j = m % 2, m // 2 % 2
                    s_score.wait(eng, batch, m + 1)
                    n = batch if cross else 0
                    eng.scalar_tensor_tensor(out=t[:, i, :, :], in0=ps[:, SC + i, :].rearrange("p (h k) -> p h k", h=2), scalar=-SCALE,
                                             in1=mask[:, n, j, :][:, None, :].broadcast_to([P, 2, S]),
                                             op0=ALU.mult, op1=ALU.mult).then_inc(s_t.sem, 1)
                    eng.wait_ge(s_in, NM * DMA)
                    s_t.wait(eng, batch, m + 1)
                    for k in range(2):
                        ins = eng.tensor_tensor_reduce(t[:, i, k, :], t[:, i, k, :], off[:, j, :], 1.0, NEVER,
                                                       ALU.add, ALU.min, nmax[:, m % 4, k:k + 1])
                    ins.then_inc(s_max.sem, 1)

                def layer_norm(batch):
                    for s in range(SB):
                        eng.tensor_scalar(xn[:, s, :], X[:, batch, s, :], moments[:, batch, s, 0:1],
                                          rstd[:, batch, s:s + 1], ALU.subtract, ALU.mult).then_inc(s_xn.sem, 1)

                def high_parts(batch, name, n):
                    k = 0 if name == "q" else 1
                    s_free.wait(eng, *number_of(batch, name, n))
                    eng.tensor_copy(high[:, k, :, :], low[:, k, :, :].bitcast(F32)).then_inc(s_hi.sem, 1)

                def values(batch, n, first):
                    s_item.wait(eng, *number_of(batch, "v", n))
                    if not first:
                        s_pv.wait(eng, batch - 1, 4 * n + 4)
                    eng.tensor_tensor(v[:, :, S * n:S * (n + 1)], ps[:, IB, :].rearrange("p (s e) -> p s e", s=SB),
                                      b_v[:, S * n:S * (n + 1)][:, None, :].broadcast_to([P, SB, S]), ALU.add)\
                       .then_inc(s_free.sem, 1)

                def residual(batch, s, links):
                    s_item.wait(eng, *number_of(batch, "out", s))
                    eng.tensor_tensor(part[:], ps[:, IB, :], b_o, ALU.add).then_inc(s_free.sem, 1)
                    s_free.wait(eng, *number_of(batch, "out", s))
                    links.add(eng.tensor_tensor(part[:], X[:, batch, s, :], part[:], ALU.add))
                    keep_rows(eng, links, g, batch, s, part[:], six, two)

                links = Links(eng, s_link)
                links.start(0)
                roots_of_variances(eng, g, s_var, s_root, links)
                layer_norm(0)
                for n in range(2):
                    high_parts(0, "q", n)
                    high_parts(0, "k", n)
                values(0, 0, True)
                eng.wait_ge(s_in, NM * DMA)
                mask_off(0, links)
                maxima(0, 0)
                maxima(0, 1)
                eng.sem_inc(s_link, LINKS0 - links.n)

                def batch_steps(batch, first, last, links):
                    for m in range(STEPS):
                        u, T = m // 2, m // 4
                        if m + 2 < STEPS:
                            maxima(batch, m + 2)
                        elif not last:
                            if m + 2 == STEPS and cross:
                                s_max.wait(eng, batch, STEPS)
                                mask_off(batch + 1, links)
                            maxima(batch + 1, m + 2 - STEPS)
                        if m % 4 == 0:
                            s_turn.wait(eng, batch, m + 1)
                            if not (first and u < 2):
                                s_pv.wait(eng, batch, u - 1)
                            eng.tensor_copy(probT[:, u % 2, 2 * (m % 2):2 * (m % 2) + 2, :, :]
                                            .rearrange("p h c q -> p (h c q)"), ps[:, PT + m % 2, :]).then_inc(s_cpv.sem, 1)
                        if m % 4 == 3:
                            s_exp.wait(eng, batch, m + 1)
                            if T or not first:
                                s_sums.wait(eng, batch, 2 * T - 1)
                            eng.reciprocal(rz[:], z[:, T % 2, :, :].rearrange("p j h -> p (j h)")).then_inc(s_rz.sem, 1)
                        if m == 0 and not last:
                            s_turned.wait(eng, batch, 2)
                            layer_norm(batch + 1)
                        if m == 1:
                            values(batch, 1, first)
                        if m in (3, 5) and not first:
                            residual(batch - 1, m // 2 - 1, links)
                        if (m % 4 == 2 and m > 2) or m == STEPS - 1:
                            G = NG - 1 if m == STEPS - 1 else T - 1
                            s_taken.wait(eng, batch, 2 * G + 2)
                            s_pv.wait(eng, batch, 2 * G + 2)
                            if G == 0 and not first:
                                s_item.wait(eng, *number_of(batch - 1, "out", 1))
                            eng.tensor_tensor(heads[:, G, :], ps[:, OB + G % 2, 0:S], rz_wide[:], ALU.mult).then_inc(s_norm.sem, 1)
                        if m in (7, 9, 11, 13) and not last:
                            high_parts(batch + 1, "kq"[m // 2 % 2], (m - 7) // 4)
                        if m == 15 and not last:
                            values(batch + 1, 0, False)

                linked_batches(eng, s_link, batch_steps, LINKS0, LINKS)
                links.start(NB * LINKS + LINKS0)
                for s in range(SB):
                    residual(NB - 1, s, links)

            @block.scalar
            def _(eng):
                def probabilities(batch, m):
                    T, j, p = m // 4, m // 2 % 2, m % 2
                    s_max.wait(eng, batch, m + 1)
                    for i in range(2):
                        ins = eng.activation(prob[:, m % 2, i, :], t[:, p, i, :], ACT.Exp, scale=-1.0,
                                             bias=nmax[:, m % 4, i:i + 1],
                                             accum_out=z[:, T % 2, j, 2 * p + i:2 * p + i + 1])
                    ins.then_inc(s_exp.sem, 1)

                def take(own, name, n, first):
                    s_item.wait(eng, *number_of(own, name, n))
                    k = 0 if name == "q" else 1
                    if n:
                        stacked(eng, own, name, 0)
                    elif not first:
                        stacked(eng, own - 1, name, 1)
                    for T in range(2):
                        ins = eng.activation(low[:, k, T, :].bitcast(F32), ps[:, IB, S * T:S * (T + 1)], ACT.Identity,
                                             bias=g["b_feat"][:, 2 * layer + k, 2 * n + T:2 * n + T + 1])
                    ins.then_inc(s_free.sem, 1)

                def take_x(own, n):
                    s_turned.wait(eng, own, n + 1)
                    for c in range(2):
                        ins = eng.activation(xT[:, 2 * n + c, :], ps[:, TB, S * c:S * (c + 1)], ACT.Identity,
                                             bias=g["gb"][:, layer, 1, 2 * n + c:2 * n + c + 1],
                                             scale=g["gb"][:, layer, 0, 2 * n + c:2 * n + c + 1])
                    ins.then_inc(s_x.sem, 1)

                def take_sums(batch, T, first):
                    s_sums.wait(eng, batch, 2 * T + 1)
                    eng.activation(rzT[:], ps[0:HG, TB, 0:S], ACT.Copy).then_inc(s_taken.sem, 1)

                def take_spread(batch, T, first):
                    s_sums.wait(eng, batch, 2 * T + 2)
                    if T or not first:
                        s_norm.wait(eng, batch, T)
                    eng.activation(rz_wide[:], ps[:, TB, 0:S], ACT.Copy).then_inc(s_taken.sem, 1)

                eng.wait_ge(s_var, 1)
                eng.activation(rstd[:], rstd[:], ACT.Sqrt).then_inc(s_root, 1)
                take_x(0, 0)
                take_x(0, 1)
                for name, n in ahead[:4]:
                    take(0, name, n, True)
                probabilities(0, 0)

                def batch_steps(batch, first, last):
                    at, _ = items_of(first, last)
                    for m in range(STEPS):
                        u = m // 2
                        s_turn.wait(eng, batch, m)
                        if m + 1 < STEPS:
                            probabilities(batch, m + 1)
                        elif not last:
                            probabilities(batch + 1, 0)
                        if m % 4:
                            s_turn.wait(eng, batch, m + 1)
                            if not (first and u < 2):
                                s_pv.wait(eng, batch, u - 1)
                            eng.activation(probT[:, u % 2, 2 * (m % 2):2 * (m % 2) + 2, :, :]
                                           .rearrange("p h c q -> p (h c q)"), ps[:, PT + m % 2, :], ACT.Copy)\
                               .then_inc(s_cpa.sem, 1)
                        if m % 4 == 1 and m > 1:
                            take_spread(batch, m // 4 - 1, first)
                        if m in (2, 3) and not last:
                            take_x(batch + 1, m - 2)
                        if m in at and at[m][0] in "qk":
                            take(batch + 1, *at[m], False)
                        if m % 4 == 0 and m or m == STEPS - 1:
                            take_sums(batch, (m - 1) // 4, first)
                    take_spread(batch, NG - 1, first)

                every_batch(eng, batch_steps)

            @block.gpsimd
            def _(eng):
                def low_parts(batch, first):
                    for n in range(2):
                        for k in range(2):
                            if not first:
                                s_score.wait(eng, batch - 1, 8 * n + 8)
                            s_hi.wait(eng, batch, 2 * n + 1 + k)
                            eng.tensor_tensor(low[:, k, :, :], low[:, k, :, :].bitcast(F32), high[:, k, :, :].bitcast(F32),
                                              ALU.subtract).then_inc(s_lo.sem, 1)
                            eng.wait_ge(s_in, NM * DMA)
                            stack(eng, batch, "qk"[k], n, (2,))

                low_parts(0, True)
                with eng.Fori(1, NB) as batch:
                    low_parts(batch, False)


def roots_of_variances(eng, g, s_var, s_root, links):
    eng.tensor_scalar(g["rstd"][:], g["moments"][:, :, :, 1], EPS, None, ALU.add).then_inc(s_var, 1)
    eng.wait_ge(s_root, 1)
    links.add(eng.reciprocal(g["rstd"][:], g["rstd"][:]))


def mlp(nc, d, g):
    X, ident, moments, rstd, ps = g["X"], g["ident"], g["moments"], g["rstd"], g["ps"]
    w1 = g["w_self"]
    w2 = g["w_cross"][:].rearrange("p c (q n) -> p (c q) n", n=D)
    NI = FC // 2
    RING = 4
    XB, HB, YB = 0, 2, 4

    with ExitStack() as ctx:
        def sb(name, shape, dt=F32):
            return ctx.enter_context(nc.sbuf_tensor("mlp_" + name, shape, dt))

        def sem(name):
            return g["whole"].enter_context(nc.semaphore("mlp_" + name))

        xn = sb("xn", [P, SB, D])
        xT = sb("xT", [P, DC, S])
        h = sb("h", [P, RING, 2, S])
        part = sb("part", [P, SB, D])
        res = sb("res", [P, SB, D])

        s_var, s_root, s_link = sem("var"), sem("root"), sem("link")
        s_xn = Count(sem("xn"), SB)
        s_xt = Count(sem("xt"), 2)
        s_x = Count(sem("x"), 2)
        s_h = Count(sem("h"), NI)
        s_gelu = Count(sem("gelu"), NI)
        s_y = Count(sem("y"), NI)
        s_part = Count(sem("part"), SB)
        s_res = Count(sem("res"), SB)
        s_out = Count(sem("out"), SB * DMA)

        with nc.Block() as block:
            @block.tensor
            def _(eng):
                def turn(batch, n, first):
                    s_xn.wait(eng, batch, SB)
                    if not first:
                        s_x.wait(eng, batch - 1, n + 1)
                    for c in range(2):
                        for s in range(SB):
                            mm = eng.transpose(ps[:, XB + n, S * c + P * s:S * c + P * (s + 1)],
                                               xn[:, s, P * (2 * n + c):P * (2 * n + c + 1)], ident[:])
                    mm.then_inc(s_xt.sem, 1)

                def hidden(batch, n, first):
                    if not (first and n < 2):
                        s_gelu.wait(eng, batch, n - 1)
                    if n == 0:
                        s_x.wait(eng, batch, 2)
                    for i in range(2):
                        for c in range(DC):
                            mm = eng.matmul(ps[:, HB + n % 2, S * i:S * (i + 1)], w1[:, c, P * (2 * n + i):P * (2 * n + i + 1)],
                                            xT[:, c, :], start=(c == 0), stop=(c == DC - 1))
                    mm.then_inc(s_h.sem, 1)

                def output(batch, n, first):
                    s_gelu.wait(eng, batch, n + 1)
                    if n == 0 and not first:
                        s_part.wait(eng, batch - 1, SB)
                    for i in range(2):
                        for s in range(SB):
                            mm = eng.matmul(ps[:, YB + s, :], h[:, n % RING, i, P * s:P * (s + 1)], w2[:, 2 * n + i, :],
                                            start=(n == 0 and i == 0), stop=(n == NI - 1 and i == 1))
                    mm.then_inc(s_y.sem, 1)

                turn(0, 0, True)
                turn(0, 1, True)

                def batch_items(batch, first, last):
                    hidden(batch, 0, first)
                    for n in range(1, NI):
                        hidden(batch, n, first)
                        output(batch, n - 1, first)
                    if not last:
                        turn(batch + 1, 0, False)
                        turn(batch + 1, 1, False)
                    output(batch, NI - 1, first)

                every_batch(eng, batch_items)

            @block.scalar
            def _(eng):
                def take_x(batch, first):
                    if not first:
                        s_h.wait(eng, batch - 1, NI)
                    for n in range(2):
                        s_xt.wait(eng, batch, n + 1)
                        for c in range(2):
                            ins = eng.activation(xT[:, 2 * n + c, :], ps[:, XB + n, S * c:S * (c + 1)], ACT.Identity,
                                                 bias=g["gb"][:, 2, 1, 2 * n + c:2 * n + c + 1],
                                                 scale=g["gb"][:, 2, 0, 2 * n + c:2 * n + c + 1])
                        ins.then_inc(s_x.sem, 1)

                eng.wait_ge(s_var, 1)
                eng.activation(rstd[:], rstd[:], ACT.Sqrt).then_inc(s_root, 1)
                take_x(0, True)

                def batch_items(batch, first, last):
                    for n in range(NI):
                        s_h.wait(eng, batch, n + 1)
                        if not (first and n < RING):
                            s_y.wait(eng, batch, n - RING + 1)
                        for i in range(2):
                            ins = eng.activation(h[:, n % RING, i, :], ps[:, HB + n % 2, S * i:S * (i + 1)],
                                                 ACT.Gelu_apprx_tanh, bias=g["b1"][:, 2 * n + i:2 * n + i + 1])
                        ins.then_inc(s_gelu.sem, 1)
                    if not last:
                        take_x(batch + 1, False)

                every_batch(eng, batch_items)

            @block.vector
            def _(eng):
                def layer_norm(batch):
                    for s in range(SB):
                        eng.tensor_scalar(xn[:, s, :], X[:, batch, s, :], moments[:, batch, s, 0:1],
                                          rstd[:, batch, s:s + 1], ALU.subtract, ALU.mult).then_inc(s_xn.sem, 1)

                links = Links(eng, s_link)
                links.start(0)
                roots_of_variances(eng, g, s_var, s_root, links)
                layer_norm(0)

                def batch_items(batch, first, last):
                    if not last:
                        s_xt.wait(eng, batch, 2)
                        layer_norm(batch + 1)
                    if not first:
                        s_res.wait(eng, batch - 1, SB)
                    s_y.wait(eng, batch, NI)
                    for s in range(SB):
                        eng.tensor_tensor(part[:, s, :], ps[:, YB + s, :], g["b_row"][:, 4, :], ALU.add)\
                           .then_inc(s_part.sem, 1)
                    if not first:
                        s_out.wait(eng, batch - 1, SB * DMA)
                    for s in range(SB):
                        s_part.wait(eng, batch, s + 1)
                        eng.tensor_tensor(res[:, s, :], part[:, s, :], X[:, batch, s, :], ALU.add).then_inc(s_res.sem, 1)

                every_batch(eng, batch_items)

            @block.sync
            def _(eng):
                def batch_out(batch, first, last):
                    for s in range(SB):
                        s_res.wait(eng, batch, s + 1)
                        eng.dma_start(d["out"][batch].rearrange("(s p) n -> p s n", p=P)[:, s, :], res[:, s, :])\
                           .then_inc(s_out.sem, DMA)

                every_batch(eng, batch_out)
                s_out.wait(eng, NB - 1, SB * DMA)


def build(nc, d):
    with ExitStack() as ctx:
        def sb(name, shape, dt=F32):
            return ctx.enter_context(nc.sbuf_tensor(name, shape, dt))

        g = {
            "whole": ctx,
            "X": sb("X", [P, NB, SB, D]),
            "moments": sb("moments", [P, NB, SB, 2]),
            "rstd": sb("rstd", [P, NB, SB]),
            "ident": sb("ident", [P, P]),
            "sel": sb("sel", [HG, P]),
            "row": sb("row", [P, 4]),
            "gb": sb("gb", [P, 3, 2, DC]),
            "b_feat": sb("b_feat", [P, 4, DC]),
            "b_row": sb("b_row", [P, 5, D]),
            "b1": sb("b1", [P, FC]),
            "w_self": sb("w_self", [P, DC, 4 * D]),
            "ps": ctx.enter_context(nc.psum_tensor("ps", [P, 8, 512], F32)),
        }
        layer0(nc, d, g)
        g["w_cross"] = sb("w_cross", [P, DC, 4 * D])
        attention(nc, d, g, "self")
        attention(nc, d, g, "cross")
        mlp(nc, d, g)


def kernel(**inputs):
    import concourse.bacc as bacc
    from concourse.bass_utils import run_bass_kernel_spmd

    a = {name: np.asarray(x) for name, x in inputs.items()}
    L0 = {k: a["L0_xattn_" + k] for k in ("Wq", "bq", "Wk", "bk", "Wv", "bv")}
    L1 = {k[len("L1_xattn_"):]: x for k, x in a.items() if k.startswith("L1_xattn_")}

    def rows_to_partitions(w):
        return w.reshape(w.shape[0] // P, P, -1).transpose(1, 0, 2)

    def by_partition(b):
        return b.reshape(-1, P).T

    def along_columns(b):
        return np.broadcast_to(b, (P, b.shape[0]))

    def twice(w):
        w = w.reshape(w.shape[0], NH, 1, HD0)
        return np.concatenate([w, w], 2).reshape(w.shape[0], D)

    where = np.arange(P) % QD
    row = np.zeros((P, 4), np.float32)
    row[:, NEG_LO] = np.where(where >= HD0, -1.0, 0.0)
    row[:, IS_LOW] = np.where(where < HD0, 1.0, 0.0)
    row[:, ONE_AT] = np.where(where == HD0, 1.0, 0.0)
    row[:, FAR_AT] = np.where(where == HD0, FAR, 0.0)

    arrays = {
        "x": a["x"],
        "ctx": a["ctx_2048"],
        "ctxT": a["ctx_2048"].transpose(0, 2, 1),
        "mask0": a["mask_Bx1x2048_bf1"].view(np.uint8),
        "mask_self": a["mask_1x1xSxS2_fc1"],
        "mask_cross": a["mask_Bx1xSxS2_ff1"],
        "w0": rows_to_partitions(np.concatenate([twice(L0["Wq"].T), twice(L0["Wk"].T), L0["Wv"].T], 1)),
        "b0": np.stack([by_partition(twice(L0[k][None])[0]) for k in ("bq", "bk")], 1),
        "bv0": along_columns(L0["bv"]),
        "w_self": rows_to_partitions(np.concatenate([L1["w_qkv"], L1["w_ao"]], 1)),
        "w_cross": rows_to_partitions(np.concatenate([L1["w_q"], L1["w_kv"], L1["w_co"]], 1)),
        "w1": rows_to_partitions(L1["w1"]),
        "w2": rows_to_partitions(L1["w2"]),
        "gb": np.stack([np.stack([by_partition(L1[f"ln{n}_{k}"]) for k in "sb"], 1) for n in (1, 2, 3)], 1),
        "b_feat": np.stack([by_partition(b) for b in (L1["b_qkv"][0:D], L1["b_qkv"][D:2 * D], L1["b_q"], L1["b_kv"][0:D])], 1),
        "b_row": np.stack([along_columns(b) for b in (L1["b_qkv"][2 * D:], L1["b_ao"], L1["b_kv"][D:], L1["b_co"], L1["b2"])], 1),
        "b1": by_partition(L1["b1"]),
        "ident": np.eye(P, dtype=np.float32),
        "sel": np.kron(np.eye(HG), np.ones((1, QD))).astype(np.float32),
        "row": row,
    }
    arrays = {name: np.ascontiguousarray(x) for name, x in arrays.items()}
    nc = bacc.Bacc("TRN2", target_bir_lowering=False, num_devices=1)
    d = {name: nc.dram_tensor("in_" + name, x.shape, mybir.dt.from_np(x.dtype), kind="ExternalInput").ap()
         for name, x in arrays.items()}
    d["out"] = nc.dram_tensor("out", (NB, S, D), F32, kind="ExternalOutput").ap()
    build(nc, d)
    arrays = {"in_" + name: x for name, x in arrays.items()}
    return run_bass_kernel_spmd(nc, [arrays], core_ids=[0]).results[0]["out"]
```

```python
from contextlib import ExitStack

import numpy as np

import concourse.bass as bass
from concourse import mybir

F32 = mybir.dt.float32
F32R = mybir.dt.float32r
U8 = mybir.dt.uint8
ALU = mybir.AluOpType
ACT = mybir.ActivationFunctionType
AX = mybir.AxisListType.X

P = 128
NB = 8
S = 256
D = 512
NH = 16
SB = S // P
DC = D // P
HG = 4
NG = NH // HG
QD = P // HG
HD0 = S // NH
HD1 = D // NH
FF = 4 * D
FC = FF // P
EPS = 1e-5
FAR = 1.0e30
OFF = 10000.0
NEVER = 3.0e38
DMA = 16

NEG_LO, IS_LOW, ONE_AT, FAR_AT = range(4)


class Count:

    def __init__(self, sem, per, before=0):
        self.sem, self.per, self.before = sem, per, before

    def at(self, batch, k):
        return batch * self.per + (self.before + k)

    def wait(self, eng, batch, k):
        eng.wait_ge(self.sem, self.at(batch, k))


def every_batch(eng, body):
    body(0, True, False)
    with eng.Fori(1, NB - 1) as batch:
        body(batch, False, False)
    body(NB - 1, False, True)


class Links:

    def __init__(self, eng, sem):
        self.eng, self.sem, self.n, self.base = eng, sem, 0, 0

    def start(self, base):
        self.base, self.n = base, 0

    def add(self, ins):
        ins.then_inc(self.sem, 1)
        self.n += 1
        self.eng.wait_ge(self.sem, self.base + self.n)


def keep_rows(eng, links, g, batch, s, rows, six, two):
    links.add(eng.bn_stats(six[:], rows))
    eng.tensor_scalar(g["X"][:, batch, s, :], rows, 1.0, None, ALU.mult)
    links.add(eng.bn_aggr(two[:], six[:]))
    links.add(eng.tensor_scalar(g["moments"][:, batch, s, :], two[:], 1.0, None, ALU.mult))


def linked_batches(eng, sem, body, before, per):
    links = Links(eng, sem)

    def padded(batch, first, last):
        links.start(batch * per + before)
        body(batch, first, last, links)
        if links.n < per:
            eng.sem_inc(sem, per - links.n)
            eng.wait_ge(sem, links.base + per)
        assert links.n <= per, links.n

    every_batch(eng, padded)


def layer0_items(last):
    at = {0: [("q", 2)], 1: [("k", 2)], 4: [("q", 3)], 5: [("k", 3)], 7: [("v", 1)]}
    if not last:
        at.update({18: [("q", 0)], 19: [("k", 0)], 22: [("q", 1)], 23: [("k", 1)], 27: [("v", 0)]})
    for G in range(NG):
        at.setdefault(min(8 * G + 8, 31), []).append(("turn", G))
        at.setdefault(min(8 * G + 9, 31), []).append(("spread", G))
    index = {name: n for n, name in enumerate(x for step in sorted(at) for x in at[step])}
    return at, index


def layer0(nc, d, g):
    STEPS, UNITS = 32, 16
    at_full, index_full = layer0_items(False)
    at_last, index_last = layer0_items(True)
    A_ITEMS = 5
    X, ident, sel, row, moments = g["X"], g["ident"], g["sel"], g["row"], g["moments"]
    ps = g["ps"]
    SC, PT, OB, IB = 0, 4, 6, 7

    with ExitStack() as ctx:
        def sb(name, shape, dt=F32):
            return ctx.enter_context(nc.sbuf_tensor(name, shape, dt))

        def sem(name):
            return g["whole"].enter_context(nc.semaphore("l0_" + name))

        w0 = sb("w0", [P, SB, 2 * D + S])
        b0 = sb("b0", [P, 2, NG])
        bv0 = sb("bv0", [P, S])
        x_in = sb("x_in", [P, SB, D])
        c_in = sb("c_in", [P, SB, D])
        m_in = sb("m_in", [P, D], U8)
        mask = sb("mask", [P, D])
        mask_done = sb("mask_done", [P, D])
        far = sb("far", [P, D])
        raw = sb("raw", [P, 2, D])
        q_hi = sb("q_hi", [P, D], F32R)
        rest = sb("rest", [P, D])
        q1 = sb("q1", [P, D], F32R)
        q2 = sb("q2", [P, D], F32R)
        k1 = sb("k1", [P, D], F32R)
        k2 = sb("k2", [P, D], F32R)
        q_stack = sb("q_stack", [P, NH // 2, D], F32R)
        k_stack = sb("k_stack", [P, NH // 2, D], F32R)
        v = sb("v", [P, DC, NH, 2 * HD0])
        nmax = sb("nmax", [P, 4, 2])
        prob = sb("prob", [P, 2, 2, D])
        probT = sb("probT", [P, 2, HG, DC, P])
        z = sb("z", [P, 2, DC, HG])
        rz = sb("rz", [P, DC * HG])
        rzT = sb("rzT", [HG, D])
        rz_wide = sb("rz_wide", [P, D])
        out_n = sb("out_n", [P, 2, D])
        mean_a = sb("mean_a", [P, SB, D])
        second = sb("second", [P, SB, D])
        std_a = sb("std_a", [P, SB, D])
        sums = sb("sums", [P, 4, SB])
        cnt = sb("cnt", [P, 2])
        x_mean = sb("x_mean", [P, SB])
        x_var = sb("x_var", [P, SB])
        x_rstd = sb("x_rstd", [P, SB])
        six = sb("six", [P, 6])
        two = sb("two", [P, 2])
        x_masked = sb("x_masked", [P, SB, D])
        scrap = sb("scrap", [P, D])

        s_set = sem("set")
        s_big = sem("big")
        s_v0 = sem("v0")
        s_load = Count(sem("load"), 3 * DMA)
        s_score = Count(sem("score"), STEPS)
        s_max = Count(sem("max"), STEPS)
        s_exp = Count(sem("exp"), STEPS)
        s_turn = Count(sem("turn"), 2 * STEPS)
        s_cpv = Count(sem("cpv"), STEPS)
        s_cpa = Count(sem("cpa"), STEPS)
        s_pv = Count(sem("pv"), UNITS)
        s_item = Count(sem("item"), len(index_full), A_ITEMS)
        s_free = Count(sem("free"), len(index_full), A_ITEMS)
        s_k1 = Count(sem("k1"), NG)
        s_q1 = Count(sem("q1"), NG)
        s_k2 = Count(sem("k2"), NG)
        s_low = Count(sem("low"), NG)
        s_q2 = Count(sem("q2"), NG)
        s_rest = Count(sem("rest"), NG)
        s_stack = {name: [Count(sem(f"stack_{name}{n}"), 2 * HG * DMA) for n in range(NG)] for name in "qk"}
        s_gv = Count(sem("gv"), 2)
        s_rz = Count(sem("rz"), NG)
        s_norm = Count(sem("norm"), NG)
        s_re = [Count(sem(f"re{k}"), NG // 2 * 8 * DMA) for k in range(2)]
        s_stat = Count(sem("stat"), SB)
        s_fin_g = Count(sem("fin_g"), 2)
        s_fin_v = Count(sem("fin_v"), 2)
        s_fin_a = Count(sem("fin_a"), 1)
        s_link = sem("link")
        LINKS, LINKS0 = 60, 40

        def number_of(batch, name, n):
            if n >= 2 or (name, n) == ("v", 1):
                return batch, index_full[(name, n)] + 1
            if isinstance(batch, int) and batch == 0:
                return 0, [("q", 0), ("k", 0), ("q", 1), ("k", 1), ("v", 0)].index((name, n)) + 1 - A_ITEMS
            return batch - 1, index_full[(name, n)] + 1

        def item_at(batch, last, name, n):
            index = index_last if last else index_full
            return index[(name, n)] + 1

        wq, wk, wv = w0[:, :, 0:D], w0[:, :, D:2 * D], w0[:, :, 2 * D:2 * D + S]

        def stack(eng, name, n):
            dst, srcs = (q_stack, (q1, q2)) if name == "q" else (k_stack, (k1, k2))
            for h in range(HG):
                for a, src in enumerate(srcs):
                    at = 2 * QD * (h % 2) + QD * a
                    eng.dma_start(dst[at:at + QD, 2 * n + h // 2, :].bitcast(F32), src[QD * h:QD * (h + 1), :].bitcast(F32))\
                       .then_inc(s_stack[name][n].sem, DMA)

        def unstaged(eng, batch, name, n, first):
            if n:
                s_stack[name][n - 1].wait(eng, batch, 2 * HG * DMA)
            elif not first:
                s_stack[name][NG - 1].wait(eng, batch - 1, 2 * HG * DMA)

        with nc.Block() as block:
            @block.sync
            def _(eng):
                for dst, src in ((w0, d["w0"]), (b0, d["b0"]), (bv0, d["bv0"]), (ident, d["ident"]),
                                 (sel, d["sel"]), (row, d["row"])):
                    eng.dma_start(dst[:], src).then_inc(s_set, DMA)

                def load(batch):
                    eng.dma_start(x_in[:], d["x"][batch].rearrange("(h p) t -> p h t", p=P)).then_inc(s_load.sem, DMA)
                    eng.dma_start(c_in[:], d["ctx"][batch].rearrange("(h p) t -> p h t", p=P)).then_inc(s_load.sem, DMA)
                    eng.dma_start(m_in[:], d["mask0"][batch].broadcast_to([P, D])).then_inc(s_load.sem, DMA)

                def stack_q(batch, n):
                    eng.wait_ge(s_set, 6 * DMA)
                    s_q2.wait(eng, batch, n + 1)
                    s_q1.wait(eng, batch, n + 1)
                    stack(eng, "q", n)

                load(0)
                stack_q(0, 0)
                stack_q(0, 1)
                for dst, src in ((g["gb"], d["gb"]), (g["b_feat"], d["b_feat"]), (g["b_row"], d["b_row"]),
                                 (g["b1"], d["b1"]), (g["w_self"], d["w_self"])):
                    eng.dma_start(dst[:], src).then_inc(s_big, DMA)

                def regroup(batch, G, first=True):
                    s_norm.wait(eng, batch, G + 1)
                    if not first:
                        s_fin_g.wait(eng, batch - 1, 2)
                    for k in range(HG):
                        head = HG * (G % 2) + k
                        for j, dst in enumerate((mean_a, second)):
                            src = out_n[QD * k + HD0 * j:QD * k + HD0 * (j + 1), G % 2, :]
                            eng.dma_start(dst[HD0 * head:HD0 * (head + 1), G // 2, :], src).then_inc(s_re[G % 2].sem, DMA)

                def batch_loads(batch, first, last):
                    stack_q(batch, 2)
                    if not first:
                        regroup(batch - 1, NG - 1)
                    stack_q(batch, 3)
                    if not last:
                        eng.wait_ge(s_set, 6 * DMA)
                        s_item.wait(eng, batch, item_at(batch, last, "v", 1))
                        s_stat.wait(eng, batch, SB)
                        load(batch + 1)
                    regroup(batch, 0, first)
                    regroup(batch, 1)
                    if not last:
                        stack_q(batch + 1, 0)
                        stack_q(batch + 1, 1)
                    regroup(batch, 2)

                every_batch(eng, batch_loads)
                regroup(NB - 1, NG - 1)
                eng.wait_ge(s_big, 5 * DMA)

            @block.tensor
            def _(eng):
                def scores(batch, m):
                    G, j, p = m // 8, m // 2 % 4, m % 2
                    if m % 8 == 0:
                        for name in "qk":
                            s_stack[name][G].wait(eng, batch, 2 * HG * DMA)
                    for i in range(2):
                        r = slice(2 * QD * i, 2 * QD * (i + 1))
                        mm = eng.matmul(ps[:, SC + 2 * p + i, :], q_stack[r, 2 * G + p, P * j:P * (j + 1)],
                                        k_stack[r, 2 * G + p, :], start=True, stop=True)
                    mm.then_inc(s_score.sem, 1)

                def turn(batch, m):
                    for i in range(2):
                        (s_cpv, s_cpa)[i].wait(eng, batch, m)
                        for c in range(DC):
                            mm = eng.transpose(ps[:, PT + i, P * c:P * (c + 1)], prob[:, m % 2, i, P * c:P * (c + 1)],
                                               ident[:])
                        mm.then_inc(s_turn.sem, 1)

                def pv(batch, u, first):
                    G, j = u // 4, u % 4
                    s_cpv.wait(eng, batch, 2 * u + 2)
                    s_cpa.wait(eng, batch, 2 * u + 2)
                    if u % 8 == 0:
                        s_gv.wait(eng, batch, u // 8 + 1)
                    if j == 0 and not (first and u == 0):
                        s_norm.wait(eng, batch, G)
                    for c in range(DC):
                        for k in range(HG):
                            mm = eng.matmul(ps[QD * k:QD * (k + 1), OB, P * j:P * (j + 1)], v[:, c, HG * G + k, :],
                                            probT[:, u % 2, k, c, :], start=(c == 0), stop=(c == DC - 1))
                    mm.then_inc(s_pv.sem, 1)

                def item(batch, name, n, number):
                    if not (isinstance(batch, int) and batch == 0 and number == -A_ITEMS):
                        s_free.wait(eng, batch, number)
                    bank = ps[:, IB, :]
                    if name in "qk":
                        w, src = (wq, x_in) if name == "q" else (wk, c_in)
                        for c in range(SB):
                            mm = eng.matmul(bank, w[:, c, P * n:P * (n + 1)], src[:, c, :], start=(c == 0), stop=(c == SB - 1))
                    elif name == "v":
                        for t in range(DC):
                            for c in range(SB):
                                mm = eng.matmul(bank[:, P * t:P * (t + 1)], c_in[:, c, P * t:P * (t + 1)],
                                                wv[:, c, P * n:P * (n + 1)], start=(c == 0), stop=(c == SB - 1))
                    elif name == "turn":
                        s_rz.wait(eng, batch, n + 1)
                        for j in range(DC):
                            mm = eng.transpose(ps[0:HG, IB, P * j:P * (j + 1)], rz[:, HG * j:HG * (j + 1)], ident[:])
                    else:
                        mm = eng.matmul(bank, sel[:], rzT[:], start=True, stop=True)
                    mm.then_inc(s_item.sem, 1)

                eng.wait_ge(s_set, 6 * DMA)
                s_load.wait(eng, 0, 3 * DMA)
                for n, (name, tile) in enumerate((("q", 0), ("k", 0), ("q", 1), ("k", 1), ("v", 0))):
                    item(0, name, tile, n - A_ITEMS)
                scores(0, 0)
                scores(0, 1)

                def batch_steps(batch, first, last):
                    at, index = (at_last, index_last) if last else (at_full, index_full)
                    for m in range(STEPS):
                        s_exp.wait(eng, batch, m + 1)
                        if m + 2 < STEPS:
                            scores(batch, m + 2)
                        elif not last:
                            scores(batch + 1, m + 2 - STEPS)
                        turn(batch, m)
                        if m % 8 == 0 and m:
                            item(batch, "turn", m // 8 - 1, index[("turn", m // 8 - 1)])
                        if m % 2 == 0 and m:
                            pv(batch, m // 2 - 1, first)
                        for name, n in at.get(m, []):
                            if m == STEPS - 1 and name == "spread":
                                pv(batch, UNITS - 1, first)
                            if (name, n) == ("q", 0):
                                s_load.wait(eng, batch + 1, 3 * DMA)
                            if name != "turn" or m == STEPS - 1:
                                item(batch, name, n, index[(name, n)])

                every_batch(eng, batch_steps)

            @block.vector
            def _(eng):
                def maxima(batch, m):
                    s_score.wait(eng, batch, m + 1)
                    eng.tensor_reduce(nmax[:, m % 4, :], ps[:, SC + 2 * (m % 2):SC + 2 * (m % 2) + 2, :], AX, ALU.max,
                                      negate=True).then_inc(s_max.sem, 1)

                def masks(links):
                    links.add(eng.tensor_copy(mask[:], m_in[:]))
                    links.add(eng.tensor_scalar(far[:], mask[:], 1.0, row[:, FAR_AT:FAR_AT + 1], ALU.subtract, ALU.mult))

                def masked_x(batch, h):
                    if h == 0:
                        eng.tensor_reduce(cnt[:, 0:1], mask[:], AX, ALU.add)
                    eng.tensor_tensor_reduce(x_masked[:, h, :], x_in[:, h, :], mask[:], 1.0, 0.0, ALU.mult, ALU.add,
                                             sums[:, 0, h:h + 1]).then_inc(s_stat.sem, 1)

                def squares_of_x(batch, h, links):
                    s_stat.wait(eng, batch, h + 1)
                    links.add(eng.tensor_tensor_reduce(scrap[:], x_masked[:, h, :], x_masked[:, h, :], 1.0, 0.0,
                                                       ALU.mult, ALU.add, sums[:, 1, h:h + 1]))

                def keep_x(batch, links):
                    links.add(eng.tensor_scalar(X[:, batch, :, :], x_masked[:], 1.0, None, ALU.mult))

                def moments_of_x(links):
                    links.add(eng.reciprocal(cnt[:, 1:2], cnt[:, 0:1]))
                    links.add(eng.tensor_scalar(x_mean[:], sums[:, 0, :], cnt[:, 1:2], None, ALU.mult))
                    links.add(eng.tensor_scalar(x_var[:], sums[:, 1, :], cnt[:, 1:2], None, ALU.mult))
                    links.add(eng.tensor_tensor(sums[:, 2, :], x_mean[:], x_mean[:], ALU.mult))
                    links.add(eng.tensor_tensor(x_var[:], x_var[:], sums[:, 2, :], ALU.subtract))
                    links.add(eng.tensor_scalar(x_var[:], x_var[:], 0.0, EPS, ALU.max, ALU.add))

                def tile(batch, name, n, first, links):
                    if name == "q":
                        s_free.wait(eng, *number_of(batch, name, n))
                        if not first:
                            s_score.wait(eng, batch - 1, 8 * n + 8)
                        unstaged(eng, batch, name, n, first)
                        links.add(eng.tensor_copy(q_hi[:], raw[:, 0, :]))
                        eng.scalar_tensor_tensor(out=q1[:], in0=q_hi[:].bitcast(F32), scalar=row[:, NEG_LO:NEG_LO + 1],
                                                 in1=raw[:, 0, :], op0=ALU.mult, op1=ALU.add).then_inc(s_q1.sem, 1)
                    else:
                        s_free.wait(eng, *number_of(batch, name, n))
                        if not first:
                            s_score.wait(eng, batch - 1, 8 * n + 8)
                        unstaged(eng, batch, name, n, first)
                        eng.tensor_copy(k1[:], raw[:, 1, :]).then_inc(s_k1.sem, 1)

                def low_part(batch, n):
                    s_rest.wait(eng, batch, n + 1)
                    eng.scalar_tensor_tensor(out=k2[:], in0=rest[:], scalar=row[:, IS_LOW:IS_LOW + 1],
                                             in1=far[:], op0=ALU.mult, op1=ALU.add).then_inc(s_k2.sem, 1)

                def values(batch, hf, first):
                    s_item.wait(eng, *number_of(batch, "v", hf))
                    if not first:
                        s_pv.wait(eng, batch - 1, 8 * hf + 8)
                        s_gv.wait(eng, batch - 1, hf + 1)
                    half = slice(NH // 2 * hf, NH // 2 * (hf + 1))
                    eng.tensor_tensor(v[:, :, half, 0:HD0],
                                      ps[:, IB, :].rearrange("p (c h e) -> p c h e", c=DC, e=HD0),
                                      bv0[:, P * hf:P * (hf + 1)].rearrange("p (h e) -> p h e", e=HD0)[:, None, :, :]
                                      .broadcast_to([P, DC, NH // 2, HD0]), ALU.add).then_inc(s_free.sem, 1)

                links = Links(eng, s_link)
                links.start(0)
                eng.wait_ge(s_set, 6 * DMA)
                links.add(eng.tensor_scalar(b0[:, 0, :], b0[:, 0, :], float(HD0) ** -0.5, None, ALU.mult))
                eng.memset(cnt[:], 0.0).then_inc(s_v0, 1)
                s_load.wait(eng, 0, 3 * DMA)
                masks(links)
                for h in range(SB):
                    masked_x(0, h)
                for h in range(SB):
                    squares_of_x(0, h, links)
                keep_x(0, links)
                for n in range(2):
                    tile(0, "q", n, True, links)
                    tile(0, "k", n, True, links)
                    low_part(0, n)
                values(0, 0, True)
                maxima(0, 0)
                maxima(0, 1)
                if links.n < LINKS0:
                    eng.sem_inc(s_link, LINKS0 - links.n)

                def batch_steps(batch, first, last, links):
                    for m in range(STEPS):
                        u = m // 2
                        if m + 2 < STEPS:
                            maxima(batch, m + 2)
                        elif not last:
                            maxima(batch + 1, m + 2 - STEPS)
                        s_turn.wait(eng, batch, 2 * m + 1)
                        if m % 2 == 0 and not (first and u < 2):
                            s_pv.wait(eng, batch, u - 1)
                        eng.tensor_copy(probT[:, u % 2, 2 * (m % 2), :, :].rearrange("p c q -> p (c q)"),
                                        ps[:, PT, :]).then_inc(s_cpv.sem, 1)
                        if m % 8 == 7:
                            G = m // 8
                            s_exp.wait(eng, batch, m + 1)
                            if G:
                                s_item.wait(eng, batch, item_at(batch, last, "turn", G - 1))
                            elif not first:
                                s_item.wait(eng, batch - 1, index_full[("turn", NG - 1)] + 1)
                            eng.reciprocal(rz[:], z[:, G % 2, :, :].rearrange("p j h -> p (j h)")).then_inc(s_rz.sem, 1)
                        if (m % 8 == 1 and m > 1) or m == STEPS - 1:
                            G = (m - 1) // 8 if m == STEPS - 1 else m // 8 - 1
                            s_free.wait(eng, batch, item_at(batch, last, "spread", G))
                            s_pv.wait(eng, batch, 4 * G + 4)
                            if G >= 2:
                                s_re[G % 2].wait(eng, batch, 8 * DMA)
                            elif not first:
                                s_re[G % 2].wait(eng, batch - 1, 2 * 8 * DMA)
                            eng.tensor_tensor(out_n[:, G % 2, :], ps[:, OB, :], rz_wide[:], ALU.mult).then_inc(s_norm.sem, 1)
                        if m in (1, 2, 5, 6):
                            tile(batch, "kq"[m % 2], 2 + m // 4, first, links)
                        if m in (3, 7):
                            low_part(batch, 2 + m // 4)
                        if m == 8:
                            values(batch, 1, first)
                        if not first and m == 11:
                            finish_variance(batch - 1)
                        if not first and m == 13:
                            finish_norm(batch - 1, links)
                        if not first and m in (16, 18):
                            finish_mask(batch - 1, m // 2 - 8, links)
                        if m == 18:
                            links.add(eng.tensor_copy(mask_done[:], mask[:]))
                        if m == 22:
                            moments_of_x(links)
                        if m == 19 and not last:
                            s_load.wait(eng, batch + 1, 3 * DMA)
                            masks(links)
                        if m in (26, 27) and not last:
                            masked_x(batch + 1, m - 26)
                        if m in (29, 30) and not last:
                            squares_of_x(batch + 1, m - 29, links)
                        if m == 30 and not last:
                            keep_x(batch + 1, links)
                        if m in (19, 20, 23, 24) and not last:
                            tile(batch + 1, "kq"[m % 2], (m - 19) // 4, False, links)
                        if m in (21, 25) and not last:
                            low_part(batch + 1, (m - 21) // 4)
                        if m == 28 and not last:
                            values(batch + 1, 0, False)

                def finish_variance(batch):
                    s_fin_g.wait(eng, batch, 1)
                    eng.tensor_scalar(std_a[:], std_a[:], 0.0, None, ALU.max).then_inc(s_fin_v.sem, 1)

                def finish_norm(batch, links):
                    s_fin_a.wait(eng, batch, 1)
                    links.add(eng.reciprocal(x_rstd[:], x_rstd[:]))
                    for h in range(SB):
                        ins = eng.tensor_scalar(X[:, batch, h, :], X[:, batch, h, :], x_mean[:, h:h + 1],
                                                x_rstd[:, h:h + 1], ALU.subtract, ALU.mult)
                    ins.then_inc(s_fin_v.sem, 1)

                def finish_mask(batch, h, links):
                    s_fin_g.wait(eng, batch, 2)
                    links.add(eng.tensor_tensor(scrap[:], X[:, batch, h, :], mask_done[:], ALU.mult))
                    keep_rows(eng, links, g, batch, h, scrap[:], six, two)

                linked_batches(eng, s_link, batch_steps, LINKS0, LINKS)
                links.start(NB * LINKS + LINKS0)
                finish_variance(NB - 1)
                finish_norm(NB - 1, links)
                for h in range(SB):
                    finish_mask(NB - 1, h, links)

            @block.scalar
            def _(eng):
                def probabilities(batch, m):
                    G, j, p = m // 8, m // 2 % 4, m % 2
                    s_max.wait(eng, batch, m + 1)
                    for i in range(2):
                        ins = eng.activation(prob[:, m % 2, i, :], ps[:, SC + 2 * p + i, :], ACT.Exp,
                                             bias=nmax[:, m % 4, i:i + 1],
                                             accum_out=z[:, G % 2, j, 2 * p + i:2 * p + i + 1])
                    ins.then_inc(s_exp.sem, 1)

                def take(batch, name, n, first, number):
                    s_item.wait(eng, batch, number + 1)
                    own = batch + 1 if n < 2 and name in "qkv" else batch
                    if name in "qk":
                        k = 0 if name == "q" else 1
                        if not (first and n == 0):
                            (s_q1, s_k2)[k].wait(eng, own, n)
                            (s_q2, s_rest)[k].wait(eng, own, n)
                        eng.activation(raw[:, k, :], ps[:, IB, :], ACT.Identity, bias=b0[:, k, n:n + 1],
                                       scale=(float(HD0) ** -0.5 if k == 0 else 1.0)).then_inc(s_free.sem, 1)
                    elif name == "turn":
                        eng.activation(rzT[:], ps[0:HG, IB, :], ACT.Copy).then_inc(s_free.sem, 1)
                    elif name == "spread":
                        if not (first and n == 0):
                            s_norm.wait(eng, batch, n)
                        eng.activation(rz_wide[:], ps[:, IB, :], ACT.Copy).then_inc(s_free.sem, 1)

                eng.wait_ge(s_v0, 1)
                for n, (name, tile) in enumerate((("q", 0), ("k", 0), ("q", 1), ("k", 1))):
                    s_item.wait(eng, 0, n + 1 - A_ITEMS)
                    k = n % 2
                    if tile:
                        (s_q1, s_k2)[k].wait(eng, 0, 1)
                        (s_q2, s_rest)[k].wait(eng, 0, 1)
                    eng.activation(raw[:, k, :], ps[:, IB, :], ACT.Identity, bias=b0[:, k, tile:tile + 1],
                                   scale=(float(HD0) ** -0.5 if k == 0 else 1.0)).then_inc(s_free.sem, 1)
                probabilities(0, 0)

                def finish_roots(batch):
                    s_fin_v.wait(eng, batch, 1)
                    eng.activation(std_a[:], std_a[:], ACT.Sqrt)
                    eng.activation(x_rstd[:], x_var[:], ACT.Sqrt).then_inc(s_fin_a.sem, 1)

                def batch_steps(batch, first, last):
                    at, index = (at_last, index_last) if last else (at_full, index_full)
                    for m in range(STEPS):
                        u = m // 2
                        s_turn.wait(eng, batch, 2 * m)
                        if m + 1 < STEPS:
                            probabilities(batch, m + 1)
                        elif not last:
                            probabilities(batch + 1, 0)
                        s_turn.wait(eng, batch, 2 * m + 2)
                        if m % 2 == 0 and not (first and u < 2):
                            s_pv.wait(eng, batch, u - 1)
                        eng.activation(probT[:, u % 2, 2 * (m % 2) + 1, :, :].rearrange("p c q -> p (c q)"),
                                       ps[:, PT + 1, :], ACT.Copy).then_inc(s_cpa.sem, 1)
                        for name, n in at.get(m, []):
                            if name != "v":
                                take(batch, name, n, first and m < 8, index[(name, n)])
                        if not first and m == 12:
                            finish_roots(batch - 1)

                every_batch(eng, batch_steps)
                finish_roots(NB - 1)

            @block.gpsimd
            def _(eng):
                def parts(batch, name, n, first):
                    if name == "q":
                        if not first:
                            s_score.wait(eng, batch - 1, 8 * n + 8)
                        unstaged(eng, batch, name, n, first)
                        if not (first and n == 0):
                            s_k2.wait(eng, batch, n)
                        s_free.wait(eng, *number_of(batch, name, n))
                        low, one = (row[:, k:k + 1].broadcast_to([P, D]) for k in (IS_LOW, ONE_AT))
                        eng.tensor_tensor(rest[:], raw[:, 0, :], low, ALU.mult).then_inc(s_low.sem, 1)
                        s_low.wait(eng, batch, n + 1)
                        eng.tensor_tensor(q2[:], rest[:], one, ALU.add).then_inc(s_q2.sem, 1)
                    else:
                        s_k1.wait(eng, batch, n + 1)
                        s_q2.wait(eng, batch, n + 1)
                        eng.tensor_tensor(rest[:], raw[:, 1, :], k1[:].bitcast(F32), ALU.subtract).then_inc(s_rest.sem, 1)
                        eng.wait_ge(s_set, 6 * DMA)
                        s_k2.wait(eng, batch, n + 1)
                        stack(eng, "k", n)

                def squares(batch, hf):
                    s_free.wait(eng, *number_of(batch, "v", hf))
                    half = slice(NH // 2 * hf, NH // 2 * (hf + 1))
                    vv = v[:, :, half, 0:HD0]
                    eng.tensor_tensor(v[:, :, half, HD0:2 * HD0], vv, vv, ALU.mult).then_inc(s_gv.sem, 1)

                def finish_a(batch):
                    for by_parity in s_re:
                        by_parity.wait(eng, batch, NG // 2 * 8 * DMA)
                    eng.tensor_tensor(std_a[:], mean_a[:], mean_a[:], ALU.mult).then_inc(s_g, 1)
                    eng.wait_ge(s_g, 2 * batch + 1)
                    eng.tensor_tensor(std_a[:], second[:], std_a[:], ALU.subtract).then_inc(s_fin_g.sem, 1)

                def finish_b(batch):
                    eng.wait_ge(s_set, 6 * DMA)
                    s_fin_v.wait(eng, batch, 2)
                    s_fin_a.wait(eng, batch, 1)
                    eng.tensor_tensor(X[:, batch, :, :], X[:, batch, :, :], std_a[:], ALU.mult).then_inc(s_g, 1)
                    eng.wait_ge(s_set, 6 * DMA)
                    eng.wait_ge(s_g, 2 * batch + 2)
                    eng.tensor_tensor(X[:, batch, :, :], X[:, batch, :, :], mean_a[:], ALU.add).then_inc(s_fin_g.sem, 1)

                s_g = sem("g")
                eng.wait_ge(s_set, 6 * DMA)
                for name, n in (("q", 0), ("k", 0), ("q", 1), ("k", 1)):
                    parts(0, name, n, True)
                squares(0, 0)

                def batch_parts(batch, first, last):
                    for name, n in (("q", 2), ("k", 2), ("q", 3), ("k", 3)):
                        parts(batch, name, n, first)
                    squares(batch, 1)
                    if not first:
                        finish_a(batch - 1)
                        finish_b(batch - 1)
                    if not last:
                        for name, n in (("q", 0), ("k", 0), ("q", 1), ("k", 1)):
                            parts(batch + 1, name, n, False)
                        squares(batch + 1, 0)

                every_batch(eng, batch_parts)
                finish_a(NB - 1)
                finish_b(NB - 1)


def layer1_items(last):
    at = {1: ("v", 1), 3: ("out", 0), 5: ("out", 1)}
    if not last:
        at.update({7: ("q", 0), 9: ("k", 0), 11: ("q", 1), 13: ("k", 1), 15: ("v", 0)})
    return at


def attention(nc, d, g, which):
    cross = which == "cross"
    layer = 1 if cross else 0
    STEPS, UNITS = 16, 8
    BEFORE = 5
    X, ident, sel, moments, rstd, ps = g["X"], g["ident"], g["sel"], g["moments"], g["rstd"], g["ps"]
    w = g["w_cross"] if cross else g["w_self"]
    wq, wk, wv, wo = (w[:, :, D * k:D * (k + 1)] for k in range(4))
    b_v, b_o = g["b_row"][:, 2 * layer, :], g["b_row"][:, 2 * layer + 1, :]
    SC, PT, OB, IB, TB = 0, 2, 4, 6, 7
    NM = NB if cross else 1
    SCALE = float(HD1) ** -0.5

    def items_of(first, last):
        at = {m: x for m, x in layer1_items(last).items() if not (first and x[0] == "out")}
        return at, {at[m]: n for n, m in enumerate(sorted(at))}

    full, full_index = items_of(False, False)
    FIRST_SHORT = 2
    ahead = [("q", 0), ("k", 0), ("v", 0), ("q", 1), ("k", 1)]

    with ExitStack() as ctx:
        def sb(name, shape, dt=F32):
            return ctx.enter_context(nc.sbuf_tensor(f"{which}_{name}", shape, dt))

        def sem(name):
            return g["whole"].enter_context(nc.semaphore(f"{which}_{name}"))

        mask = sb("mask", [P, NM, SB, S])
        off = sb("off", [P, SB, S])
        ctxT = sb("ctxT", [P, DC, S]) if cross else None
        xn = sb("xn", [P, SB, D])
        xT = sb("xT", [P, DC, S])
        low = sb("low", [P, 2, 2, S], F32R)
        high = sb("high", [P, 2, 2, S], F32R)
        q_stack = sb("q_stack", [3 * QD, HG, NG, S], F32R)
        k_stack = sb("k_stack", [3 * QD, HG, NG, S], F32R)
        v = sb("v", [P, SB, D])
        t = sb("t", [P, 2, 2, S])
        nmax = sb("nmax", [P, 4, 2])
        prob = sb("prob", [P, 2, 2, S])
        probT = sb("probT", [P, 2, HG, SB, P])
        z = sb("z", [P, 2, SB, HG])
        rz = sb("rz", [P, SB * HG])
        rzT = sb("rzT", [HG, S])
        rz_wide = sb("rz_wide", [P, S])
        heads = sb("heads", [P, NG, S])
        part = sb("part", [P, D])
        six = sb("six", [P, 6])
        two = sb("two", [P, 2])

        s_in = sem("in")
        s_w = sem("w")
        s_ctx = Count(sem("ctx"), DMA)
        s_t = Count(sem("t"), STEPS)
        s_var = sem("var")
        s_root = sem("root")
        s_xn = Count(sem("xn"), SB)
        s_score = Count(sem("score"), STEPS)
        s_max = Count(sem("max"), STEPS)
        s_exp = Count(sem("exp"), STEPS)
        s_turn = Count(sem("turn"), STEPS)
        s_cpv = Count(sem("cpv"), STEPS // 4)
        s_cpa = Count(sem("cpa"), STEPS - STEPS // 4)
        s_pv = Count(sem("pv"), UNITS)
        s_item = Count(sem("item"), len(full_index), BEFORE - FIRST_SHORT)
        s_free = Count(sem("free"), len(full_index), BEFORE - FIRST_SHORT)
        s_hi = Count(sem("hi"), 4)
        s_lo = Count(sem("lo"), 4)
        s_stack = {(name, n): Count(sem(f"stack_{name}{n}"), 2 * HG * DMA) for name in "qk" for n in range(2)}
        s_third = {(name, n): Count(sem(f"third_{name}{n}"), HG * DMA) for name in "qk" for n in range(2)}
        s_turned = Count(sem("turned"), 2)
        s_x = Count(sem("x"), 2)
        s_rz = Count(sem("rz"), NG)
        s_sums = Count(sem("sums"), 2 * NG)
        s_taken = Count(sem("taken"), 2 * NG)
        s_norm = Count(sem("norm"), NG)
        s_link = sem("link")
        LINKS, LINKS0 = 40, 10

        def index_of(first, last):
            index = items_of(first, last)[1]
            return {x: n + (FIRST_SHORT if first else 0) for x, n in index.items()}

        def number_of(batch, name, n):
            if name == "out":
                if isinstance(batch, int) and batch == NB - 1:
                    return NB - 1, len(index_of(False, True)) + n + 1
                if isinstance(batch, int) and batch == NB - 2:
                    return NB - 1, index_of(False, True)[(name, n)] + 1
                return batch + 1, full_index[(name, n)] + 1
            if (name, n) == ("v", 1):
                if isinstance(batch, int):
                    return batch, index_of(batch == 0, batch == NB - 1)[(name, n)] + 1
                return batch, full_index[(name, n)] + 1
            if isinstance(batch, int) and batch == 0:
                return 0, ahead.index((name, n)) + 1 - (BEFORE - FIRST_SHORT)
            if isinstance(batch, int) and batch == 1:
                return 0, index_of(True, False)[(name, n)] + 1
            return batch - 1, full_index[(name, n)] + 1

        def owner(batch, name, n):
            if name == "out":
                return batch - 1
            return batch if (name, n) == ("v", 1) else batch + 1

        def copied(eng, batch, m):
            s_cpv.wait(eng, batch, m // 4 + 1)
            s_cpa.wait(eng, batch, m - m // 4)

        def stack(eng, batch, name, n, parts):
            k = 0 if name == "q" else 1
            s_lo.wait(eng, batch, 2 * n + 1 + k)
            dst, done = (q_stack, k_stack)[k], (s_third if parts == (2,) else s_stack)[name, n]
            for a in parts:
                src = ((high, low, high) if name == "q" else (high, high, low))[a]
                for h in range(HG):
                    eng.dma_start(dst[QD * a:QD * (a + 1), h, 2 * n:2 * n + 2, :].bitcast(F32),
                                  src[QD * h:QD * (h + 1), k, :, :].bitcast(F32)).then_inc(done.sem, DMA)

        def stacked(eng, batch, name, n):
            s_stack[name, n].wait(eng, batch, 2 * HG * DMA)
            s_third[name, n].wait(eng, batch, HG * DMA)

        with nc.Block() as block:
            @block.sync
            def _(eng):
                if cross:
                    eng.dma_start(ctxT[:], d["ctxT"][0].rearrange("(c p) s -> p c s", p=P)).then_inc(s_ctx.sem, DMA)
                for n in range(NM):
                    src = (d["mask_cross"][n] if cross else d["mask_self"][n]).rearrange("a (j p) k -> p (a j) k", p=P)
                    eng.dma_start(mask[:, n, :, :], src).then_inc(s_in, DMA)
                if not cross:
                    eng.dma_start(g["w_cross"][:], d["w_cross"]).then_inc(s_w, DMA)

                for n in range(2):
                    stack(eng, 0, "q", n, (0, 1))
                    stack(eng, 0, "k", n, (0, 1))

                def batch_loads(batch, first, last):
                    if not last:
                        if cross:
                            s_item.wait(eng, *number_of(batch, "v", 1))
                            eng.dma_start(ctxT[:], d["ctxT"][batch + 1].rearrange("(c p) s -> p c s", p=P))\
                               .then_inc(s_ctx.sem, DMA)
                        for n in range(2):
                            stack(eng, batch + 1, "q", n, (0, 1))
                            stack(eng, batch + 1, "k", n, (0, 1))

                every_batch(eng, batch_loads)
                if not cross:
                    eng.wait_ge(s_w, DMA)

            @block.tensor
            def _(eng):
                def scores(batch, m):
                    T, j, p = m // 4, m // 2 % 2, m % 2
                    if m % 8 == 0:
                        for name in "qk":
                            stacked(eng, batch, name, m // 8)
                    for i in range(2):
                        mm = eng.matmul(ps[:, SC + p, S * i:S * (i + 1)], q_stack[:, 2 * p + i, T, P * j:P * (j + 1)],
                                        k_stack[:, 2 * p + i, T, :], start=True, stop=True)
                    mm.then_inc(s_score.sem, 1)

                def turn(batch, m):
                    if m >= 2:
                        copied(eng, batch, m - 2)
                    else:
                        copied(eng, batch, -1)
                    for i in range(2):
                        for c in range(SB):
                            k = SB * i + c
                            mm = eng.transpose(ps[:, PT + m % 2, P * k:P * (k + 1)], prob[:, m % 2, i, P * c:P * (c + 1)],
                                               ident[:])
                    mm.then_inc(s_turn.sem, 1)

                def pv(batch, u, first):
                    T, j = u // 2, u % 2
                    copied(eng, batch, 2 * u + 1)
                    if u % 4 == 0:
                        s_free.wait(eng, *number_of(batch, "v", u // 4))
                    if j == 0 and not (first and T < 2):
                        s_norm.wait(eng, batch, T - 1)
                    for c in range(SB):
                        for k in range(HG):
                            mm = eng.matmul(ps[QD * k:QD * (k + 1), OB + T % 2, P * j:P * (j + 1)],
                                            v[:, c, QD * (HG * T + k):QD * (HG * T + k + 1)], probT[:, u % 2, k, c, :],
                                            start=(c == 0), stop=(c == SB - 1))
                    mm.then_inc(s_pv.sem, 1)

                def item(name, n, own, parts=(0, 1)):
                    if 0 in parts and not (isinstance(own, int) and own == 0 and (name, n) == ahead[0]):
                        where, number = number_of(own, name, n)
                        s_free.wait(eng, where, number - 1)
                    bank = ps[:, IB, :]
                    if name in "qk":
                        if (name, n) == ("q", 0) and 0 in parts:
                            s_x.wait(eng, own, 2)
                        wt, src = (wq, xT) if name == "q" else (wk, ctxT if cross else xT)
                        if cross and name == "k" and n == 0 and 0 in parts:
                            s_ctx.wait(eng, own, DMA)
                        for T in parts:
                            for c in range(DC):
                                mm = eng.matmul(bank[:, S * T:S * (T + 1)], wt[:, c, P * (2 * n + T):P * (2 * n + T + 1)],
                                                src[:, c, :], start=(c == 0), stop=(c == DC - 1))
                    elif name == "v":
                        src = ctxT if cross else xT
                        for s in parts:
                            for c in range(DC):
                                mm = eng.matmul(bank[:, S * s:S * (s + 1)], src[:, c, P * s:P * (s + 1)],
                                                wv[:, c, S * n:S * (n + 1)], start=(c == 0), stop=(c == DC - 1))
                    else:
                        if n == 0 and 0 in parts:
                            s_norm.wait(eng, own, NG)
                        for T in range(NG // 2 * parts[0], NG // 2 * (parts[-1] + 1)):
                            mm = eng.matmul(bank, heads[:, T, P * n:P * (n + 1)], wo[:, T, :], start=(T == 0), stop=(T == NG - 1))
                    if 1 in parts:
                        mm.then_inc(s_item.sem, 1)

                def turn_x(own, n):
                    s_xn.wait(eng, own, SB)
                    if n:
                        s_x.wait(eng, own, 1)
                    for c in range(2):
                        for s in range(SB):
                            mm = eng.transpose(ps[:, TB, S * c + P * s:S * c + P * (s + 1)],
                                               xn[:, s, P * (2 * n + c):P * (2 * n + c + 1)], ident[:])
                    mm.then_inc(s_turned.sem, 1)

                def turn_sums(batch, T, last):
                    if T == 0:
                        s_x.wait(eng, batch if last else batch + 1, 2)
                    s_rz.wait(eng, batch, T + 1)
                    s_taken.wait(eng, batch, 2 * T)
                    for j in range(SB):
                        mm = eng.transpose(ps[0:HG, TB, P * j:P * (j + 1)], rz[:, HG * j:HG * (j + 1)], ident[:])
                    mm.then_inc(s_sums.sem, 1)

                def spread_sums(batch, T):
                    s_taken.wait(eng, batch, 2 * T + 1)
                    eng.matmul(ps[:, TB, 0:S], sel[:], rzT[:], start=True, stop=True).then_inc(s_sums.sem, 1)

                turn_x(0, 0)
                turn_x(0, 1)
                for name, n in ahead[:4]:
                    item(name, n, 0)
                scores(0, 0)
                scores(0, 1)
                item(*ahead[4], 0)

                def batch_steps(batch, first, last):
                    at, _ = items_of(first, last)
                    for m in range(STEPS):
                        s_exp.wait(eng, batch, m + 1)
                        if m + 2 < STEPS:
                            scores(batch, m + 2)
                        elif not last:
                            scores(batch + 1, m + 2 - STEPS)
                        turn(batch, m)
                        if m % 2 == 0 and m:
                            pv(batch, m // 2 - 1, first)
                        if m in (2, 3) and not last:
                            if m == 2:
                                s_taken.wait(eng, batch, 0)
                            turn_x(batch + 1, m - 2)
                        for part, step in enumerate((m + 1, m)):
                            if step % 2 and step in at:
                                name, n = at[step]
                                item(name, n, owner(batch, name, n), (part,))
                        if m % 4 == 1 and m > 1:
                            spread_sums(batch, m // 4 - 1)
                        if m % 4 == 0 and m or m == STEPS - 1:
                            turn_sums(batch, (m - 1) // 4, last)
                    pv(batch, UNITS - 1, first)
                    spread_sums(batch, NG - 1)

                every_batch(eng, batch_steps)
                item("out", 0, NB - 1)
                item("out", 1, NB - 1)

            @block.vector
            def _(eng):
                def mask_off(batch, links):
                    n = batch if cross else 0
                    links.add(eng.tensor_scalar(off[:], mask[:, n, :, :], -1.0, 1.0, ALU.mult, ALU.add))
                    links.add(eng.tensor_scalar(off[:], off[:], OFF, None, ALU.mult))

                def maxima(batch, m):
                    i, j = m % 2, m // 2 % 2
                    s_score.wait(eng, batch, m + 1)
                    n = batch if cross else 0
                    eng.scalar_tensor_tensor(out=t[:, i, :, :], in0=ps[:, SC + i, :].rearrange("p (h k) -> p h k", h=2), scalar=-SCALE,
                                             in1=mask[:, n, j, :][:, None, :].broadcast_to([P, 2, S]),
                                             op0=ALU.mult, op1=ALU.mult).then_inc(s_t.sem, 1)
                    eng.wait_ge(s_in, NM * DMA)
                    s_t.wait(eng, batch, m + 1)
                    for k in range(2):
                        ins = eng.tensor_tensor_reduce(t[:, i, k, :], t[:, i, k, :], off[:, j, :], 1.0, NEVER,
                                                       ALU.add, ALU.min, nmax[:, m % 4, k:k + 1])
                    ins.then_inc(s_max.sem, 1)

                def layer_norm(batch):
                    for s in range(SB):
                        eng.tensor_scalar(xn[:, s, :], X[:, batch, s, :], moments[:, batch, s, 0:1],
                                          rstd[:, batch, s:s + 1], ALU.subtract, ALU.mult).then_inc(s_xn.sem, 1)

                def high_parts(batch, name, n):
                    k = 0 if name == "q" else 1
                    s_free.wait(eng, *number_of(batch, name, n))
                    eng.tensor_copy(high[:, k, :, :], low[:, k, :, :].bitcast(F32)).then_inc(s_hi.sem, 1)

                def values(batch, n, first):
                    s_item.wait(eng, *number_of(batch, "v", n))
                    if not first:
                        s_pv.wait(eng, batch - 1, 4 * n + 4)
                    eng.tensor_tensor(v[:, :, S * n:S * (n + 1)], ps[:, IB, :].rearrange("p (s e) -> p s e", s=SB),
                                      b_v[:, S * n:S * (n + 1)][:, None, :].broadcast_to([P, SB, S]), ALU.add)\
                       .then_inc(s_free.sem, 1)

                def residual(batch, s, links):
                    s_item.wait(eng, *number_of(batch, "out", s))
                    eng.tensor_tensor(part[:], ps[:, IB, :], b_o, ALU.add).then_inc(s_free.sem, 1)
                    s_free.wait(eng, *number_of(batch, "out", s))
                    links.add(eng.tensor_tensor(part[:], X[:, batch, s, :], part[:], ALU.add))

                links = Links(eng, s_link)
                links.start(0)
                roots_of_variances(eng, g, s_var, s_root, links)
                layer_norm(0)
                high_parts(0, "q", 0)
                high_parts(0, "k", 0)
                values(0, 0, True)
                eng.wait_ge(s_in, NM * DMA)
                mask_off(0, links)
                high_parts(0, "q", 1)
                maxima(0, 0)
                maxima(0, 1)
                high_parts(0, "k", 1)
                eng.sem_inc(s_link, LINKS0 - links.n)

                def batch_steps(batch, first, last, links):
                    for m in range(STEPS):
                        u, T = m // 2, m // 4
                        if m + 2 < STEPS:
                            maxima(batch, m + 2)
                        elif not last:
                            if m + 2 == STEPS and cross:
                                s_max.wait(eng, batch, STEPS)
                                mask_off(batch + 1, links)
                            maxima(batch + 1, m + 2 - STEPS)
                        if m % 4 == 0:
                            s_turn.wait(eng, batch, m + 1)
                            if not (first and u < 2):
                                s_pv.wait(eng, batch, u - 1)
                            eng.tensor_copy(probT[:, u % 2, 2 * (m % 2):2 * (m % 2) + 2, :, :]
                                            .rearrange("p h c q -> p (h c q)"), ps[:, PT + m % 2, :]).then_inc(s_cpv.sem, 1)
                        if m % 4 == 3:
                            s_exp.wait(eng, batch, m + 1)
                            if T or not first:
                                s_sums.wait(eng, batch, 2 * T - 1)
                            eng.reciprocal(rz[:], z[:, T % 2, :, :].rearrange("p j h -> p (j h)")).then_inc(s_rz.sem, 1)
                        if m == 0 and not last:
                            s_turned.wait(eng, batch, 2)
                            layer_norm(batch + 1)
                        if m == 1:
                            values(batch, 1, first)
                        if m in (5, 7) and not first:
                            keep_rows(eng, links, g, batch - 1, m // 2 - 2, part[:], six, two)
                        if m in (3, 5) and not first:
                            residual(batch - 1, m // 2 - 1, links)
                        if m == 15 and not last:
                            values(batch + 1, 0, False)
                        if (m % 4 == 2 and m > 2) or m == STEPS - 1:
                            G = NG - 1 if m == STEPS - 1 else T - 1
                            s_taken.wait(eng, batch, 2 * G + 2)
                            s_pv.wait(eng, batch, 2 * G + 2)
                            if G == 0 and not first:
                                s_item.wait(eng, *number_of(batch - 1, "out", 1))
                            eng.tensor_tensor(heads[:, G, :], ps[:, OB + G % 2, 0:S], rz_wide[:], ALU.mult).then_inc(s_norm.sem, 1)
                        if m in (7, 9, 11, 13) and not last:
                            high_parts(batch + 1, "kq"[m // 2 % 2], (m - 7) // 4)

                linked_batches(eng, s_link, batch_steps, LINKS0, LINKS)
                links.start(NB * LINKS + LINKS0)
                for s in range(SB):
                    residual(NB - 1, s, links)
                    keep_rows(eng, links, g, NB - 1, s, part[:], six, two)

            @block.scalar
            def _(eng):
                def probabilities(batch, m):
                    T, j, p = m // 4, m // 2 % 2, m % 2
                    s_max.wait(eng, batch, m + 1)
                    for i in range(2):
                        ins = eng.activation(prob[:, m % 2, i, :], t[:, p, i, :], ACT.Exp, scale=-1.0,
                                             bias=nmax[:, m % 4, i:i + 1],
                                             accum_out=z[:, T % 2, j, 2 * p + i:2 * p + i + 1])
                    ins.then_inc(s_exp.sem, 1)

                def take(own, name, n, first):
                    s_item.wait(eng, *number_of(own, name, n))
                    k = 0 if name == "q" else 1
                    if n:
                        stacked(eng, own, name, 0)
                    elif not first:
                        stacked(eng, own - 1, name, 1)
                    for T in range(2):
                        ins = eng.activation(low[:, k, T, :].bitcast(F32), ps[:, IB, S * T:S * (T + 1)], ACT.Identity,
                                             bias=g["b_feat"][:, 2 * layer + k, 2 * n + T:2 * n + T + 1])
                    ins.then_inc(s_free.sem, 1)

                def take_x(own, n):
                    s_turned.wait(eng, own, n + 1)
                    for c in range(2):
                        ins = eng.activation(xT[:, 2 * n + c, :], ps[:, TB, S * c:S * (c + 1)], ACT.Identity,
                                             bias=g["gb"][:, layer, 1, 2 * n + c:2 * n + c + 1],
                                             scale=g["gb"][:, layer, 0, 2 * n + c:2 * n + c + 1])
                    ins.then_inc(s_x.sem, 1)

                def take_sums(batch, T):
                    s_sums.wait(eng, batch, 2 * T + 1)
                    eng.activation(rzT[:], ps[0:HG, TB, 0:S], ACT.Copy).then_inc(s_taken.sem, 1)

                def take_spread(batch, T, first):
                    s_sums.wait(eng, batch, 2 * T + 2)
                    if T or not first:
                        s_norm.wait(eng, batch, T)
                    eng.activation(rz_wide[:], ps[:, TB, 0:S], ACT.Copy).then_inc(s_taken.sem, 1)

                eng.wait_ge(s_var, 1)
                eng.activation(rstd[:], rstd[:], ACT.Sqrt).then_inc(s_root, 1)
                take_x(0, 0)
                take_x(0, 1)
                take(0, "q", 0, True)
                take(0, "k", 0, True)
                take(0, "q", 1, True)
                probabilities(0, 0)
                take(0, "k", 1, True)

                def batch_steps(batch, first, last):
                    at, _ = items_of(first, last)
                    for m in range(STEPS):
                        u = m // 2
                        s_turn.wait(eng, batch, m)
                        if m + 1 < STEPS:
                            probabilities(batch, m + 1)
                        elif not last:
                            probabilities(batch + 1, 0)
                        if m % 4:
                            s_turn.wait(eng, batch, m + 1)
                            if not (first and u < 2):
                                s_pv.wait(eng, batch, u - 1)
                            eng.activation(probT[:, u % 2, 2 * (m % 2):2 * (m % 2) + 2, :, :]
                                           .rearrange("p h c q -> p (h c q)"), ps[:, PT + m % 2, :], ACT.Copy)\
                               .then_inc(s_cpa.sem, 1)
                        if m % 4 == 1 and m > 1:
                            take_spread(batch, m // 4 - 1, first)
                        if m in (2, 3) and not last:
                            take_x(batch + 1, m - 2)
                        if m in at and at[m][0] in "qk":
                            take(batch + 1, *at[m], False)
                        if m % 4 == 0 and m or m == STEPS - 1:
                            take_sums(batch, (m - 1) // 4)
                    take_spread(batch, NG - 1, first)

                every_batch(eng, batch_steps)

            @block.gpsimd
            def _(eng):
                def low_parts(batch, first):
                    for n in range(2):
                        for k in range(2):
                            if not first:
                                s_score.wait(eng, batch - 1, 8 * n + 8)
                            s_hi.wait(eng, batch, 2 * n + 1 + k)
                            eng.tensor_tensor(low[:, k, :, :], low[:, k, :, :].bitcast(F32), high[:, k, :, :].bitcast(F32),
                                              ALU.subtract).then_inc(s_lo.sem, 1)
                            eng.wait_ge(s_in, NM * DMA)
                            stack(eng, batch, "qk"[k], n, (2,))

                low_parts(0, True)
                with eng.Fori(1, NB) as batch:
                    low_parts(batch, False)


def roots_of_variances(eng, g, s_var, s_root, links):
    eng.tensor_scalar(g["rstd"][:], g["moments"][:, :, :, 1], EPS, None, ALU.add).then_inc(s_var, 1)
    eng.wait_ge(s_root, 1)
    links.add(eng.reciprocal(g["rstd"][:], g["rstd"][:]))


def mlp(nc, d, g):
    X, ident, moments, rstd, ps = g["X"], g["ident"], g["moments"], g["rstd"], g["ps"]
    NI = FC // 2
    RING = 2
    TURN = 3
    XB, HB, YB = 0, 2, 4

    with ExitStack() as ctx:
        def sb(name, shape, dt=F32):
            return ctx.enter_context(nc.sbuf_tensor("mlp_" + name, shape, dt))

        def sem(name):
            return g["whole"].enter_context(nc.semaphore("mlp_" + name))

        b2 = sb("b2", [P, D])
        w_in = [sb(f"w_in{k}", [P, 2, D]) for k in range(2)]
        w1_hi, w1_lo = (sb(n, [P, DC, FF], F32R) for n in ("w1_hi", "w1_lo"))
        w2_hi, w2_lo = (sb(n, [P, FC, D], F32R) for n in ("w2_hi", "w2_lo"))
        xn = sb("xn", [P, SB, D])
        xT = sb("xT", [P, DC, S])
        x_hi = sb("x_hi", [P, DC, S], F32R)
        x_lo = sb("x_lo", [P, DC, S], F32R)
        h = sb("h", [P, RING, 2, S])
        h_lo = sb("h_lo", [P, RING, 2, S], F32R)
        h_hi = sb("h_hi", [P, RING, 2, S], F32R)
        res = sb("res", [P, SB, D])

        s_var, s_root, s_link = sem("var"), sem("root"), sem("link")
        s_b2 = sem("b2")
        s_w_in = [[sem(f"w_in{k}{odd}") for odd in range(2)] for k in range(2)]
        s_w_hi = sem("w_hi")
        s_w1_lo = sem("w1_lo")
        s_w2_lo = sem("w2_lo")
        s_xn = Count(sem("xn"), SB)
        s_xt = Count(sem("xt"), 2)
        s_x = Count(sem("x"), 2)
        s_x_hi = Count(sem("x_hi"), 1)
        s_x_lo = Count(sem("x_lo"), 1)
        s_h = Count(sem("h"), NI)
        s_gelu = Count(sem("gelu"), NI)
        s_h_hi = Count(sem("h_hi"), NI)
        s_h_lo = Count(sem("h_lo"), NI)
        s_y = Count(sem("y"), NI)
        s_part = Count(sem("part"), SB)
        s_res = Count(sem("res"), SB)
        s_out = Count(sem("out"), SB * DMA)

        def share1(w, n):
            return w[:, :, P * n:P * (n + 1)]

        def share2(w, n):
            return w[:, n, :]

        def share_in(k, n):
            w = w_in[k][:, n % 2, :]
            return w if k else w.rearrange("p (c m) -> p c m", c=DC)

        with nc.Block() as block:
            @block.tensor
            def _(eng):
                def turn(batch, n, first):
                    s_xn.wait(eng, batch, SB)
                    if not first:
                        s_x.wait(eng, batch - 1, n + 1)
                    for c in range(2):
                        for s in range(SB):
                            mm = eng.transpose(ps[:, XB + n, S * c + P * s:S * c + P * (s + 1)],
                                               xn[:, s, P * (2 * n + c):P * (2 * n + c + 1)], ident[:])
                    mm.then_inc(s_xt.sem, 1)

                def hidden(batch, n, first):
                    if first:
                        eng.wait_ge(s_w1_lo, 2 * n + 2)
                    if not (first and n < 2):
                        s_gelu.wait(eng, batch, n - 1)
                    if n == 0:
                        s_x_lo.wait(eng, batch, 1)
                    for i in range(2):
                        col = slice(P * (2 * n + i), P * (2 * n + i + 1))
                        terms = [(w, x, c) for c in range(DC) for w, x in ((w1_hi, x_hi), (w1_hi, x_lo), (w1_lo, x_hi))]
                        for k, (w, x, c) in enumerate(terms):
                            mm = eng.matmul(ps[:, HB + n % 2, S * i:S * (i + 1)], w[:, c, col], x[:, c, :],
                                            start=(k == 0), stop=(k == len(terms) - 1))
                    mm.then_inc(s_h.sem, 1)

                def output(batch, n, first):
                    if first:
                        eng.wait_ge(s_w2_lo, 2 * n + 2)
                    s_h_lo.wait(eng, batch, n + 1)
                    if n == 0 and not first:
                        s_part.wait(eng, batch - 1, SB)
                    terms = [(h, w, i) for i in range(2) for h, w in ((h_hi, w2_hi), (h_hi, w2_lo), (h_lo, w2_hi))]
                    for k, (h, w, i) in enumerate(terms):
                        for s in range(SB):
                            mm = eng.matmul(ps[:, YB + s, :], h[:, n % RING, i, P * s:P * (s + 1)], w[:, 2 * n + i, :],
                                            start=(n == 0 and k == 0), stop=(n == NI - 1 and k == len(terms) - 1))
                    mm.then_inc(s_y.sem, 1)

                turn(0, 0, True)
                turn(0, 1, True)

                def batch_items(batch, first, last):
                    hidden(batch, 0, first)
                    for n in range(1, NI):
                        hidden(batch, n, first)
                        if n == TURN and not last:
                            turn(batch + 1, 0, False)
                            turn(batch + 1, 1, False)
                        output(batch, n - 1, first)
                    output(batch, NI - 1, first)

                every_batch(eng, batch_items)

            @block.scalar
            def _(eng):
                def take_x(batch, first):
                    if not first:
                        s_x_lo.wait(eng, batch - 1, 1)
                    for n in range(2):
                        s_xt.wait(eng, batch, n + 1)
                        for c in range(2):
                            ins = eng.activation(xT[:, 2 * n + c, :], ps[:, XB + n, S * c:S * (c + 1)], ACT.Identity,
                                                 bias=g["gb"][:, 2, 1, 2 * n + c:2 * n + c + 1],
                                                 scale=g["gb"][:, 2, 0, 2 * n + c:2 * n + c + 1])
                        ins.then_inc(s_x.sem, 1)

                def high_weights(n):
                    for k, hi in enumerate((share1(w1_hi, n), share2(w2_hi, n))):
                        eng.wait_ge(s_w_in[k][n % 2], (n // 2 + 1) * DMA)
                        eng.activation(hi, share_in(k, n), ACT.Copy).then_inc(s_w_hi, 1)

                eng.wait_ge(s_var, 1)
                eng.activation(rstd[:], rstd[:], ACT.Sqrt).then_inc(s_root, 1)
                take_x(0, True)
                high_weights(0)
                high_weights(1)

                def batch_items(batch, first, last):
                    for n in range(NI):
                        if first and n + 1 < NI:
                            high_weights(2 * n + 2)
                            high_weights(2 * n + 3)
                        s_h.wait(eng, batch, n + 1)
                        if not (first and n < RING):
                            s_h_lo.wait(eng, batch, n - RING + 1)
                        for i in range(2):
                            ins = eng.activation(h[:, n % RING, i, :], ps[:, HB + n % 2, S * i:S * (i + 1)],
                                                 ACT.Gelu_apprx_tanh, bias=g["b1"][:, 2 * n + i:2 * n + i + 1])
                        ins.then_inc(s_gelu.sem, 1)
                        if n == TURN and not last:
                            take_x(batch + 1, False)

                every_batch(eng, batch_items)

            @block.gpsimd
            def _(eng):
                for n in range(FC):
                    eng.wait_ge(s_w_hi, 2 * n + 2)
                    eng.tensor_tensor(share2(w2_lo, n), share_in(1, n), share2(w2_hi, n).bitcast(F32), ALU.subtract)\
                       .then_inc(s_w2_lo, 1)

            @block.vector
            def _(eng):
                def layer_norm(batch):
                    for s in range(SB):
                        eng.tensor_scalar(xn[:, s, :], X[:, batch, s, :], moments[:, batch, s, 0:1],
                                          rstd[:, batch, s:s + 1], ALU.subtract, ALU.mult).then_inc(s_xn.sem, 1)

                def low_weights(n):
                    eng.wait_ge(s_w_hi, 2 * n + 1)
                    eng.tensor_tensor(share1(w1_lo, n), share_in(0, n), share1(w1_hi, n).bitcast(F32), ALU.subtract)\
                       .then_inc(s_w1_lo, 1)

                def split_x(batch, first):
                    if not first:
                        s_h.wait(eng, batch - 1, NI)
                    s_x.wait(eng, batch, 2)
                    eng.tensor_copy(x_hi[:], xT[:]).then_inc(s_x_hi.sem, 1)
                    s_x_hi.wait(eng, batch, 1)
                    eng.tensor_tensor(x_lo[:], xT[:], x_hi[:].bitcast(F32), ALU.subtract).then_inc(s_x_lo.sem, 1)

                def split_h(batch, n, first):
                    s_gelu.wait(eng, batch, n + 1)
                    if not (first and n < RING):
                        s_y.wait(eng, batch, n - RING + 1)
                    eng.tensor_copy(h_hi[:, n % RING, :, :], h[:, n % RING, :, :]).then_inc(s_h_hi.sem, 1)
                    s_h_hi.wait(eng, batch, n + 1)
                    eng.tensor_tensor(h_lo[:, n % RING, :, :], h[:, n % RING, :, :], h_hi[:, n % RING, :, :].bitcast(F32), ALU.subtract)\
                       .then_inc(s_h_lo.sem, 1)

                links = Links(eng, s_link)
                links.start(0)
                roots_of_variances(eng, g, s_var, s_root, links)
                layer_norm(0)
                split_x(0, True)
                low_weights(0)
                low_weights(1)
                eng.wait_ge(s_b2, DMA)

                def batch_items(batch, first, last):
                    if not last:
                        s_xt.wait(eng, batch, 2)
                        layer_norm(batch + 1)
                    for n in range(NI):
                        if first and n + 1 < NI:
                            low_weights(2 * n + 2)
                            low_weights(2 * n + 3)
                        split_h(batch, n, first)
                    if not last:
                        split_x(batch + 1, False)
                    if not first:
                        s_out.wait(eng, batch - 1, SB * DMA)
                    s_y.wait(eng, batch, NI)
                    for s in range(SB):
                        eng.tensor_tensor(res[:, s, :], ps[:, YB + s, :], b2[:], ALU.add)\
                           .then_inc(s_part.sem, 1)
                    for s in range(SB):
                        s_part.wait(eng, batch, s + 1)
                        eng.tensor_tensor(res[:, s, :], res[:, s, :], X[:, batch, s, :], ALU.add).then_inc(s_res.sem, 1)

                every_batch(eng, batch_items)

            @block.sync
            def _(eng):
                for n in range(FC):
                    for k, (w, lo) in enumerate(((d["w1"][:, :, P * n:P * (n + 1)], s_w1_lo), (d["w2"][:, n, :], s_w2_lo))):
                        if n >= 2:
                            eng.wait_ge(lo, n - 1)
                        eng.dma_start(share_in(k, n), w).then_inc(s_w_in[k][n % 2], DMA)
                    if n == 1:
                        eng.dma_start(b2[:], d["b2"]).then_inc(s_b2, DMA)

                def batch_out(batch, first, last):
                    for s in range(SB):
                        s_res.wait(eng, batch, s + 1)
                        eng.dma_start(d["out"][batch].rearrange("(s p) n -> p s n", p=P)[:, s, :], res[:, s, :])\
                           .then_inc(s_out.sem, DMA)

                every_batch(eng, batch_out)
                s_out.wait(eng, NB - 1, SB * DMA)


def build(nc, d):
    with ExitStack() as ctx:
        g = {"whole": ctx}
        g["ps"] = ctx.enter_context(nc.psum_tensor("ps", [P, 8, 512], F32))

        def keep(until, name, shape):
            g[name] = until.enter_context(nc.sbuf_tensor(name, shape, F32))

        keep(ctx, "X", [P, NB, SB, D])
        keep(ctx, "moments", [P, NB, SB, 2])
        keep(ctx, "rstd", [P, NB, SB])
        keep(ctx, "ident", [P, P])
        keep(ctx, "sel", [HG, P])
        keep(ctx, "row", [P, 4])
        keep(ctx, "gb", [P, 3, 2, DC])
        keep(ctx, "b_feat", [P, 4, DC])
        keep(ctx, "b1", [P, FC])
        with ExitStack() as attentions:
            keep(attentions, "b_row", [P, 4, D])
            keep(attentions, "w_self", [P, DC, 4 * D])
            layer0(nc, d, g)
            keep(attentions, "w_cross", [P, DC, 4 * D])
            attention(nc, d, g, "self")
            attention(nc, d, g, "cross")
        mlp(nc, d, g)


def kernel(**inputs):
    import concourse.bacc as bacc
    from concourse.bass_utils import run_bass_kernel_spmd

    a = {name: np.asarray(x) for name, x in inputs.items()}
    L0 = {k: a["L0_xattn_" + k] for k in ("Wq", "bq", "Wk", "bk", "Wv", "bv")}
    L1 = {k[len("L1_xattn_"):]: x for k, x in a.items() if k.startswith("L1_xattn_")}

    def rows_to_partitions(w):
        return w.reshape(w.shape[0] // P, P, -1).transpose(1, 0, 2)

    def by_partition(b):
        return b.reshape(-1, P).T

    def along_columns(b):
        return np.broadcast_to(b, (P, b.shape[0]))

    def twice(w):
        w = w.reshape(w.shape[0], NH, 1, HD0)
        return np.concatenate([w, w], 2).reshape(w.shape[0], D)

    where = np.arange(P) % QD
    row = np.zeros((P, 4), np.float32)
    row[:, NEG_LO] = np.where(where >= HD0, -1.0, 0.0)
    row[:, IS_LOW] = np.where(where < HD0, 1.0, 0.0)
    row[:, ONE_AT] = np.where(where == HD0, 1.0, 0.0)
    row[:, FAR_AT] = np.where(where == HD0, FAR, 0.0)

    arrays = {
        "x": a["x"],
        "ctx": a["ctx_2048"],
        "ctxT": a["ctx_2048"].transpose(0, 2, 1),
        "mask0": a["mask_Bx1x2048_bf1"].view(np.uint8),
        "mask_self": a["mask_1x1xSxS2_fc1"],
        "mask_cross": a["mask_Bx1xSxS2_ff1"],
        "w0": rows_to_partitions(np.concatenate([twice(L0["Wq"].T), twice(L0["Wk"].T), L0["Wv"].T], 1)),
        "b0": np.stack([by_partition(twice(L0[k][None])[0]) for k in ("bq", "bk")], 1),
        "bv0": along_columns(L0["bv"]),
        "w_self": rows_to_partitions(np.concatenate([L1["w_qkv"], L1["w_ao"]], 1)),
        "w_cross": rows_to_partitions(np.concatenate([L1["w_q"], L1["w_kv"], L1["w_co"]], 1)),
        "w1": rows_to_partitions(L1["w1"]),
        "w2": rows_to_partitions(L1["w2"]),
        "gb": np.stack([np.stack([by_partition(L1[f"ln{n}_{k}"]) for k in "sb"], 1) for n in (1, 2, 3)], 1),
        "b_feat": np.stack([by_partition(b) for b in (L1["b_qkv"][0:D], L1["b_qkv"][D:2 * D], L1["b_q"], L1["b_kv"][0:D])], 1),
        "b_row": np.stack([along_columns(b) for b in (L1["b_qkv"][2 * D:], L1["b_ao"], L1["b_kv"][D:], L1["b_co"])], 1),
        "b2": along_columns(L1["b2"]),
        "b1": by_partition(L1["b1"]),
        "ident": np.eye(P, dtype=np.float32),
        "sel": np.kron(np.eye(HG), np.ones((1, QD))).astype(np.float32),
        "row": row,
    }
    arrays = {name: np.ascontiguousarray(x) for name, x in arrays.items()}
    nc = bacc.Bacc("TRN2", target_bir_lowering=False, num_devices=1)
    d = {name: nc.dram_tensor("in_" + name, x.shape, mybir.dt.from_np(x.dtype), kind="ExternalInput").ap()
         for name, x in arrays.items()}
    d["out"] = nc.dram_tensor("out", (NB, S, D), F32, kind="ExternalOutput").ap()
    build(nc, d)
    arrays = {"in_" + name: x for name, x in arrays.items()}
    return run_bass_kernel_spmd(nc, [arrays], core_ids=[0]).results[0]["out"]
```
